# Optimizing a Trainium2 kernel written in Bass

```python
import numpy as np
import jax
import jax.numpy as jnp

def _softmax(x, axis=-1):
    return jax.nn.softmax(x, axis=axis)

def _gelu(x):
    return jax.nn.gelu(x, approximate=True)

def _silu(x):
    return jax.nn.silu(x)

def _sigmoid(x):
    return jax.nn.sigmoid(x)

def _layernorm(x, axis=-1, eps=1e-05):
    m = jnp.mean(x, axis=axis, keepdims=True)
    v = jnp.var(x, axis=axis, keepdims=True)
    return (x - m) / jnp.sqrt(v + eps)

def _scatter_add(tgt, idx, src, axis=0):
    return tgt.at[idx].add(src)

def _segment_sum(src, seg, n):
    return jax.ops.segment_sum(src, seg, n)
kernel_name = 'mk_lm_tower_d2_tok_ids256_r4_97fa5b'

def setup_inputs(seed: int=0):
    np.random.seed(seed)
    _w = jnp.asarray

    def _rec_inputs():
        import jax
        import jax.numpy as jnp
        _rk = jax.random.key(seed)
        x = jax.random.randint(jax.random.fold_in(_rk, 1), (32, 512), 0, 64, jnp.int32)
        itok_BS_0_255 = jax.random.randint(jax.random.fold_in(_rk, 21), (32, 512), 0, 64, jnp.int32)
        itok_BS_0_511 = jax.random.randint(jax.random.fold_in(_rk, 22), (32, 512), 0, 128, jnp.int32)
        itok_BS_0_127 = jax.random.randint(jax.random.fold_in(_rk, 23), (32, 512), 0, 128, jnp.int32)
        itok_BS_0_63 = jax.random.randint(jax.random.fold_in(_rk, 24), (32, 512), 0, 64, jnp.int32)
        itok_BS_0_3 = jax.random.randint(jax.random.fold_in(_rk, 25), (32, 512), 0, 4, jnp.int32)
        return (x, itok_BS_0_255, itok_BS_0_511, itok_BS_0_127, itok_BS_0_63, itok_BS_0_3)
    x, itok_BS_0_255, itok_BS_0_511, itok_BS_0_127, itok_BS_0_63, itok_BS_0_3 = _rec_inputs()

    def _L0_tok_setup():
        import jax, jax.numpy as jnp
        import numpy as np
        B, S = (128, 512)
        D_OUT = 64
        EMB = 16
        EPS_W = 1e-08
        EPS_LN = 1e-05

        def ternary_linear(x, W, b):
            scale = jnp.mean(jnp.abs(W))
            w_q = jnp.clip(jnp.round(W / (scale + EPS_W)), -1.0, 1.0) * scale
            w_eff = W + jax.lax.stop_gradient(w_q - W)
            return jnp.einsum('bsk,ok->bso', x, w_eff) + b

        def layer_norm(x, gamma, beta):
            mu = jnp.mean(x, axis=-1, keepdims=True)
            var = jnp.mean(jnp.square(x - mu), axis=-1, keepdims=True)
            return (x - mu) * jax.lax.rsqrt(var + EPS_LN) * gamma + beta
        key = jax.random.key(seed)
        ks = jax.random.split(key, 16)
        vocabs = {'event_type': 64, 'fault_class': 64, 'syscall_class': 128, 'opcode_family': 128, 'transition_type': 64, 'result_class': 4}
        inp = {}
        for i, (name, v) in enumerate(vocabs.items()):
            inp[name] = jax.random.randint(ks[i], (B, S), 0, v, dtype=jnp.int64)
        inp['E_et'] = jax.random.normal(ks[6], (64, EMB), dtype=jnp.float32)
        inp['E_fc'] = jax.random.normal(ks[7], (64, EMB), dtype=jnp.float32)
        inp['E_sc'] = jax.random.normal(ks[8], (128, EMB), dtype=jnp.float32)
        inp['E_of'] = jax.random.normal(ks[9], (128, EMB), dtype=jnp.float32)
        inp['E_tt'] = jax.random.normal(ks[10], (64, EMB), dtype=jnp.float32)
        inp['E_rc'] = jax.random.normal(ks[11], (4, EMB), dtype=jnp.float32)
        inp['W'] = jax.random.normal(ks[12], (D_OUT, 96), dtype=jnp.float32) * 0.1
        inp['b'] = jnp.zeros((D_OUT,), dtype=jnp.float32)
        inp['gamma'] = jnp.ones((D_OUT,), dtype=jnp.float32)
        inp['beta'] = jnp.zeros((D_OUT,), dtype=jnp.float32)
        return inp
    _L0_tok_all = _L0_tok_setup()
    _L0_tok_in = {k: v for k, v in _L0_tok_all.items() if k in ('E_et', 'E_fc', 'E_sc', 'E_of', 'E_tt', 'E_rc', 'W', 'b', 'gamma', 'beta')}
    del _L0_tok_all

    def _L0_attn_setup():
        import jax, jax.numpy as jnp
        import numpy as np
        B, T, H, D, N, R, K = (2, 256, 64, 256, 16, 16, 4)
        EPS = 1e-05

        def layer_norm(x, g, b):
            m = jnp.mean(x, -1, keepdims=True)
            v = jnp.mean((x - m) ** 2, -1, keepdims=True)
            return (x - m) * jax.lax.rsqrt(v + EPS) * g + b

        def rms_norm(x, w):
            return x * jax.lax.rsqrt(jnp.mean(x * x, -1, keepdims=True) + EPS) * w

        def selective_scan(u, dt, A, Bm, Cm, Dp):
            dA = jnp.exp(dt[..., None] * A)
            dBu = (dt * u)[..., None] * Bm[:, :, None, :]

            def step(h, inp):
                dA_t, dBu_t, C_t = inp
                h = dA_t * h + dBu_t
                return (h, jnp.einsum('bdn,bn->bd', h, C_t))
            h0 = jnp.zeros((u.shape[0], u.shape[2], A.shape[1]), u.dtype)
            _, ys = jax.lax.scan(step, h0, (dA.swapaxes(0, 1), dBu.swapaxes(0, 1), Cm.swapaxes(0, 1)))
            return ys.swapaxes(0, 1) + u * Dp

        def mamba_mixer(h, inproj_w, conv_w, conv_b, xproj_w, dtproj_w, dtproj_b, A_log, Dp, outproj_w):
            proj = jnp.einsum('bth,eh->bte', h, inproj_w)
            u, gate = (proj[..., :D], proj[..., D:])
            uc = jax.lax.conv_general_dilated(u.swapaxes(1, 2), conv_w, (1,), [(K - 1, 0)], dimension_numbers=('NCH', 'OIH', 'NCH'), feature_group_count=D)
            u = jax.nn.silu(uc + conv_b[None, :, None]).swapaxes(1, 2)
            ssm = jnp.einsum('btd,ed->bte', u, xproj_w)
            dt_r, Bm, Cm = (ssm[..., :R], ssm[..., R:R + N], ssm[..., R + N:])
            dt = jax.nn.softplus(jnp.einsum('btr,dr->btd', dt_r, dtproj_w) + dtproj_b)
            A = -jnp.exp(A_log)
            y = selective_scan(u, dt, A, Bm, Cm, Dp)
            y = y * jax.nn.silu(gate)
            return jnp.einsum('btd,hd->bth', y, outproj_w)

        def _forward(x, pre_g, pre_b, post_g, post_b, norm_w, inproj_w, conv_w, conv_b, xproj_w, dtproj_w, dtproj_b, A_log, D_param, outproj_w, normf_w):
            h = layer_norm(x, pre_g, pre_b)
            for i in range(2):
                h = h + mamba_mixer(rms_norm(h, norm_w[i]), inproj_w[i], conv_w[i], conv_b[i], xproj_w[i], dtproj_w[i], dtproj_b[i], A_log[i], D_param[i], outproj_w[i])
            h = rms_norm(h, normf_w)
            return layer_norm(h, post_g, post_b)
        key = jax.random.key(seed)
        ks = jax.random.split(key, 8)
        s = 0.05
        A0 = jnp.log(jnp.arange(1, N + 1, dtype=jnp.float32))
        return {'x': jax.random.normal(ks[0], (B, T, H), jnp.float32), 'pre_g': jnp.ones((H,), jnp.float32), 'pre_b': jnp.zeros((H,), jnp.float32), 'post_g': jnp.ones((H,), jnp.float32), 'post_b': jnp.zeros((H,), jnp.float32), 'norm_w': jnp.ones((2, H), jnp.float32), 'inproj_w': jax.random.normal(ks[1], (2, 2 * D, H), jnp.float32) * s, 'conv_w': jax.random.normal(ks[2], (2, D, 1, K), jnp.float32) * s, 'conv_b': jnp.zeros((2, D), jnp.float32), 'xproj_w': jax.random.normal(ks[3], (2, R + 2 * N, D), jnp.float32) * s, 'dtproj_w': jax.random.normal(ks[4], (2, D, R), jnp.float32) * s, 'dtproj_b': jax.random.normal(ks[5], (2, D), jnp.float32) * s, 'A_log': jnp.broadcast_to(A0, (2, D, N)) + 0.0, 'D_param': jnp.ones((2, D), jnp.float32), 'outproj_w': jax.random.normal(ks[6], (2, H, D), jnp.float32) * s, 'normf_w': jnp.ones((H,), jnp.float32)}
    _L0_attn_all = _L0_attn_setup()
    _L0_attn_in = {k: v for k, v in _L0_attn_all.items() if k in ('pre_g', 'pre_b', 'post_g', 'post_b', 'norm_w', 'inproj_w', 'conv_w', 'conv_b', 'xproj_w', 'dtproj_w', 'dtproj_b', 'A_log', 'D_param', 'outproj_w', 'normf_w')}
    del _L0_attn_all

    def _L0_ffn_setup():
        import jax, jax.numpy as jnp
        import numpy as np
        B, S, D, H, E, K = (8, 2048, 64, 256, 8, 2)
        key = jax.random.key(seed)
        ks = jax.random.split(key, 7)
        s_in = 1.0 / np.sqrt(D)
        s_hid = 1.0 / np.sqrt(H)
        return {'x': jax.random.normal(ks[0], (B, S, D), dtype=jnp.float32), 'Wg': jax.random.uniform(ks[1], (E, D), jnp.float32, -s_in, s_in), 'bg': jax.random.uniform(ks[2], (E,), jnp.float32, -s_in, s_in), 'W1': jax.random.uniform(ks[3], (E, H, D), jnp.float32, -s_in, s_in), 'b1': jax.random.uniform(ks[4], (E, H), jnp.float32, -s_in, s_in), 'W2': jax.random.uniform(ks[5], (E, D, H), jnp.float32, -s_hid, s_hid), 'b2': jax.random.uniform(ks[6], (E, D), jnp.float32, -s_hid, s_hid)}
    _L0_ffn_all = _L0_ffn_setup()
    _L0_ffn_in = {k: v for k, v in _L0_ffn_all.items() if k in ('Wg', 'bg', 'W1', 'b1', 'W2', 'b2')}
    del _L0_ffn_all

    def _L1_attn_setup():
        import jax, jax.numpy as jnp
        import numpy as np
        import math
        B, S, D = (4, 1024, 64)
        key = jax.random.key(seed)
        ks = jax.random.split(key, 9)
        s = 1.0 / math.sqrt(D)
        return {'src': jax.random.normal(ks[0], (B, S, D), dtype=jnp.float32), 'Wq': jax.random.normal(ks[1], (D, D), dtype=jnp.float32) * s, 'bq': jax.random.normal(ks[2], (D,), dtype=jnp.float32) * s, 'Wk': jax.random.normal(ks[3], (D, D), dtype=jnp.float32) * s, 'bk': jax.random.normal(ks[4], (D,), dtype=jnp.float32) * s, 'Wv': jax.random.normal(ks[5], (D, D), dtype=jnp.float32) * s, 'bv': jax.random.normal(ks[6], (D,), dtype=jnp.float32) * s, 'Wo': jax.random.normal(ks[7], (D, D), dtype=jnp.float32) * s, 'bo': jax.random.normal(ks[8], (D,), dtype=jnp.float32) * s}
    _L1_attn_all = _L1_attn_setup()
    _L1_attn_in = {k: v for k, v in _L1_attn_all.items() if k in ('Wq', 'bq', 'Wk', 'bk', 'Wv', 'bv', 'Wo', 'bo')}
    del _L1_attn_all

    def _L1_ffn_setup():
        import jax, jax.numpy as jnp
        import numpy as np
        B, S, H, F, E, K = (8, 1024, 64, 128, 16, 2)
        EPS = 1e-05
        key = jax.random.key(seed)
        ks = jax.random.split(key, 9)
        sc = 0.02
        return {'x': jax.random.normal(ks[0], (B, S, H), dtype=jnp.float32), 'gate_w': jax.random.normal(ks[1], (H, E), dtype=jnp.float32) * sc, 'gate_b': jnp.zeros((E,), dtype=jnp.float32), 'w1': jax.random.normal(ks[2], (E, H, F), dtype=jnp.float32) * sc, 'b1': jnp.zeros((E, F), dtype=jnp.float32), 'w2': jax.random.normal(ks[3], (E, F, H), dtype=jnp.float32) * sc, 'b2': jnp.zeros((E, H), dtype=jnp.float32), 'gamma': jnp.ones((H,), dtype=jnp.float32), 'beta': jnp.zeros((H,), dtype=jnp.float32)}
    _L1_ffn_all = _L1_ffn_setup()
    _L1_ffn_in = {k: v for k, v in _L1_ffn_all.items() if k in ('gate_w', 'gate_b', 'w1', 'b1', 'w2', 'b2', 'gamma', 'beta')}
    del _L1_ffn_all
    return {'x': x, 'itok_BS_0_255': itok_BS_0_255, 'itok_BS_0_511': itok_BS_0_511, 'itok_BS_0_127': itok_BS_0_127, 'itok_BS_0_63': itok_BS_0_63, 'itok_BS_0_3': itok_BS_0_3, 'L0_tok_E_et': _L0_tok_in['E_et'], 'L0_tok_E_fc': _L0_tok_in['E_fc'], 'L0_tok_E_sc': _L0_tok_in['E_sc'], 'L0_tok_E_of': _L0_tok_in['E_of'], 'L0_tok_E_tt': _L0_tok_in['E_tt'], 'L0_tok_E_rc': _L0_tok_in['E_rc'], 'L0_tok_W': _L0_tok_in['W'], 'L0_tok_b': _L0_tok_in['b'], 'L0_tok_gamma': _L0_tok_in['gamma'], 'L0_tok_beta': _L0_tok_in['beta'], 'L0_attn_pre_g': _L0_attn_in['pre_g'], 'L0_attn_pre_b': _L0_attn_in['pre_b'], 'L0_attn_post_g': _L0_attn_in['post_g'], 'L0_attn_post_b': _L0_attn_in['post_b'], 'L0_attn_norm_w': _L0_attn_in['norm_w'], 'L0_attn_inproj_w': _L0_attn_in['inproj_w'], 'L0_attn_conv_w': _L0_attn_in['conv_w'], 'L0_attn_conv_b': _L0_attn_in['conv_b'], 'L0_attn_xproj_w': _L0_attn_in['xproj_w'], 'L0_attn_dtproj_w': _L0_attn_in['dtproj_w'], 'L0_attn_dtproj_b': _L0_attn_in['dtproj_b'], 'L0_attn_A_log': _L0_attn_in['A_log'], 'L0_attn_D_param': _L0_attn_in['D_param'], 'L0_attn_outproj_w': _L0_attn_in['outproj_w'], 'L0_attn_normf_w': _L0_attn_in['normf_w'], 'L0_ffn_Wg': _L0_ffn_in['Wg'], 'L0_ffn_bg': _L0_ffn_in['bg'], 'L0_ffn_W1': _L0_ffn_in['W1'], 'L0_ffn_b1': _L0_ffn_in['b1'], 'L0_ffn_W2': _L0_ffn_in['W2'], 'L0_ffn_b2': _L0_ffn_in['b2'], 'L1_attn_Wq': _L1_attn_in['Wq'], 'L1_attn_bq': _L1_attn_in['bq'], 'L1_attn_Wk': _L1_attn_in['Wk'], 'L1_attn_bk': _L1_attn_in['bk'], 'L1_attn_Wv': _L1_attn_in['Wv'], 'L1_attn_bv': _L1_attn_in['bv'], 'L1_attn_Wo': _L1_attn_in['Wo'], 'L1_attn_bo': _L1_attn_in['bo'], 'L1_ffn_gate_w': _L1_ffn_in['gate_w'], 'L1_ffn_gate_b': _L1_ffn_in['gate_b'], 'L1_ffn_w1': _L1_ffn_in['w1'], 'L1_ffn_b1': _L1_ffn_in['b1'], 'L1_ffn_w2': _L1_ffn_in['w2'], 'L1_ffn_b2': _L1_ffn_in['b2'], 'L1_ffn_gamma': _L1_ffn_in['gamma'], 'L1_ffn_beta': _L1_ffn_in['beta']}

def reference(x, itok_BS_0_255, itok_BS_0_511, itok_BS_0_127, itok_BS_0_63, itok_BS_0_3, L0_tok_E_et, L0_tok_E_fc, L0_tok_E_sc, L0_tok_E_of, L0_tok_E_tt, L0_tok_E_rc, L0_tok_W, L0_tok_b, L0_tok_gamma, L0_tok_beta, L0_attn_pre_g, L0_attn_pre_b, L0_attn_post_g, L0_attn_post_b, L0_attn_norm_w, L0_attn_inproj_w, L0_attn_conv_w, L0_attn_conv_b, L0_attn_xproj_w, L0_attn_dtproj_w, L0_attn_dtproj_b, L0_attn_A_log, L0_attn_D_param, L0_attn_outproj_w, L0_attn_normf_w, L0_ffn_Wg, L0_ffn_bg, L0_ffn_W1, L0_ffn_b1, L0_ffn_W2, L0_ffn_b2, L1_attn_Wq, L1_attn_bq, L1_attn_Wk, L1_attn_bk, L1_attn_Wv, L1_attn_bv, L1_attn_Wo, L1_attn_bo, L1_ffn_gate_w, L1_ffn_gate_b, L1_ffn_w1, L1_ffn_b1, L1_ffn_w2, L1_ffn_b2, L1_ffn_gamma, L1_ffn_beta):
    import jax
    import jax.numpy as jnp

    def _L0_tok_ref(event_type, fault_class, syscall_class, opcode_family, transition_type, result_class, E_et, E_fc, E_sc, E_of, E_tt, E_rc, W, b, gamma, beta):
        import jax, jax.numpy as jnp
        import numpy as np
        B, S = (128, 512)
        D_OUT = 64
        EMB = 16
        EPS_W = 1e-08
        EPS_LN = 1e-05

        def ternary_linear(x, W, b):
            scale = jnp.mean(jnp.abs(W))
            w_q = jnp.clip(jnp.round(W / (scale + EPS_W)), -1.0, 1.0) * scale
            w_eff = W + jax.lax.stop_gradient(w_q - W)
            return jnp.einsum('bsk,ok->bso', x, w_eff) + b

        def layer_norm(x, gamma, beta):
            mu = jnp.mean(x, axis=-1, keepdims=True)
            var = jnp.mean(jnp.square(x - mu), axis=-1, keepdims=True)
            return (x - mu) * jax.lax.rsqrt(var + EPS_LN) * gamma + beta
        combined = jnp.concatenate([E_et[event_type], E_fc[fault_class], E_sc[syscall_class], E_of[opcode_family], E_tt[transition_type], E_rc[result_class]], axis=-1)
        z = ternary_linear(combined, W, b)
        return layer_norm(z, gamma, beta)

    def _L0_attn_ref(x, pre_g, pre_b, post_g, post_b, norm_w, inproj_w, conv_w, conv_b, xproj_w, dtproj_w, dtproj_b, A_log, D_param, outproj_w, normf_w):
        import jax, jax.numpy as jnp
        import numpy as np
        B, T, H, D, N, R, K = (2, 256, 64, 256, 16, 16, 4)
        EPS = 1e-05

        def layer_norm(x, g, b):
            m = jnp.mean(x, -1, keepdims=True)
            v = jnp.mean((x - m) ** 2, -1, keepdims=True)
            return (x - m) * jax.lax.rsqrt(v + EPS) * g + b

        def rms_norm(x, w):
            return x * jax.lax.rsqrt(jnp.mean(x * x, -1, keepdims=True) + EPS) * w

        def selective_scan(u, dt, A, Bm, Cm, Dp):
            dA = jnp.exp(dt[..., None] * A)
            dBu = (dt * u)[..., None] * Bm[:, :, None, :]

            def step(h, inp):
                dA_t, dBu_t, C_t = inp
                h = dA_t * h + dBu_t
                return (h, jnp.einsum('bdn,bn->bd', h, C_t))
            h0 = jnp.zeros((u.shape[0], u.shape[2], A.shape[1]), u.dtype)
            _, ys = jax.lax.scan(step, h0, (dA.swapaxes(0, 1), dBu.swapaxes(0, 1), Cm.swapaxes(0, 1)))
            return ys.swapaxes(0, 1) + u * Dp

        def mamba_mixer(h, inproj_w, conv_w, conv_b, xproj_w, dtproj_w, dtproj_b, A_log, Dp, outproj_w):
            proj = jnp.einsum('bth,eh->bte', h, inproj_w)
            u, gate = (proj[..., :D], proj[..., D:])
            uc = jax.lax.conv_general_dilated(u.swapaxes(1, 2), conv_w, (1,), [(K - 1, 0)], dimension_numbers=('NCH', 'OIH', 'NCH'), feature_group_count=D)
            u = jax.nn.silu(uc + conv_b[None, :, None]).swapaxes(1, 2)
            ssm = jnp.einsum('btd,ed->bte', u, xproj_w)
            dt_r, Bm, Cm = (ssm[..., :R], ssm[..., R:R + N], ssm[..., R + N:])
            dt = jax.nn.softplus(jnp.einsum('btr,dr->btd', dt_r, dtproj_w) + dtproj_b)
            A = -jnp.exp(A_log)
            y = selective_scan(u, dt, A, Bm, Cm, Dp)
            y = y * jax.nn.silu(gate)
            return jnp.einsum('btd,hd->bth', y, outproj_w)

        def _forward(x, pre_g, pre_b, post_g, post_b, norm_w, inproj_w, conv_w, conv_b, xproj_w, dtproj_w, dtproj_b, A_log, D_param, outproj_w, normf_w):
            h = layer_norm(x, pre_g, pre_b)
            for i in range(2):
                h = h + mamba_mixer(rms_norm(h, norm_w[i]), inproj_w[i], conv_w[i], conv_b[i], xproj_w[i], dtproj_w[i], dtproj_b[i], A_log[i], D_param[i], outproj_w[i])
            h = rms_norm(h, normf_w)
            return layer_norm(h, post_g, post_b)
        return _forward(x, pre_g, pre_b, post_g, post_b, norm_w, inproj_w, conv_w, conv_b, xproj_w, dtproj_w, dtproj_b, A_log, D_param, outproj_w, normf_w)

    def _L0_ffn_ref(x, Wg, bg, W1, b1, W2, b2):
        import jax, jax.numpy as jnp
        import numpy as np
        B, S, D, H, E, K = (8, 2048, 64, 256, 8, 2)
        gate_scores = jnp.einsum('bsd,ed->bse', x, Wg) + bg
        topk_scores, topk_idx = jax.lax.top_k(gate_scores, K)
        topk_probs = jax.nn.softmax(topk_scores, axis=-1)
        combine = jnp.sum(topk_probs[..., None] * jax.nn.one_hot(topk_idx, E, dtype=x.dtype), axis=-2)
        out = jnp.zeros_like(x)
        for e in range(E):
            h = jax.nn.relu(jnp.einsum('bsd,hd->bsh', x, W1[e]) + b1[e])
            y = jnp.einsum('bsh,dh->bsd', h, W2[e]) + b2[e]
            out = out + combine[..., e:e + 1] * y
        return out

    def _L1_attn_ref(src, Wq, bq, Wk, bk, Wv, bv, Wo, bo):
        import jax, jax.numpy as jnp
        import numpy as np
        import math
        B, S, D = (4, 1024, 64)
        q = src @ Wq.T + bq
        k = src @ Wk.T + bk
        v = src @ Wv.T + bv
        row_mask = (q[:, :, 0] != 0) & (k[:, :, 0] != 0)
        mask = row_mask[:, :, None]
        scale = 1.0 / math.sqrt(D)
        scores = jnp.einsum('bid,bjd->bij', q, k) * scale
        scores = jnp.where(mask, scores, jnp.float32(-1000000000.0))
        prob = jax.nn.softmax(scores, axis=-1)
        prob = jnp.where(mask, prob, 0.0)
        out = jnp.einsum('bij,bjd->bid', prob, v)
        return out @ Wo.T + bo

    def _L1_ffn_ref(x, gate_w, gate_b, w1, b1, w2, b2, gamma, beta):
        import jax, jax.numpy as jnp
        import numpy as np
        B, S, H, F, E, K = (8, 1024, 64, 128, 16, 2)
        EPS = 1e-05
        gate_logits = x @ gate_w + gate_b
        topk_vals, topk_idx = jax.lax.top_k(gate_logits, K)
        topk_w = jax.nn.softmax(topk_vals, axis=-1)
        h = jax.nn.relu(jnp.einsum('bsh,ehf->bsef', x, w1) + b1)
        expert_out = jnp.einsum('bsef,efh->bseh', h, w2) + b2
        sel = jnp.take_along_axis(expert_out, topk_idx[:, :, :, None], axis=2)
        moe = jnp.sum(topk_w[..., None] * sel, axis=2)
        y = x + moe
        mu = jnp.mean(y, axis=-1, keepdims=True)
        var = jnp.var(y, axis=-1, keepdims=True)
        return (y - mu) / jnp.sqrt(var + EPS) * gamma + beta
    h = _L0_tok_ref(x, itok_BS_0_255, itok_BS_0_511, itok_BS_0_127, itok_BS_0_63, itok_BS_0_3, L0_tok_E_et, L0_tok_E_fc, L0_tok_E_sc, L0_tok_E_of, L0_tok_E_tt, L0_tok_E_rc, L0_tok_W, L0_tok_b, L0_tok_gamma, L0_tok_beta)
    h = h + _L0_attn_ref(_layernorm(h, axis=-1), L0_attn_pre_g, L0_attn_pre_b, L0_attn_post_g, L0_attn_post_b, L0_attn_norm_w, L0_attn_inproj_w, L0_attn_conv_w, L0_attn_conv_b, L0_attn_xproj_w, L0_attn_dtproj_w, L0_attn_dtproj_b, L0_attn_A_log, L0_attn_D_param, L0_attn_outproj_w, L0_attn_normf_w)
    h = h + _L0_ffn_ref(_layernorm(h, axis=-1), L0_ffn_Wg, L0_ffn_bg, L0_ffn_W1, L0_ffn_b1, L0_ffn_W2, L0_ffn_b2)
    h = h + _L1_attn_ref(_layernorm(h, axis=-1), L1_attn_Wq, L1_attn_bq, L1_attn_Wk, L1_attn_bk, L1_attn_Wv, L1_attn_bv, L1_attn_Wo, L1_attn_bo)
    h = h + _L1_ffn_ref(_layernorm(h, axis=-1), L1_ffn_gate_w, L1_ffn_gate_b, L1_ffn_w1, L1_ffn_b1, L1_ffn_w2, L1_ffn_b2, L1_ffn_gamma, L1_ffn_beta)
    return h

_drawn_inputs = setup_inputs


def setup_inputs(seed=0):
    import zlib

    import numpy as np

    out = dict(_drawn_inputs(seed))
    spreads = {'L0_tok_b': (0.0, 0.1),
     'L0_tok_gamma': (1.0, 0.2),
     'L0_tok_beta': (0.0, 0.1),
     'L0_attn_pre_g': (1.0, 0.2),
     'L0_attn_pre_b': (0.0, 0.1),
     'L0_attn_post_g': (1.0, 0.2),
     'L0_attn_post_b': (0.0, 0.1),
     'L0_attn_norm_w': (1.0, 0.6),
     'L0_attn_conv_b': (0.0, 0.8),
     'L0_attn_D_param': (1.0, 0.6),
     'L0_attn_normf_w': (1.0, 0.2),
     'L1_ffn_gate_b': (0.0, 0.43),
     'L1_ffn_b1': (0.0, 0.8),
     'L1_ffn_b2': (0.0, 0.361),
     'L1_ffn_gamma': (1.0, 0.2),
     'L1_ffn_beta': (0.0, 0.1)}
    factors = {'L0_attn_inproj_w': 6.536,
     'L0_attn_conv_w': 8.0,
     'L0_attn_xproj_w': 8.0,
     'L0_attn_dtproj_w': 8.0,
     'L0_attn_dtproj_b': 8.0,
     'L0_attn_A_log': 8.0,
     'L0_attn_outproj_w': 6.44,
     'L0_ffn_b1': 5.526,
     'L0_ffn_b2': 4.484,
     'L1_attn_bq': 5.843,
     'L1_attn_bk': 8.0,
     'L1_ffn_gate_w': 2.701,
     'L1_ffn_w1': 8.0,
     'L1_ffn_w2': 8.0}
    for name, (base, spread) in spreads.items():
        noise = np.random.default_rng([zlib.crc32(name.encode()), seed]).standard_normal(out[name].shape)
        drawn = base * np.exp(spread * noise) if base else spread * noise
        out[name] = jnp.asarray(drawn.astype(out[name].dtype))
    for name, factor in factors.items():
        out[name] = (out[name] * factor).astype(out[name].dtype)
    return out
```

```python
from contextlib import ExitStack

import concourse.bass as bass
from concourse import mybir

ALU = mybir.AluOpType
ACT = mybir.ActivationFunctionType
F32 = mybir.dt.float32
BF16 = mybir.dt.bfloat16
I32 = mybir.dt.int32
AX = mybir.AxisListType.X

P = 128
CREDIT = 2
EPS = 1e-5
DROPPED = -1e30


def wait_all(eng, passed, *waits):
    for sem, value in waits:
        eng.wait_ge(sem, value)
    eng.sem_inc(passed, 1)


class Steps:

    def __init__(self, eng, sem, base, passed=None):
        self.eng, self.sem, self.base, self.n, self.passed = eng, sem, base, 0, passed

    def then(self, ins):
        ins.then_inc(self.sem, 1)
        self.n += 1
        if self.passed is not None:
            wait_all(self.eng, self.passed, (self.sem, self.base + self.n))
        else:
            self.eng.wait_ge(self.sem, self.base + self.n)


def spread(ap, shape):
    return ap.to_broadcast(shape)


class Net:

    def __init__(self, nc, ctx, t, B, S, D):
        self.nc, self.t, self.B, self.S, self.D = nc, t, B, S, D
        self.T = S // P
        self.H = ctx.enter_context(nc.sbuf_tensor("H", [P, B, self.T, D], F32))
        self.ident = ctx.enter_context(nc.sbuf_tensor("ident", [P, P], F32))
        self.used = []

    def semaphore(self, ctx, name):
        sem = ctx.enter_context(self.nc.semaphore(name))
        self.used.append(sem)
        return sem

    def clear_semaphores(self):
        numbers = [s.num for s in self.used]
        self.used = []
        with self.nc.Block() as block:
            @block.gpsimd
            def _(pool):
                pool.sem_clear(range(min(numbers), max(numbers) + 1))


def centre_and_variance(nc, st, x, total, centred, square, shape):
    D = shape[-1]
    st.then(nc.vector.reduce_sum(total, x, axis=AX))
    st.then(nc.vector.scalar_tensor_tensor(centred, total.unsqueeze(2).to_broadcast(shape), -1.0 / D, x,
                                           ALU.mult, ALU.add))
    st.then(nc.vector.tensor_tensor(square, centred, centred, ALU.mult))
    return nc.vector.reduce_sum(total, square, axis=AX)


def token_stage(net, X):
    nc, t, B, S, D, T = net.nc, net.t, net.B, net.S, net.D, net.T
    PAIRS = B // 2
    N = 2 * S
    NT = 2 * T
    NK = 4
    KW = t["tok_W"].shape[0]
    SHAPE = [P, NT, D]
    LN_STEPS = 3
    with ExitStack() as ctx:
        def sb(name, shape, dt=F32):
            return ctx.enter_context(nc.sbuf_tensor(name, shape, dt))

        def sem(name):
            return net.semaphore(ctx, name)

        emb = sb("t_emb", [KW + 1, NK, P])
        w = sb("w", [KW + 1, NK, D])
        absw = sb("absw", [KW, NK, D])
        wsum = sb("wsum", [KW, 1])
        ones = sb("ones", [KW, KW])
        thr = sb("thr", [KW, 3])
        pos = sb("pos", [KW, NK, D])
        neg = sb("neg", [KW, NK, D])
        weff = sb("weff", [KW + 1, NK, D])
        table = sb("table", [P, NK, 3, D], BF16)
        rest = sb("rest", [P, NK, D])
        vocab = sb("vocab", [P, NK])
        affine = sb("affine", [P, 4, D])
        half = sb("half", [P, NT])
        ids = [sb(f"ids{k}", [P, NK, N], I32) for k in range(2)]
        hot = [sb(f"hot{k}", [P, NK, N], BF16) for k in range(2)]
        total = sb("total", [P, NT])
        rstd = sb("rstd", [P, NT])
        cen = sb("cen", SHAPE)
        sq = sb("sq", SHAPE)
        z = [ctx.enter_context(nc.psum_tensor(f"z{k}", SHAPE, F32)) for k in range(2)]
        tab_ps = ctx.enter_context(nc.psum_tensor("tab_ps", [P, NK, D], F32))
        sum_ps = ctx.enter_context(nc.psum_tensor("sum_ps", [KW, 1], F32))

        loaded = sem("loaded")
        set_up = sem("set_up")
        wsum_ready = sem("wsum_ready")
        scale_ready = sem("scale_ready")
        weff_ready = sem("weff_ready")
        tables_ready = sem("tables_ready")
        table_split = sem("table_split")
        ids_loaded = [sem(f"ids_loaded{k}") for k in range(2)]
        hot_ready = sem("hot_ready")
        z_ready = sem("z_ready")
        dve_step = sem("dve_step")
        var_ready = sem("var_ready")
        pool_step = sem("pool_step")
        pool_passed, dve_passed = sem("pool_passed"), sem("dve_passed")
        rstd_ready = sem("rstd_ready")
        x_done = sem("x_done")
        block = ctx.enter_context(nc.Block())

        IDS = [("id_event", 0, 0, 64), ("id_fault", 0, 64, 64), ("id_syscall", 1, 0, P), ("id_opcode", 2, 0, P),
               ("id_transition", 3, 0, 64), ("id_result", 3, 64, 64)]

        @block.sync
        def _(sp):
            sp.dma_start(net.ident[:], t["ident"]).then_inc(loaded, 16)
            sp.dma_start(emb[:], t["tok_E"]).then_inc(loaded, 16)
            sp.dma_start(w[0:KW], t["tok_W"]).then_inc(loaded, 16)
            sp.dma_start(weff[KW:KW + 1], t["tok_b"]).then_inc(loaded, 16)
            sp.dma_start(vocab[:], t["vocab"]).then_inc(loaded, 16)
            for k, name in enumerate(("tok_gamma", "tok_beta", "pre_g", "pre_b")):
                sp.dma_start(affine[:, k, :], t[name].partition_broadcast(P)).then_inc(loaded, 16)

            def load_ids(p, k):
                for name, tile, first, rows in IDS:
                    src = t[name].rearrange("(q two) s -> q (two s)", two=2)[p].partition_broadcast(rows)
                    sp.dma_start(ids[k][first:first + rows, tile, :], src).then_inc(ids_loaded[k], 16)

            load_ids(0, 0)
            load_ids(1, 1) if PAIRS > 1 else None
            if PAIRS > 2:
                with sp.Fori(0, PAIRS // 2 - 1) as i:
                    for k in range(2):
                        sp.wait_ge(hot_ready, i * 2 + (k + 1))
                        load_ids(i * 2 + (k + 2), k)

        @block.gpsimd
        def _(pool):
            nc.gpsimd.memset(ones[:], 1.0).then_inc(set_up, 1)
            nc.gpsimd.memset(half[:], -0.5).then_inc(set_up, 1)
            pool.wait_ge(set_up, 2)

            def one_pair(p):
                for n in range(3):
                    st = Steps(pool, pool_step, p * 3 + n)
                    wait_all(pool, pool_passed, (var_ready, p * 3 + (n + 1)))
                    st.then(nc.gpsimd.tensor_scalar(rstd[:], total[:], 1.0 / D, EPS, ALU.mult, ALU.add))
                    nc.gpsimd.tensor_tensor(rstd[:], rstd[:], half[:], ALU.pow).then_inc(rstd_ready, 1)

            with pool.Fori(0, PAIRS) as p:
                one_pair(p)

        @block.vector
        def _(dve):
            dve.wait_ge(loaded, 16 * 9)
            st = Steps(dve, weff_ready, 0)
            st.then(nc.vector.scalar_tensor_tensor(absw[:], w[0:KW], -1.0, w[0:KW], ALU.mult, ALU.max))
            nc.vector.reduce_sum(wsum[:], absw[:].rearrange("p k d -> p (k d)"), axis=AX).then_inc(wsum_ready, 1)
            dve.wait_ge(scale_ready, 1)
            nw = 1.0 / (96 * D)
            st.then(nc.vector.tensor_scalar(thr[:, 0:1], sum_ps[:], nw, None, ALU.mult))
            st.then(nc.vector.tensor_scalar(thr[:, 1:2], thr[:, 0:1], 1e-8, 0.5, ALU.add, ALU.mult))
            st.then(nc.vector.tensor_scalar(thr[:, 2:3], thr[:, 1:2], -1.0, None, ALU.mult))
            st.then(nc.vector.tensor_scalar(pos[:], w[0:KW], thr[:, 1:2], thr[:, 0:1], ALU.is_gt, ALU.mult))
            st.then(nc.vector.tensor_scalar(neg[:], w[0:KW], thr[:, 2:3], thr[:, 0:1], ALU.is_lt, ALU.mult))
            st.then(nc.vector.tensor_tensor(pos[:], pos[:], neg[:], ALU.subtract))
            st.then(nc.vector.tensor_tensor(pos[:], pos[:], w[0:KW], ALU.subtract))
            st.then(nc.vector.tensor_tensor(weff[0:KW], w[0:KW], pos[:], ALU.add))
            dve.wait_ge(tables_ready, 1)
            st = Steps(dve, table_split, 0)
            st.then(nc.vector.tensor_copy(table[:, :, 0, :], tab_ps[:]))
            st.then(nc.vector.tensor_tensor(rest[:], tab_ps[:], table[:, :, 0, :], ALU.subtract))
            st.then(nc.vector.tensor_copy(table[:, :, 1, :], rest[:]))
            st.then(nc.vector.tensor_tensor(table[:, :, 2, :], rest[:], table[:, :, 1, :], ALU.subtract))

            def one_hot(p, k, turn):
                dve.wait_ge(ids_loaded[k], turn * (16 * len(IDS)) + 16 * len(IDS))
                if not (isinstance(p, int) and p < 2):
                    dve.wait_ge(z_ready, p - 1)
                for tile in range(NK):
                    last = nc.vector.tensor_scalar(hot[k][:, tile, :], ids[k][:, tile, :], vocab[:, tile:tile + 1],
                                                   None, ALU.is_equal)
                last.then_inc(hot_ready, 1)

            def normalise(p, k):
                xr = X[:, bass.ds(p * 2, 2)].rearrange("p b t d -> p (b t) d")
                hr = net.H[:, bass.ds(p * 2, 2)].rearrange("p b t d -> p (b t) d")
                st = Steps(dve, dve_step, p * STEPS, passed=dve_passed)
                dve.wait_ge(z_ready, p + 1)
                for n, (src, dst) in enumerate(((z[k][:], hr), (hr, xr), (xr, xr))):
                    centre_and_variance(nc, st, src, total[:], cen[:], sq[:], SHAPE).then_inc(var_ready, 1)
                    dve.wait_ge(rstd_ready, p * 3 + (n + 1))
                    st.then(nc.vector.tensor_tensor(dst, cen[:], rstd[:].unsqueeze(2).to_broadcast(SHAPE), ALU.mult))
                    if n != 1:
                        g, b = affine[:, n, :], affine[:, n + 1, :]
                        st.then(nc.vector.tensor_tensor(dst, dst, g.unsqueeze(1).to_broadcast(SHAPE), ALU.mult))
                        st.then(nc.vector.tensor_tensor(dst, dst, b.unsqueeze(1).to_broadcast(SHAPE), ALU.add))
                    
                assert st.n == STEPS

            STEPS = 3 * 4 + 4
            one_hot(0, 0, 0)
            if PAIRS > 1:
                one_hot(1, 1, 0)
            normalise(0, 0)
            if PAIRS > 2:
                with dve.Fori(0, PAIRS // 2 - 1) as i:
                    one_hot(i * 2 + 2, 0, i + 1)
                    normalise(i * 2 + 1, 1)
                    one_hot(i * 2 + 3, 1, i + 1)
                    normalise(i * 2 + 2, 0)
            if PAIRS > 1:
                normalise(PAIRS - 1, 1)

        @block.tensor
        def _(pe):
            pe.wait_ge(set_up, 2)
            pe.wait_ge(wsum_ready, 1)
            nc.tensor.matmul(sum_ps[:], ones[:], wsum[:], start=True, stop=True).then_inc(scale_ready, 1)
            pe.wait_ge(weff_ready, 9)
            for tile in range(NK):
                last = nc.tensor.matmul(tab_ps[:, tile, :], emb[:, tile, :], weff[:, tile, :], start=True, stop=True)
            last.then_inc(tables_ready, 1)
            pe.wait_ge(table_split, 4)

            def project(p, k):
                pe.wait_ge(hot_ready, p + 1)
                if not (isinstance(p, int) and p < 2):
                    pe.wait_ge(rstd_ready, p * 3 - 5)
                for m in range(NT):
                    for tile in range(NK):
                        for part in range(3):
                            last = nc.tensor.matmul(z[k][:, m, :], hot[k][:, tile, m * P:(m + 1) * P],
                                                    table[:, tile, part, :], start=(tile == 0 and part == 0),
                                                    stop=(tile == NK - 1 and part == 2))
                last.then_inc(z_ready, 1)

            project(0, 0)
            if PAIRS > 1:
                project(1, 1)
            if PAIRS > 2:
                with pe.Fori(0, PAIRS // 2 - 1) as i:
                    for k in range(2):
                        project(i * 2 + (k + 2), k)


def mamba_stage(net, X, layer):
    nc, t, B, S, D, T = net.nc, net.t, net.B, net.S, net.D, net.T
    NC, NS = t["m_A_log"].shape[2:4]
    R = t["m_dtproj_w"].shape[1]
    BC = 2 * NS
    DT0 = 3 * BC
    L = layer
    with ExitStack() as ctx:
        def sb(name, shape, dt=F32):
            return ctx.enter_context(nc.sbuf_tensor(f"m{L}_{name}", shape, dt))

        def sem(name):
            return net.semaphore(ctx, f"m{L}_{name}")

        def bank(name):
            return ctx.enter_context(nc.psum_tensor(f"m{L}_{name}", [P, S], F32))

        w_in = sb("w_in", [P, 2 * NC * P])
        w_conv = sb("w_conv", [P, 2, NC * P])
        w_norm = sb("w_norm", [P, 1])
        w_u = sb("w_u", [P, 2, NC * P])
        w_g = sb("w_g", [D, NC * P])
        conv_b = sb("conv_b", [P, NC])
        w_x = sb("w_x", [P, NC, DT0 + R])
        w_dt = sb("w_dt", [P, NC * P])
        dt_b = sb("dt_b", [P, NC])
        decay = sb("decay", [P, NC, NS])
        skip = sb("skip", [P, NC])
        w_out = sb("w_out", [P, NC, D])
        pick = sb("pick", [DT0, BC, P], BF16)
        pick_row = sb("pick_row", [DT0, BC])
        half = sb("half", [P, T])
        sq = sb("sq", [P, T, D])
        ssq = sb("ssq", [P, T])
        rstd = sb("rstd", [P, T])
        xn = sb("xn", [P, T, 2, D])
        xT = sb("xT", [P, S + 3])
        u = [sb(f"u{k}", [P, NC, S]) for k in range(2)]
        gate = [sb(f"gate{k}", [P, NC, S]) for k in range(2)]
        dt = [sb(f"dt{k}", [P, NC, S]) for k in range(2)]
        dtu = [sb(f"dtu{k}", [P, NC, S]) for k in range(2)]
        parts = [sb(f"parts{k}", [DT0, S], BF16) for k in range(2)]
        dt_low = sb("dt_low", [P, S])
        rest = sb("rest", [DT0, S])
        mid = sb("mid", [DT0, S], BF16)
        pos = sb("pos", [P, NC, S])
        ex = sb("ex", [P, NC, S])
        one_ex = sb("one_ex", [P, NC, S])
        log = sb("log", [P, NC, S])
        lost = sb("lost", [P, NC, S])
        Bs = [sb(f"Bs{k}", [P, S]) for k in range(2)]
        dA = [sb(f"dA{k}", [P, NC, S]) for k in range(2)]
        dBu = [sb(f"dBu{k}", [P, NC, S]) for k in range(2)]
        hs = [sb(f"hs{k}", [P, NC, S]) for k in range(2)]
        hC = [sb(f"hC{k}", [P, NC, S]) for k in range(2)]
        yv = sb("yv", [P, NC, S])
        yg = sb("yg", [P, NC, S])
        W0, W1 = bank("W0"), bank("W1")
        Bb = [bank(f"Bb{k}") for k in range(2)]
        Cb = [bank(f"Cb{k}") for k in range(2)]
        Y = [bank(f"Y{c}") for c in range(NC)]

        loaded, pads, w_step, weights_ready = sem("loaded"), sem("pads"), sem("w_step"), sem("weights_ready")
        decay_ready = sem("decay_ready")
        sq_ready, ssq_ready, var_eps, rstd_ready = sem("sq_ready"), sem("ssq_ready"), sem("var_eps"), sem("rstd_ready")
        xn_ready, xT_ps_ready, xT_ready = sem("xn_ready"), sem("xT_ps_ready"), sem("xT_ready")
        proj_ready, silu_done, ssm_ready = sem("proj_ready"), sem("silu_done"), sem("ssm_ready")
        hi_ready, rest_ready, mid_ready = sem("hi_ready"), sem("rest_ready"), sem("mid_ready")
        mid_tmp, lo_ready = sem("mid_tmp"), sem("lo_ready")
        dt_ps_ready, dt_ps_read = sem("dt_ps_ready"), sem("dt_ps_read")
        abs_ready, ex_ready, one_ex_ready = sem("abs_ready"), sem("ex_ready"), sem("one_ex_ready")
        log_ready, lost_ready = sem("log_ready"), sem("lost_ready")
        dt_sum, dt_ready, dtu_ready = sem("dt_sum"), sem("dt_ready"), sem("dtu_ready")
        bb_ready, bb_copied, dbu_ready, da_ready = sem("bb_ready"), sem("bb_copied"), sem("dbu_ready"), sem("da_ready")
        cb_ready, scan_done, hc_ready, summed = sem("cb_ready"), sem("scan_done"), sem("hc_ready"), sem("summed")
        y_read, yg_ready, out_ready, x_done = sem("y_read"), sem("yg_ready"), sem("out_ready"), sem("x_done")
        pool_passed = sem("pool_passed")
        block = ctx.enter_context(nc.Block())

        def rows(eng, first, body):
            first()
            if B > 2:
                with eng.Fori(0, B // 2 - 1) as i:
                    for k in range(2):
                        body(i * 2 + k, k, True)
            body(B - 2, 0, True)
            body(B - 1, 1, False)

        LOADS = 12

        @block.sync
        def _(sp):
            sp.dma_start(w_in[:], t["m_in_w"][L]).then_inc(loaded, 16)
            for pair in range(2):
                for copy in range(2):
                    sp.dma_start(w_conv[copy * D:(copy + 1) * D, pair, :],
                                 t["m_conv_w"][L, 3 - 2 * pair - copy].partition_broadcast(D)).then_inc(loaded, 16)
            sp.dma_start(w_norm[:], t["m_norm_w"][L]).then_inc(loaded, 16)
            sp.dma_start(conv_b[:], t["m_conv_b"][L]).then_inc(loaded, 16)
            sp.dma_start(w_x[:], t["m_xproj_w"][L]).then_inc(loaded, 16)
            sp.dma_start(w_dt[DT0:DT0 + R, :], t["m_dtproj_w"][L]).then_inc(loaded, 16)
            sp.dma_start(dt_b[:], t["m_dtproj_b"][L]).then_inc(loaded, 16)
            sp.dma_start(skip[:], t["m_D"][L]).then_inc(loaded, 16)
            sp.dma_start(w_out[:], t["m_out_w"][L]).then_inc(loaded, 16)
            sp.dma_start(decay[:], t["m_A_log"][L]).then_inc(decay_ready, 16)

        @block.gpsimd
        def _(pool):
            nc.gpsimd.memset(half[:], -0.5).then_inc(pads, 1)
            nc.gpsimd.memset(xT[:], 0.0).then_inc(pads, 1)
            pool.wait_ge(pads, 2)
            pool.sem_inc(dbu_ready, CREDIT)

            def inverse_rms(r):
                wait_all(pool, pool_passed, (ssq_ready, r + 1))
                nc.gpsimd.tensor_scalar(rstd[:], ssq[:], 1.0 / D, EPS, ALU.mult, ALU.add).then_inc(var_eps, 1)
                pool.wait_ge(var_eps, r + 1)
                nc.gpsimd.tensor_tensor(rstd[:], rstd[:], half[:], ALU.pow).then_inc(rstd_ready, 1)

            def low_part(r, k, before=None):
                lo = slice(2 * BC, 3 * BC)
                alone = [] if before is None else [(dbu_ready, before + (CREDIT + 1))]
                wait_all(pool, pool_passed, (rest_ready, r + 1), *alone)
                nc.gpsimd.tensor_copy(mid[lo, :], rest[lo, :]).then_inc(mid_tmp, 1)
                pool.wait_ge(mid_tmp, r + 1)
                nc.gpsimd.tensor_tensor(parts[k][lo, :], rest[lo, :], mid[lo, :], ALU.subtract).then_inc(lo_ready, 1)
                pool.wait_ge(lo_ready, r + 1)

            def one_plus(r):
                wait_all(pool, pool_passed, (ex_ready, r + 1), (lost_ready, r), (log_ready, r))
                nc.gpsimd.tensor_scalar(one_ex[:], ex[:], 1.0, None, ALU.add).then_inc(one_ex_ready, 1)

            def step_sizes(r, k):
                pool.wait_ge(log_ready, r + 1)
                pool.wait_ge(lost_ready, r + 1)
                nc.gpsimd.tensor_tensor(pos[:], pos[:], log[:], ALU.add).then_inc(dt_sum, 1)
                pool.wait_ge(dt_sum, r + 1)
                if not (isinstance(r, int) and r == 0):
                    pool.wait_ge(da_ready, r * NS - NS)
                nc.gpsimd.tensor_tensor(dt[k][:], pos[:], lost[:], ALU.subtract).then_inc(dt_ready, 1)
                pool.wait_ge(dt_ready, r + 1)
                pool.wait_ge(silu_done, r * 4 + 4)
                nc.gpsimd.tensor_tensor(dtu[k][:], dt[k][:], u[k][:], ALU.mult).then_inc(dtu_ready, 1)
                pool.wait_ge(dtu_ready, r + 1)

            def state_input(r, k, n):
                q = r * NS + n
                pool.wait_ge(bb_copied, q + (CREDIT + 1))
                pool.wait_ge(scan_done, q + 1)
                nc.gpsimd.tensor_tensor(dBu[n % 2][:], dtu[k][:], Bs[n % 2][:].unsqueeze(1).to_broadcast([P, NC, S]),
                                        ALU.mult).then_inc(dbu_ready, 1)

            def gated(r, k):
                pool.wait_ge(y_read, r + 1)
                pool.wait_ge(out_ready, r)
                nc.gpsimd.tensor_tensor(yg[:], yv[:], gate[k][:], ALU.mult).then_inc(yg_ready, 1)

            def first():
                inverse_rms(0)
                low_part(0, 0)
                one_plus(0)
                step_sizes(0, 0)

            def body(r, k, more):
                for n in range(NS):
                    state_input(r, k, n)
                    if more and n == 1:
                        inverse_rms(r + 1)
                    if more and n == 8:
                        low_part(r + 1, 1 - k, r * NS + n)
                    if more and n == 11:
                        one_plus(r + 1)
                    if more and n == 13:
                        step_sizes(r + 1, 1 - k)
                gated(r, k)

            rows(pool, first, body)

        @block.scalar
        def _(act):
            act.wait_ge(decay_ready, 16)
            nc.scalar.activation(decay[:], decay[:], ACT.Exp).then_inc(decay_ready, 1)
            act.wait_ge(decay_ready, 17)
            nc.scalar.mul(decay[:], decay[:], -1.0).then_inc(decay_ready, 1)
            act.wait_ge(decay_ready, 18)
            act.wait_ge(loaded, 16 * LOADS)
            act.wait_ge(pads, 2)
            act.sem_inc(bb_copied, CREDIT)

            def copy_xT(r):
                act.wait_ge(xT_ps_ready, r + 1)
                act.wait_ge(proj_ready, r * 4)
                nc.scalar.copy(xT[0:D, 2:S + 2], W0[0:D, :])
                nc.scalar.copy(xT[D:2 * D, 3:S + 3], W0[D:2 * D, :]).then_inc(xT_ready, 1)

            def activate(r, k):
                for j in range(2 * NC):
                    W = (W1, W0)[j % 2]
                    dst = (u if j < NC else gate)[k][:, j % NC, :]
                    act.wait_ge(proj_ready, r * 4 + (j + 1))
                    if not (isinstance(r, int) and r == 0) and j == 0:
                        act.wait_ge(yg_ready, r - 1)
                    bias = conv_b[:, j:j + 1] if j < NC else 0.0
                    nc.scalar.activation(dst, W[:], ACT.Silu, bias=bias).then_inc(silu_done, 1)

            def high_part(r, k):
                act.wait_ge(ssm_ready, r + 1)
                act.wait_ge(dt_ps_ready, r * 2)
                if not (isinstance(r, int) and r == 0):
                    act.wait_ge(cb_ready, r * NS - NS)
                nc.scalar.copy(dt_low[DT0:DT0 + R, :], W1[DT0:DT0 + R, :])
                nc.scalar.copy(parts[k][:], W1[0:DT0, :]).then_inc(hi_ready, 1)

            def middle_part(r, k):
                m = slice(BC, 2 * BC)
                act.wait_ge(rest_ready, r + 1)
                nc.scalar.copy(parts[k][m, :], rest[m, :]).then_inc(mid_ready, 1)

            def softplus_exp(r):
                act.wait_ge(dt_ready, r)
                act.wait_ge(lost_ready, r)
                for c in range(NC):
                    W = (W0, W1)[c]
                    act.wait_ge(dt_ps_ready, r * 2 + (c + 1))
                    nc.scalar.activation(ex[:, c, :], W[:], ACT.Abs, bias=dt_b[:, c:c + 1]).then_inc(abs_ready, 1)
                    nc.scalar.activation(pos[:, c, :], W[:], ACT.Relu, bias=dt_b[:, c:c + 1]).then_inc(dt_ps_read, 1)
                act.wait_ge(abs_ready, r * 2 + 2)
                nc.scalar.activation(ex[:], ex[:], ACT.Exp, scale=-1.0).then_inc(ex_ready, 1)

            def softplus_log(r):
                act.wait_ge(one_ex_ready, r + 1)
                nc.scalar.activation(log[:], one_ex[:], ACT.Ln).then_inc(log_ready, 1)

            def state(r, k, n):
                q = r * NS + n
                act.wait_ge(bb_ready, q + 1)
                act.wait_ge(dbu_ready, q + 1)
                nc.scalar.copy(Bs[n % 2][:], Bb[n % 2][:]).then_inc(bb_copied, 1)
                if n == 0:
                    act.wait_ge(dt_ready, r + 1)
                act.wait_ge(scan_done, q + 1)
                for c in range(NC):
                    last = nc.scalar.activation(dA[n % 2][:, c, :], dt[k][:, c, :], ACT.Exp, scale=decay[:, c, n:n + 1])
                last.then_inc(da_ready, 1)

            def first():
                copy_xT(0)
                activate(0, 0)
                high_part(0, 0)
                middle_part(0, 0)
                softplus_exp(0)
                softplus_log(0)

            def body(r, k, more):
                for n in range(NS):
                    state(r, k, n)
                    if more and n == 3:
                        copy_xT(r + 1)
                    if more and n == 5:
                        activate(r + 1, 1 - k)
                    if more and n == 7:
                        high_part(r + 1, 1 - k)
                    if more and n == 8:
                        middle_part(r + 1, 1 - k)
                    if more and n == 10:
                        softplus_exp(r + 1)
                    if more and n == 12:
                        softplus_log(r + 1)

            rows(act, first, body)

        @block.vector
        def _(dve):
            dve.wait_ge(loaded, 16 * LOADS)
            st = Steps(dve, w_step, 0)
            st.then(nc.vector.tensor_tensor(pick_row[:], net.ident[0:DT0, 0:BC], net.ident[0:DT0, BC:2 * BC], ALU.add))
            st.then(nc.vector.tensor_tensor(pick_row[:], pick_row[:], net.ident[0:DT0, 2 * BC:3 * BC], ALU.add))
            st.then(nc.vector.tensor_copy(pick[:], pick_row[:].unsqueeze(2).to_broadcast([DT0, BC, P])))
            st.then(nc.vector.tensor_scalar(w_in[:], w_in[:], w_norm[:, 0:1], None, ALU.mult))
            st.then(nc.vector.tensor_tensor(w_u[:], w_conv[:], w_in[:, 0:NC * P].unsqueeze(1).to_broadcast([P, 2, NC * P]),
                                            ALU.mult))
            nc.vector.tensor_copy(w_g[:], w_in[0:D, NC * P:2 * NC * P]).then_inc(weights_ready, 1)
            dve.sem_inc(scan_done, CREDIT)
            dve.sem_inc(hc_ready, CREDIT)

            def row(r):
                return X[:, bass.ds(r, 1)].rearrange("p a t d -> p (a t) d")

            def squares(r):
                nc.vector.tensor_tensor(sq[:], row(r), row(r), ALU.mult).then_inc(sq_ready, 1)
                dve.wait_ge(sq_ready, r + 1)
                nc.vector.reduce_sum(ssq[:], sq[:], axis=AX).then_inc(ssq_ready, 1)

            def normalise(r):
                dve.wait_ge(rstd_ready, r + 1)
                dve.wait_ge(xT_ps_ready, r)
                shape = [P, T, 2, D]
                nc.vector.tensor_tensor(xn[:], row(r).unsqueeze(2).to_broadcast(shape),
                                        rstd[:].unsqueeze(2).unsqueeze(3).to_broadcast(shape),
                                        ALU.mult).then_inc(xn_ready, 1)

            def remainder(r, k):
                dve.wait_ge(hi_ready, r + 1)
                dve.wait_ge(mid_ready, r)
                dve.wait_ge(lo_ready, r)
                nc.vector.tensor_tensor(rest[:], W1[0:DT0, :], parts[k][:], ALU.subtract).then_inc(rest_ready, 1)

            def rounding_loss(r):
                dve.wait_ge(one_ex_ready, r + 1)
                dve.wait_ge(dt_ready, r)
                nc.vector.scalar_tensor_tensor(lost[:], one_ex[:], -1.0, ex[:], ALU.add, ALU.subtract).then_inc(lost_ready, 1)

            def scan(r, n):
                q = r * NS + n
                dve.wait_ge(da_ready, q + 1)
                dve.wait_ge(dbu_ready, q + (CREDIT + 1))
                for c in range(NC):
                    last = nc.vector.tensor_tensor_scan(hs[n % 2][:, c, :], dA[n % 2][:, c, :], dBu[n % 2][:, c, :], 0.0,
                                                        ALU.mult, ALU.add)
                last.then_inc(scan_done, 1)

            def times_c(r, n):
                q = r * NS + n
                dve.wait_ge(scan_done, q + (CREDIT + 1))
                dve.wait_ge(cb_ready, q + 1)
                dve.wait_ge(summed, q + 1)
                nc.vector.tensor_tensor(hC[n % 2][:], hs[n % 2][:], Cb[n % 2][:].unsqueeze(1).to_broadcast([P, NC, S]),
                                        ALU.mult).then_inc(hc_ready, 1)

            def skip_path(r, k):
                dve.wait_ge(summed, r * NS + (CREDIT + NS))
                dve.wait_ge(yg_ready, r)
                for c in range(NC):
                    last = nc.vector.scalar_tensor_tensor(yv[:, c, :], u[k][:, c, :], skip[:, c:c + 1], Y[c][:],
                                                          ALU.mult, ALU.add)
                last.then_inc(y_read, 1)

            def residual(r):
                dve.wait_ge(out_ready, r + 1)
                nc.vector.tensor_tensor(row(r), row(r), W0[:, 0:T * D].rearrange("p (t d) -> p t d", d=D),
                                        ALU.add).then_inc(x_done, 1)

            def first():
                squares(0)
                normalise(0)
                remainder(0, 0)
                rounding_loss(0)

            def body(r, k, more):
                for n in range(NS):
                    scan(r, n)
                    if n:
                        times_c(r, n - 1)
                    if more and n == 0:
                        squares(r + 1)
                    if more and n == 2:
                        normalise(r + 1)
                    if more and n == 7:
                        remainder(r + 1, 1 - k)
                    if more and n == 12:
                        rounding_loss(r + 1)
                times_c(r, NS - 1)
                skip_path(r, k)
                residual(r)

            rows(dve, first, body)

        @block.tensor
        def _(pe):
            pe.wait_ge(weights_ready, 1)
            pe.wait_ge(loaded, 16 * LOADS)
            pe.sem_inc(summed, CREDIT)

            def transpose(r):
                pe.wait_ge(xn_ready, r + 1)
                if not (isinstance(r, int) and r == 0):
                    pe.wait_ge(x_done, r - 1)
                for m in range(T):
                    last = nc.tensor.transpose(W0[:, m * P:(m + 1) * P], xn[:, m].rearrange("p a d -> p (a d)"), net.ident[:])
                last.then_inc(xT_ps_ready, 1)

            def project_u(r):
                pe.wait_ge(xT_ready, r + 1)
                pe.wait_ge(dt_ps_read, r * NC)
                for c in range(NC):
                    W = (W1, W0)[c]
                    for pair in range(2):
                        last = nc.tensor.matmul(W[:], w_u[:, pair, c * P:(c + 1) * P], xT[:, 2 - 2 * pair:2 - 2 * pair + S],
                                                start=(pair == 0), stop=(pair == 1))
                    last.then_inc(proj_ready, 1)

            def project_gate(r):
                for c in range(NC):
                    W = (W1, W0)[c]
                    pe.wait_ge(silu_done, r * 4 + (c + 1))
                    nc.tensor.matmul(W[:], w_g[:, c * P:(c + 1) * P], xT[0:D, 2:2 + S], start=True, stop=True).then_inc(proj_ready, 1)

            def project_ssm(r, k):
                pe.wait_ge(silu_done, r * 4 + 3)
                for c in range(NC):
                    last = nc.tensor.matmul(W1[0:DT0 + R, :], w_x[:, c, :], u[k][:, c, :], start=(c == 0), stop=(c == NC - 1))
                last.then_inc(ssm_ready, 1)

            def project_dt(r):
                pe.wait_ge(hi_ready, r + 1)
                pe.wait_ge(silu_done, r * 4 + 4)
                for c in range(NC):
                    W = (W0, W1)[c]
                    if c == 1:
                        pe.wait_ge(rest_ready, r + 1)
                    nc.tensor.matmul(W[:], w_dt[DT0:DT0 + R, c * P:(c + 1) * P], dt_low[DT0:DT0 + R, :],
                                     start=True, stop=True).then_inc(dt_ps_ready, 1)

            def broadcast(r, k, n):
                q = r * NS + n
                if n == 0:
                    pe.wait_ge(mid_ready, r + 1)
                    pe.wait_ge(lo_ready, r + 1)
                pe.wait_ge(bb_copied, q + 1)
                nc.tensor.matmul(Bb[n % 2][:], pick[:, n, :], parts[k][:], start=True, stop=True).then_inc(bb_ready, 1)
                pe.wait_ge(hc_ready, q + 1)
                nc.tensor.matmul(Cb[n % 2][:], pick[:, NS + n, :], parts[k][:], start=True, stop=True).then_inc(cb_ready, 1)

            def sum_state(r, n):
                q = r * NS + n
                pe.wait_ge(hc_ready, q + (CREDIT + 1))
                if n == 0:
                    pe.wait_ge(y_read, r)
                for c in range(NC):
                    last = nc.tensor.matmul(Y[c][:], net.ident[:], hC[n % 2][:, c, :], start=(n == 0), stop=(n == NS - 1))
                last.then_inc(summed, 1)

            def output(r, more):
                pe.wait_ge(yg_ready, r + 1)
                if more:
                    pe.wait_ge(dt_ps_read, r * NC + (NC + 1))
                else:
                    pe.wait_ge(x_done, r)
                for m in range(T):
                    for c in range(NC):
                        last = nc.tensor.matmul(W0[:, m * D:(m + 1) * D], yg[:, c, m * P:(m + 1) * P], w_out[:, c, :],
                                                start=(c == 0), stop=(c == NC - 1))
                last.then_inc(out_ready, 1)

            def first():
                transpose(0)
                project_u(0)
                project_gate(0)
                project_ssm(0, 0)
                project_dt(0)

            def body(r, k, more):
                for n in range(NS):
                    broadcast(r, k, n)
                    if n:
                        sum_state(r, n - 1)
                    if more and n == 3:
                        transpose(r + 1)
                    if more and n == 4:
                        project_u(r + 1)
                    if more and n == 5:
                        project_gate(r + 1)
                    if more and n == 6:
                        project_ssm(r + 1, 1 - k)
                    if more and n == 9:
                        project_dt(r + 1)
                sum_state(r, NS - 1)
                output(r, more)

            rows(pe, first, body)


def mamba_end_stage(net, X):
    nc, t, B, S, D, T = net.nc, net.t, net.B, net.S, net.D, net.T
    G = 4 if B % 4 == 0 else 2
    SHAPE = [P, G * T, D]
    with ExitStack() as ctx:
        def sb(name, shape, dt=F32):
            return ctx.enter_context(nc.sbuf_tensor(f"e_{name}", shape, dt))

        affine = sb("affine", [P, 3, D])
        half = sb("half", [P, G * T])
        total = sb("total", [P, G * T])
        rstd = sb("rstd", [P, G * T])
        sq = sb("sq", SHAPE)
        v = sb("v", SHAPE)
        cen = sb("cen", SHAPE)
        loaded = net.semaphore(ctx, "e_loaded")
        set_up = net.semaphore(ctx, "e_set_up")
        dve_step = net.semaphore(ctx, "e_dve_step")
        var_ready = net.semaphore(ctx, "e_var_ready")
        pool_step = net.semaphore(ctx, "e_pool_step")
        pool_passed = net.semaphore(ctx, "e_pool_passed")
        rstd_ready = net.semaphore(ctx, "e_rstd_ready")
        block = ctx.enter_context(nc.Block())

        @block.sync
        def _(sp):
            for k, name in enumerate(("normf_w", "post_g", "post_b")):
                sp.dma_start(affine[:, k, :], t[name].partition_broadcast(P)).then_inc(loaded, 16)

        @block.gpsimd
        def _(pool):
            nc.gpsimd.memset(half[:], -0.5).then_inc(set_up, 1)
            pool.wait_ge(set_up, 1)
            with pool.Fori(0, 2 * (B // G)) as i:
                wait_all(pool, pool_passed, (var_ready, i + 1))
                st = Steps(pool, pool_step, i)
                st.then(nc.gpsimd.tensor_scalar(rstd[:], total[:], 1.0 / D, EPS, ALU.mult, ALU.add))
                nc.gpsimd.tensor_tensor(rstd[:], rstd[:], half[:], ALU.pow).then_inc(rstd_ready, 1)

        @block.vector
        def _(dve):
            dve.wait_ge(loaded, 48)
            STEPS = 9

            def vec(k):
                return affine[:, k, :].unsqueeze(1).to_broadcast(SHAPE)

            with dve.Fori(0, B // G) as i:
                x = X[:, bass.ds(i * G, G)].rearrange("p b t d -> p (b t) d")
                h = net.H[:, bass.ds(i * G, G)].rearrange("p b t d -> p (b t) d")
                r = rstd[:].unsqueeze(2).to_broadcast(SHAPE)
                st = Steps(dve, dve_step, i * STEPS)
                st.then(nc.vector.tensor_tensor(sq[:], x, x, ALU.mult))
                nc.vector.reduce_sum(total[:], sq[:], axis=AX).then_inc(var_ready, 1)
                dve.wait_ge(rstd_ready, i * 2 + 1)
                st.then(nc.vector.tensor_tensor(v[:], x, r, ALU.mult))
                st.then(nc.vector.tensor_tensor(v[:], v[:], vec(0), ALU.mult))
                centre_and_variance(nc, st, v[:], total[:], cen[:], sq[:], SHAPE).then_inc(var_ready, 1)
                dve.wait_ge(rstd_ready, i * 2 + 2)
                st.then(nc.vector.tensor_tensor(v[:], cen[:], r, ALU.mult))
                st.then(nc.vector.tensor_tensor(v[:], v[:], vec(1), ALU.mult))
                st.then(nc.vector.tensor_tensor(v[:], v[:], vec(2), ALU.add))
                nc.vector.tensor_tensor(h, h, v[:], ALU.add)
                assert st.n == STEPS


def experts_stage(net, name, final_out):
    nc, t, B, S, D, T = net.nc, net.t, net.B, net.S, net.D, net.T
    E = t[f"{name}_gate"].shape[1]
    J = t[f"{name}_w1"].shape[1]
    PER = J // E
    EG = 2
    with ExitStack() as ctx:
        def sb(n, shape, dt=F32):
            return ctx.enter_context(nc.sbuf_tensor(f"{name}_{n}", shape, dt))

        def sem(n):
            return net.semaphore(ctx, f"{name}_{n}")

        def ps(n, shape):
            return ctx.enter_context(nc.psum_tensor(f"{name}_{n}", shape, F32))

        w1 = sb("w1s", [D + 1, J, P])
        w2 = sb("w2s", [P, J, D])
        b2 = sb("b2s", [E, D])
        w_gate = sb("w_gate", [D + 1, E])
        order = sb("order", [P, E])
        affine = sb("affine", [P, 2, D])
        half = sb("half", [P, T])
        total = sb("total", [P, T])
        rstd = sb("rstd", [P, T])
        cen = sb("cen", [P, T, D])
        sq = sb("sq", [P, T, D])
        xn = [sb(f"xn{k}", [P, T, D]) for k in range(2)]
        xT = sb("xT", [D + 1, S])
        g = sb("g", [P, T, E])
        best = sb("best", [P, 4, T])
        mark = [sb(f"mark{k}", [P, T, E]) for k in range(4)]
        prob = sb("prob", [P, 4, T])
        comb = sb("comb", [P, T, E])
        combT = sb("combT", [E, S])
        hid = [sb(f"hid{k}", [P, S]) for k in range(2)]
        weighted = sb("weighted", [P, EG * T, D])
        acc = [sb(f"acc{k}", [P, T, D]) for k in range(2)]
        tr = ps("tr", [P, S])
        small = ps("small", [P, T, E])
        h_ps = [ps(f"h_ps{k}", [P, S]) for k in range(2)]
        y_ps = [ps(f"y_ps{k}", [P, EG * T, D]) for k in range(2)]
        b_ps = ps("b_ps", [P, T, D])
        ct_ps = ps("ct_ps", [P, S])

        loaded, set_up = sem("loaded"), sem("set_up")
        dve_step, var_ready, pool_step, rstd_ready = sem("dve_step"), sem("var_ready"), sem("pool_step"), sem("rstd_ready")
        xn_ready, xT_ps_ready, xT_ready, gates_ready = sem("xn_ready"), sem("xT_ps_ready"), sem("xT_ready"), sem("gates_ready")
        diff_ready, exp_ready = sem("diff_ready"), sem("exp_ready")
        comb_ready, combT_ps_ready, combT_ready, b_ready = sem("comb_ready"), sem("combT_ps_ready"), sem("combT_ready"), sem("b_ready")
        hid_ps_ready, hid_ready, hid_used = sem("hid_ps_ready"), sem("hid_ready"), sem("hid_used")
        y_ready, y_taken, row_done = sem("y_ready"), sem("y_taken"), sem("row_done")
        stored = [sem(f"stored{k}") for k in range(2)]
        pool_passed, pe_passed = sem("pool_passed"), sem("pe_passed")
        block = ctx.enter_context(nc.Block())
        GROUPS = E // EG
        NLN = 2 if final_out is not None else 1
        LOADS = 5 + 2 * (final_out is not None)

        @block.sync
        def _(sp):
            sp.dma_start(w1[:], t[f"{name}_w1"]).then_inc(loaded, 16)
            sp.dma_start(w2[:], t[f"{name}_w2"]).then_inc(loaded, 16)
            sp.dma_start(b2[:], t[f"{name}_b2"]).then_inc(loaded, 16)
            sp.dma_start(w_gate[:], t[f"{name}_gate"]).then_inc(loaded, 16)
            sp.dma_start(order[:], t[f"{name}_order"]).then_inc(loaded, 16)
            if final_out is not None:
                sp.dma_start(affine[:, 0, :], t["f1_gamma"].partition_broadcast(P)).then_inc(loaded, 16)
                sp.dma_start(affine[:, 1, :], t["f1_beta"].partition_broadcast(P)).then_inc(loaded, 16)
                out = final_out.rearrange("b (t p) d -> b p t d", p=P)
                with sp.Fori(0, B // 2) as i:
                    for k in range(2):
                        sp.wait_ge(row_done, i * 2 + (k + 1))
                        sp.dma_start(out[i * 2 + k], acc[k][:]).then_inc(stored[k], 16)
                for k in range(2):
                    sp.wait_ge(stored[k], 16 * (B // 2))

        @block.gpsimd
        def _(pool):
            nc.gpsimd.memset(half[:], -0.5).then_inc(set_up, 1)
            nc.gpsimd.memset(xT[:], 1.0).then_inc(set_up, 1)
            pool.wait_ge(set_up, 2)
            with pool.Fori(0, NLN * B) as i:
                wait_all(pool, pool_passed, (var_ready, i + 1))
                st = Steps(pool, pool_step, i)
                st.then(nc.gpsimd.tensor_scalar(rstd[:], total[:], 1.0 / D, EPS, ALU.mult, ALU.add))
                nc.gpsimd.tensor_tensor(rstd[:], rstd[:], half[:], ALU.pow).then_inc(rstd_ready, 1)

        @block.scalar
        def _(act):
            act.wait_ge(set_up, 2)
            act.sem_inc(hid_ready, CREDIT)
            with act.Fori(0, B) as r:
                act.wait_ge(xT_ps_ready, r + 1)
                nc.scalar.copy(xT[0:D, :], tr[0:D, :]).then_inc(xT_ready, 1)
                act.wait_ge(diff_ready, r + 1)
                nc.scalar.activation(prob[:, 0, :], prob[:, 0, :], ACT.Exp).then_inc(exp_ready, 1)
                act.wait_ge(combT_ps_ready, r + 1)
                nc.scalar.copy(combT[:], ct_ps[0:E, :]).then_inc(combT_ready, 1)
                for j in range(J):
                    act.wait_ge(hid_ps_ready, r * J + (j + 1))
                    act.wait_ge(hid_used, r * J + (j + 1))
                    nc.scalar.activation(hid[j % 2][:], h_ps[j % 2][:], ACT.Relu).then_inc(hid_ready, 1)

        @block.vector
        def _(dve):
            dve.wait_ge(loaded, 16 * LOADS)
            dve.sem_inc(y_taken, CREDIT)
            full = [P, T, D]
            small_shape = [P, T, E]

            def one_row(r, k, turn):
                st = Steps(dve, dve_step, r * STEPS)
                h = net.H[:, bass.ds(r, 1)].rearrange("p a t d -> p (a t) d")
                centre_and_variance(nc, st, h, total[:], cen[:], sq[:], full).then_inc(var_ready, 1)
                dve.wait_ge(rstd_ready, r * NLN + 1)
                nc.vector.tensor_tensor(xn[k][:], cen[:], rstd[:].unsqueeze(2).to_broadcast(full), ALU.mult).then_inc(xn_ready, 1)
                dve.wait_ge(gates_ready, r + 1)
                st.then(nc.vector.tensor_copy(g[:], small[:]))
                rank = order[:].unsqueeze(1).to_broadcast(small_shape)

                def choose(n):
                    m, f = best[:, 2 * n, :], best[:, 2 * n + 1, :]
                    a, b = mark[2 * n], mark[2 * n + 1]
                    st.then(nc.vector.reduce_max(m, g[:], axis=AX))
                    st.then(nc.vector.tensor_tensor(a[:], g[:], m.unsqueeze(2).to_broadcast(small_shape), ALU.is_equal))
                    st.then(nc.vector.tensor_tensor(a[:], a[:], rank, ALU.mult))
                    st.then(nc.vector.reduce_max(f, a[:], axis=AX))
                    st.then(nc.vector.tensor_tensor(b[:], a[:], f.unsqueeze(2).to_broadcast(small_shape), ALU.is_equal))

                choose(0)
                st.then(nc.vector.scalar_tensor_tensor(g[:], mark[1][:], DROPPED, g[:], ALU.mult, ALU.add))
                choose(1)
                nc.vector.tensor_tensor(prob[:, 0, :], best[:, 2, :], best[:, 0, :], ALU.subtract).then_inc(diff_ready, 1)
                dve.wait_ge(exp_ready, r + 1)
                st.then(nc.vector.tensor_scalar(prob[:, 1, :], prob[:, 0, :], 1.0, None, ALU.add))
                st.then(nc.vector.reciprocal(prob[:, 2, :], prob[:, 1, :]))
                st.then(nc.vector.tensor_tensor(prob[:, 3, :], prob[:, 0, :], prob[:, 2, :], ALU.mult))
                p1 = prob[:, 2, :].unsqueeze(2).to_broadcast(small_shape)
                p2 = prob[:, 3, :].unsqueeze(2).to_broadcast(small_shape)
                st.then(nc.vector.tensor_tensor(mark[1][:], mark[1][:], p1, ALU.mult))
                st.then(nc.vector.tensor_tensor(mark[3][:], mark[3][:], p2, ALU.mult))
                st.then(nc.vector.tensor_tensor(comb[:], mark[1][:], mark[3][:], ALU.add))
                dve.sem_inc(comb_ready, 1)
                a = acc[k]
                dve.wait_ge(b_ready, r + 1)
                if final_out is not None and not (isinstance(r, int) and r < 2):
                    dve.wait_ge(stored[k], turn * 16)
                st.then(nc.vector.tensor_copy(a[:], b_ps[:]))
                if final_out is not None:
                    st.then(nc.vector.tensor_tensor(a[:], a[:], xn[k][:], ALU.add))
                for q in range(GROUPS):
                    dve.wait_ge(y_ready, r * GROUPS + (q + 1))
                    shape = [P, T, D]
                    for e in range(EG):
                        c = comb[:, :, q * EG + e].unsqueeze(2).to_broadcast(shape)
                        last = nc.vector.tensor_tensor(weighted[:, e * T:(e + 1) * T, :], y_ps[q % 2][:, e * T:(e + 1) * T, :], c,
                                                       ALU.mult)
                    last.then_inc(y_taken, 1)
                    dve.wait_ge(y_taken, r * GROUPS + (q + 1 + CREDIT))
                    for e in range(EG):
                        st.then(nc.vector.tensor_tensor(a[:], a[:], weighted[:, e * T:(e + 1) * T, :], ALU.add))
                if final_out is None:
                    nc.vector.tensor_tensor(h, h, a[:], ALU.add).then_inc(row_done, 1)
                else:
                    centre_and_variance(nc, st, a[:], total[:], cen[:], sq[:], full).then_inc(var_ready, 1)
                    dve.wait_ge(rstd_ready, r * NLN + 2)
                    st.then(nc.vector.tensor_tensor(a[:], cen[:], rstd[:].unsqueeze(2).to_broadcast(full), ALU.mult))
                    st.then(nc.vector.tensor_tensor(a[:], a[:], affine[:, 0, :].unsqueeze(1).to_broadcast(full), ALU.mult))
                    st.then(nc.vector.tensor_tensor(a[:], a[:], affine[:, 1, :].unsqueeze(1).to_broadcast(full), ALU.add))
                    nc.vector.tensor_tensor(a[:], a[:], h, ALU.add).then_inc(row_done, 1)
                assert st.n == STEPS, st.n

            STEPS = 3 + 1 + 5 + 1 + 5 + 6 + 1 + E + (final_out is not None) * (1 + 3 + 3)
            for k in range(2):
                one_row(k, k, 0)
            if B > 2:
                with dve.Fori(1, B // 2) as i:
                    for k in range(2):
                        one_row(i * 2 + k, k, i)

        @block.tensor
        def _(pe):
            pe.wait_ge(loaded, 16 * LOADS)
            pe.wait_ge(set_up, 2)
            pe.sem_inc(hid_used, CREDIT)

            def one_row(r, k):
                wait_all(pe, pe_passed, (xn_ready, r + 1))
                for m in range(T):
                    last = nc.tensor.transpose(tr[0:D, m * P:(m + 1) * P], xn[k][:, m, :], net.ident[:])
                last.then_inc(xT_ps_ready, 1)
                pe.wait_ge(xT_ready, r + 1)
                for m in range(T):
                    last = nc.tensor.matmul(small[:, m, :], xT[:, m * P:(m + 1) * P], w_gate[:], start=True, stop=True)
                last.then_inc(gates_ready, 1)
                wait_all(pe, pe_passed, (comb_ready, r + 1))
                for m in range(T):
                    last = nc.tensor.transpose(ct_ps[0:E, m * P:(m + 1) * P], comb[:, m, :], net.ident[:])
                last.then_inc(combT_ps_ready, 1)
                pe.wait_ge(combT_ready, r + 1)
                for m in range(T):
                    last = nc.tensor.matmul(b_ps[:, m, :], combT[:, m * P:(m + 1) * P], b2[:], start=True, stop=True)
                last.then_inc(b_ready, 1)

                def hidden(j):
                    pe.wait_ge(hid_ready, r * J + (j + 1))
                    nc.tensor.matmul(h_ps[j % 2][:], w1[:, j, :], xT[:], start=True, stop=True).then_inc(hid_ps_ready, 1)

                def down(j):
                    e = j // PER
                    q = e // EG
                    pe.wait_ge(hid_ready, r * J + (j + 1 + CREDIT))
                    if j % (PER * EG) == 0:
                        pe.wait_ge(y_taken, r * GROUPS + (q + 1))
                    for m in range(T):
                        if PER == 1:
                            last = nc.tensor.matmul(y_ps[q % 2][:, (e % EG) * T + m, :], hid[j % 2][:, m * P:(m + 1) * P], w2[:, j, :],
                                                    start=True, stop=True)
                        else:
                            last = nc.tensor.matmul(y_ps[q % 2][:, (e % EG) * T + m, :], hid[j % 2][:, m * P:(m + 1) * P], w2[:, j, :],
                                                    start=(j % PER == 0 and m == 0 and e % EG == 0),
                                                    stop=(j % PER == PER - 1 and m == T - 1 and e % EG == EG - 1),
                                                    skip_group_check=True)
                    last.then_inc(hid_used, 1)
                    if (j + 1) % (PER * EG) == 0:
                        pe.wait_ge(hid_used, r * J + (j + 1 + CREDIT))
                        pe.sem_inc(y_ready, 1)

                hidden(0)
                for j in range(J):
                    if j + 1 < J:
                        hidden(j + 1)
                    down(j)

            with pe.Fori(0, B // 2) as i:
                for k in range(2):
                    one_row(i * 2 + k, k)


def attention_stage(net):
    nc, t, B, S, D, T = net.nc, net.t, net.B, net.S, net.D, net.T
    with ExitStack() as ctx:
        def sb(n, shape, dt=F32):
            return ctx.enter_context(nc.sbuf_tensor(f"a_{n}", shape, dt))

        def sem(n):
            return net.semaphore(ctx, f"a_{n}")

        def ps(n, shape):
            return ctx.enter_context(nc.psum_tensor(f"a_{n}", shape, F32))

        wq = sb("wq", [D + 1, D])
        wk = sb("wk", [D + 1, D])
        wv = sb("wv", [D, D + 1])
        wo = sb("wo", [D, D])
        wvo = sb("wvo", [D + 1, D + 2])
        bo = sb("bo", [P, D])
        half = sb("half", [P, T])
        total = sb("total", [P, T])
        rstd = sb("rstd", [P, T])
        cen = sb("cen", [P, T, D])
        sq = sb("sq", [P, T, D])
        xn = sb("xn", [P, T, D])
        xT = sb("xT", [D + 1, S])
        qT = sb("qT", [D + 1, S])
        kT = sb("kT", [D + 1, S])
        v = sb("v", [P, T, D + 1])
        mask = sb("mask", [P, T, 2])
        mx = sb("mx", [P, T])
        pT = [sb(f"pT{k}", [P, S]) for k in range(T)]
        factor = sb("factor", [P, T])
        o = sb("o", [P, T, D])
        ring = [ps(f"ring{k}", [P, S]) for k in range(2)]
        s_ps = ps("s_ps", [P, T, S])
        v_ps = ps("v_ps", [P, T, D + 2])
        o_ps = ps("o_ps", [P, T, D + 1])

        loaded, set_up, wvo_ps_ready, wvo_ready = sem("loaded"), sem("set_up"), sem("wvo_ps_ready"), sem("wvo_ready")
        dve_step, var_ready, pool_step, rstd_ready = sem("dve_step"), sem("var_ready"), sem("pool_step"), sem("rstd_ready")
        xn_ready, xT_ps_ready, xT_ready = sem("xn_ready"), sem("xT_ps_ready"), sem("xT_ready")
        q_ps_ready, k_ps_ready, qk_copied, v_ps_ready, v_ready = (sem("q_ps_ready"), sem("k_ps_ready"), sem("qk_copied"),
                                                                 sem("v_ps_ready"), sem("v_ready"))
        s_ready, mx_ready, max_ps_ready, max_ready = sem("s_ready"), sem("mx_ready"), sem("max_ps_ready"), sem("max_ready")
        sT_ready, p_ready, o_ready, row_done = sem("sT_ready"), sem("p_ready"), sem("o_ready"), sem("row_done")
        pool_passed, pe_passed = sem("pool_passed"), sem("pe_passed")
        block = ctx.enter_context(nc.Block())
        LOADS = 6

        @block.sync
        def _(sp):
            sp.dma_start(wq[:], t["a_wq"]).then_inc(loaded, 16)
            sp.dma_start(wk[:], t["a_wk"]).then_inc(loaded, 16)
            sp.dma_start(wv[:], t["a_wv"]).then_inc(loaded, 16)
            sp.dma_start(wo[:], t["a_wo"]).then_inc(loaded, 16)
            sp.dma_start(bo[:], t["a_bo"].partition_broadcast(P)).then_inc(loaded, 16)
            sp.dma_start(wvo[:, D:D + 2], t["a_first"]).then_inc(loaded, 16)

        @block.gpsimd
        def _(pool):
            nc.gpsimd.memset(half[:], -0.5).then_inc(set_up, 1)
            nc.gpsimd.memset(xT[:], 1.0).then_inc(set_up, 1)
            nc.gpsimd.memset(kT[:], 1.0).then_inc(set_up, 1)
            nc.gpsimd.memset(v[:], 1.0).then_inc(set_up, 1)
            pool.wait_ge(set_up, 4)
            with pool.Fori(0, B) as i:
                wait_all(pool, pool_passed, (var_ready, i + 1))
                st = Steps(pool, pool_step, i)
                st.then(nc.gpsimd.tensor_scalar(rstd[:], total[:], 1.0 / D, EPS, ALU.mult, ALU.add))
                nc.gpsimd.tensor_tensor(rstd[:], rstd[:], half[:], ALU.pow).then_inc(rstd_ready, 1)

        @block.scalar
        def _(act):
            act.wait_ge(set_up, 4)
            act.wait_ge(loaded, 16 * LOADS)
            act.wait_ge(wvo_ps_ready, 1)
            nc.scalar.copy(wvo[:, 0:D], ring[0][0:D + 1, 0:D]).then_inc(wvo_ready, 1)
            with act.Fori(0, B) as r:
                act.wait_ge(xT_ps_ready, r + 1)
                nc.scalar.copy(xT[0:D, :], ring[0][0:D, :]).then_inc(xT_ready, 1)
                act.wait_ge(q_ps_ready, r + 1)
                nc.scalar.mul(qT[0:D, :], ring[1][0:D, :], float(D) ** -0.5).then_inc(qk_copied, 1)
                act.wait_ge(k_ps_ready, r + 1)
                nc.scalar.copy(kT[0:D, :], ring[0][0:D, :]).then_inc(qk_copied, 1)
                act.wait_ge(v_ps_ready, r + 1)
                act.wait_ge(o_ready, r)
                nc.scalar.copy(v[:, :, 0:D], v_ps[:, :, 0:D]).then_inc(v_ready, 1)
                act.wait_ge(max_ps_ready, r + 1)
                nc.scalar.mul(qT[D:D + 1, :], ring[0][D:D + 1, :], -1.0).then_inc(max_ready, 1)
                for m in range(T):
                    act.wait_ge(sT_ready, r * T + (m + 1))
                    nc.scalar.activation(pT[m][:], ring[(m + 1) % 2][:], ACT.Exp).then_inc(p_ready, 1)

        @block.vector
        def _(dve):
            dve.wait_ge(loaded, 16 * LOADS)
            full = [P, T, D]
            STEPS = 3 + 2 + 3
            with dve.Fori(0, B) as r:
                st = Steps(dve, dve_step, r * STEPS)
                h = net.H[:, bass.ds(r, 1)].rearrange("p a t d -> p (a t) d")
                centre_and_variance(nc, st, h, total[:], cen[:], sq[:], full).then_inc(var_ready, 1)
                dve.wait_ge(rstd_ready, r + 1)
                nc.vector.tensor_tensor(xn[:], cen[:], rstd[:].unsqueeze(2).to_broadcast(full), ALU.mult).then_inc(xn_ready, 1)
                dve.wait_ge(v_ready, r + 1)
                st.then(nc.vector.tensor_scalar(mask[:], v_ps[:, :, D:D + 2], 0.0, None, ALU.not_equal))
                dve.wait_ge(s_ready, r + 1)
                nc.vector.reduce_max(mx[:], s_ps[:], axis=AX).then_inc(mx_ready, 1)
                dve.wait_ge(o_ready, r + 1)
                st.then(nc.vector.reciprocal(factor[:], o_ps[:, :, D]))
                st.then(nc.vector.tensor_tensor(factor[:], factor[:], mask[:, :, 0], ALU.mult))
                st.then(nc.vector.tensor_tensor(factor[:], factor[:], mask[:, :, 1], ALU.mult))
                st.then(nc.vector.tensor_tensor(o[:], o_ps[:, :, 0:D], factor[:].unsqueeze(2).to_broadcast(full), ALU.mult))
                nc.vector.tensor_tensor(h, h, bo[:].unsqueeze(1).to_broadcast(full), ALU.add).then_inc(row_done, 1)
                dve.wait_ge(row_done, r * 2 + 1)
                nc.vector.tensor_tensor(h, h, o[:], ALU.add).then_inc(row_done, 1)
                assert st.n == STEPS, st.n

        @block.tensor
        def _(pe):
            pe.wait_ge(loaded, 16 * LOADS)
            pe.wait_ge(set_up, 4)
            nc.tensor.matmul(ring[0][0:D + 1, 0:D], wv[:], wo[:], start=True, stop=True).then_inc(wvo_ps_ready, 1)
            pe.wait_ge(wvo_ready, 1)
            with pe.Fori(0, B) as r:
                wait_all(pe, pe_passed, (xn_ready, r + 1), (p_ready, r * T))
                for m in range(T):
                    last = nc.tensor.transpose(ring[0][0:D, m * P:(m + 1) * P], xn[:, m, :], net.ident[:])
                last.then_inc(xT_ps_ready, 1)
                pe.wait_ge(xT_ready, r + 1)
                nc.tensor.matmul(ring[1][0:D, :], wq[:], xT[:], start=True, stop=True).then_inc(q_ps_ready, 1)
                nc.tensor.matmul(ring[0][0:D, :], wk[:], xT[:], start=True, stop=True).then_inc(k_ps_ready, 1)
                for m in range(T):
                    last = nc.tensor.matmul(v_ps[:, m, :], xT[:, m * P:(m + 1) * P], wvo[:], start=True, stop=True)
                last.then_inc(v_ps_ready, 1)
                pe.wait_ge(qk_copied, r * 2 + 2)
                for m in range(T):
                    last = nc.tensor.matmul(s_ps[:, m, :], qT[0:D, m * P:(m + 1) * P], kT[0:D, :], start=True, stop=True)
                last.then_inc(s_ready, 1)
                pe.wait_ge(mx_ready, r + 1)
                for m in range(T):
                    last = nc.tensor.matmul(ring[0][D:D + 1, m * P:(m + 1) * P], mx[:, m:m + 1], net.ident[:], start=True, stop=True)
                last.then_inc(max_ps_ready, 1)
                pe.wait_ge(max_ready, r + 1)
                for m in range(T):
                    if m >= 2:
                        pe.wait_ge(p_ready, r * T + (m - 1))
                    nc.tensor.matmul(ring[(m + 1) % 2][:], kT[:, m * P:(m + 1) * P], qT[:], start=True, stop=True).then_inc(sT_ready, 1)
                pe.wait_ge(v_ready, r + 1)
                pe.wait_ge(p_ready, r * T + T)
                pe.wait_ge(row_done, r * 2)
                for m in range(T):
                    for c in range(T):
                        last = nc.tensor.matmul(o_ps[:, m, :], pT[c][:, m * P:(m + 1) * P], v[:, c, :],
                                                start=(c == 0), stop=(c == T - 1))
                last.then_inc(o_ready, 1)


def tower(nc, t, out, stages=5):
    B, S, D = out.shape
    with ExitStack() as ctx:
        net = Net(nc, ctx, t, B, S, D)
        with nc.sbuf_tensor("X", [P, B, S // P, D], F32) as X:
            token_stage(net, X)
            net.clear_semaphores()
            if stages > 1:
                for layer in range(2):
                    mamba_stage(net, X, layer)
                    net.clear_semaphores()
            if stages > 1:
                mamba_end_stage(net, X)
                net.clear_semaphores()
        if stages > 2:
            experts_stage(net, "f0", None)
            net.clear_semaphores()
        if stages > 3:
            attention_stage(net)
            net.clear_semaphores()
        if stages > 4:
            experts_stage(net, "f1", out)
            net.clear_semaphores()
        else:
            with nc.semaphore("dbg") as dbg, nc.Block() as block:
                @block.sync
                def _(sp):
                    sp.dma_start(out.rearrange("b (t p) d -> p b t d", p=P), net.H[:]).then_inc(dbg, 16)
                    sp.wait_ge(dbg, 16)


def lay_out(i):
    import numpy as np

    def c(*a, axis=0):
        return np.concatenate([np.asarray(x) for x in a], axis)

    a = {k: np.asarray(v) for k, v in i.items()}
    t = {"ident": np.eye(P, dtype=np.float32)}
    for name, k in (("id_event", "x"), ("id_fault", "itok_BS_0_255"), ("id_syscall", "itok_BS_0_511"),
                    ("id_opcode", "itok_BS_0_127"), ("id_transition", "itok_BS_0_63"), ("id_result", "itok_BS_0_3")):
        t[name] = a[k]
    W = a["L0_tok_W"]
    D = W.shape[0]
    tables = [("et", 0, 0, 0), ("fc", 0, 16, 64), ("sc", 1, 0, 0), ("of", 2, 0, 0), ("tt", 3, 0, 0), ("rc", 3, 16, 64)]
    E = np.zeros((33, 4, P), np.float32)
    Wt = np.zeros((32, 4, D), np.float32)
    ids = np.full((P, 4), -1, np.float32)
    for n, (name, tile, row, col) in enumerate(tables):
        e = a[f"L0_tok_E_{name}"]
        E[row:row + 16, tile, col:col + len(e)] = e.T
        Wt[row:row + 16, tile] = W[:, 16 * n:16 * n + 16].T
        ids[col:col + len(e), tile] = np.arange(len(e))
    E[32, 0, 0:64] = 1
    b = np.zeros((1, 4, D), np.float32)
    b[0, 0] = a["L0_tok_b"]
    t |= {"tok_E": E, "tok_W": Wt, "tok_b": b, "vocab": ids, "tok_gamma": a["L0_tok_gamma"], "tok_beta": a["L0_tok_beta"],
          "pre_g": a["L0_attn_pre_g"], "pre_b": a["L0_attn_pre_b"], "normf_w": a["L0_attn_normf_w"],
          "post_g": a["L0_attn_post_g"], "post_b": a["L0_attn_post_b"]}
    inw = a["L0_attn_inproj_w"].transpose(0, 2, 1)
    NL, _, E2 = inw.shape
    NC = E2 // 2 // P

    def channels(x):
        return np.ascontiguousarray(x.reshape(NL, NC, P, *x.shape[2:]).swapaxes(1, 2))

    xp = a["L0_attn_xproj_w"]
    R, NS = a["L0_attn_dtproj_w"].shape[2], a["L0_attn_A_log"].shape[2]
    bc = xp[:, R:]
    rows = c(bc, bc, bc, xp[:, :R], axis=1).transpose(0, 2, 1)
    t |= {"m_in_w": c(inw, inw, axis=1), "m_norm_w": c(a["L0_attn_norm_w"], a["L0_attn_norm_w"], axis=1)[:, :, None],
          "m_conv_w": a["L0_attn_conv_w"][:, :, 0, :].transpose(0, 2, 1), "m_conv_b": channels(a["L0_attn_conv_b"]),
          "m_xproj_w": channels(rows), "m_dtproj_w": a["L0_attn_dtproj_w"].transpose(0, 2, 1),
          "m_dtproj_b": channels(a["L0_attn_dtproj_b"]), "m_A_log": channels(a["L0_attn_A_log"]),
          "m_D": channels(a["L0_attn_D_param"]), "m_out_w": channels(a["L0_attn_outproj_w"].transpose(0, 2, 1))}

    def experts(name, w1, b1, w2, b2, gate, gate_b):
        E, H, D = w1.shape
        J = E * H // P
        t[f"{name}_w1"] = c(w1.reshape(J * P, D).T, b1.reshape(1, J * P)).reshape(D + 1, J, P)
        t[f"{name}_w2"] = w2.reshape(J, P, D).transpose(1, 0, 2)
        t[f"{name}_b2"] = b2
        t[f"{name}_gate"] = c(gate, gate_b[None])
        t[f"{name}_order"] = np.tile(np.arange(E, 0, -1, dtype=np.float32), (P, 1))

    experts("f0", a["L0_ffn_W1"], a["L0_ffn_b1"], a["L0_ffn_W2"].transpose(0, 2, 1), a["L0_ffn_b2"],
            a["L0_ffn_Wg"].T, a["L0_ffn_bg"])
    experts("f1", a["L1_ffn_w1"].transpose(0, 2, 1), a["L1_ffn_b1"], a["L1_ffn_w2"], a["L1_ffn_b2"],
            a["L1_ffn_gate_w"], a["L1_ffn_gate_b"])
    t |= {"f1_gamma": a["L1_ffn_gamma"], "f1_beta": a["L1_ffn_beta"]}
    wq, wk, bq, bk = a["L1_attn_Wq"], a["L1_attn_Wk"], a["L1_attn_bq"], a["L1_attn_bk"]
    t |= {"a_wq": c(wq.T, bq[None]), "a_wk": c(wk.T, bk[None]), "a_wv": c(a["L1_attn_Wv"], a["L1_attn_bv"][:, None], axis=1),
          "a_wo": a["L1_attn_Wo"].T, "a_bo": a["L1_attn_bo"],
          "a_first": c(c(wq[0:1].T, bq[None, 0:1]), c(wk[0:1].T, bk[None, 0:1]), axis=1)}
    return {k: np.ascontiguousarray(v) for k, v in t.items()}


def kernel(**inputs):
    import numpy as _np
    import concourse.bacc as _bacc
    from concourse.bass_utils import run_bass_kernel_spmd as _run

    nc = _bacc.Bacc("TRN2", target_bir_lowering=False, num_devices=1)
    arrays = lay_out(inputs)
    t = {k: nc.dram_tensor(f"in_{k}", v.shape, mybir.dt.from_np(v.dtype), kind="ExternalInput").ap() for k, v in arrays.items()}
    B, S = inputs["x"].shape
    D = inputs["L0_tok_W"].shape[0]
    out = nc.dram_tensor("out", (B, S, D), F32, kind="ExternalOutput").ap()
    tower(nc, t, out)
    return _run(nc, [{f"in_{k}": v for k, v in arrays.items()}], core_ids=[0]).results[0]["out"]
```

```python
from contextlib import ExitStack

import concourse.bass as bass
from concourse import mybir

ALU = mybir.AluOpType
ACT = mybir.ActivationFunctionType
F32 = mybir.dt.float32
BF16 = mybir.dt.bfloat16
I32 = mybir.dt.int32
AX = mybir.AxisListType.X

P = 128
CREDIT = 2
DEEP = 4
EPS = 1e-5
DROPPED = -1e30


def wait_all(eng, passed, *waits):
    for sem, value in waits:
        eng.wait_ge(sem, value)
    eng.sem_inc(passed, 1)


class Steps:

    def __init__(self, eng, sem, base, passed=None):
        self.eng, self.sem, self.base, self.n, self.passed = eng, sem, base, 0, passed

    def then(self, ins):
        ins.then_inc(self.sem, 1)
        self.n += 1
        if self.passed is not None:
            wait_all(self.eng, self.passed, (self.sem, self.base + self.n))
        else:
            self.eng.wait_ge(self.sem, self.base + self.n)


def spread(ap, shape):
    return ap.to_broadcast(shape)


class Net:

    def __init__(self, nc, ctx, t, B, S, D):
        self.nc, self.t, self.B, self.S, self.D = nc, t, B, S, D
        self.T = S // P
        self.H = ctx.enter_context(nc.sbuf_tensor("H", [P, B, self.T, D], F32))
        self.ident = ctx.enter_context(nc.sbuf_tensor("ident", [P, P], F32))
        self.used = []

    def semaphore(self, ctx, name):
        sem = ctx.enter_context(self.nc.semaphore(name))
        self.used.append(sem)
        return sem

    def clear_semaphores(self):
        numbers = [s.num for s in self.used]
        self.used = []
        with self.nc.Block() as block:
            @block.gpsimd
            def _(pool):
                pool.sem_clear(range(min(numbers), max(numbers) + 1))


def centre_and_variance(nc, st, x, total, centred, square, shape):
    D = shape[-1]
    st.then(nc.vector.reduce_sum(total, x, axis=AX))
    st.then(nc.vector.scalar_tensor_tensor(centred, total.unsqueeze(2).to_broadcast(shape), -1.0 / D, x,
                                           ALU.mult, ALU.add))
    st.then(nc.vector.tensor_tensor(square, centred, centred, ALU.mult))
    return nc.vector.reduce_sum(total, square, axis=AX)


def token_stage(net, X):
    nc, t, B, S, D, T = net.nc, net.t, net.B, net.S, net.D, net.T
    PAIRS = B // 2
    N = 2 * S
    NT = 2 * T
    NK = 4
    KW = t["tok_W"].shape[0]
    SHAPE = [P, NT, D]
    LN_STEPS = 3
    with ExitStack() as ctx:
        def sb(name, shape, dt=F32):
            return ctx.enter_context(nc.sbuf_tensor(name, shape, dt))

        def sem(name):
            return net.semaphore(ctx, name)

        emb = sb("t_emb", [KW + 1, NK, P])
        w = sb("w", [KW + 1, NK, D])
        absw = sb("absw", [KW, NK, D])
        wsum = sb("wsum", [KW, 1])
        ones = sb("ones", [KW, KW])
        thr = sb("thr", [KW, 3])
        pos = sb("pos", [KW, NK, D])
        neg = sb("neg", [KW, NK, D])
        weff = sb("weff", [KW + 1, NK, D])
        table = sb("table", [P, NK, 3, D], BF16)
        rest = sb("rest", [P, NK, D])
        vocab = sb("vocab", [P, NK])
        affine = sb("affine", [P, 4, D])
        half = sb("half", [P, NT])
        ids = [sb(f"ids{k}", [P, NK, N], I32) for k in range(2)]
        hot = [sb(f"hot{k}", [P, NK, N], BF16) for k in range(2)]
        total = sb("total", [P, NT])
        rstd = sb("rstd", [P, NT])
        cen = sb("cen", SHAPE)
        sq = sb("sq", SHAPE)
        z = [ctx.enter_context(nc.psum_tensor(f"z{k}", SHAPE, F32)) for k in range(2)]
        tab_ps = ctx.enter_context(nc.psum_tensor("tab_ps", [P, NK, D], F32))
        sum_ps = ctx.enter_context(nc.psum_tensor("sum_ps", [KW, 1], F32))

        loaded = sem("loaded")
        set_up = sem("set_up")
        wsum_ready = sem("wsum_ready")
        scale_ready = sem("scale_ready")
        weff_ready = sem("weff_ready")
        tables_ready = sem("tables_ready")
        table_split = sem("table_split")
        ids_loaded = [sem(f"ids_loaded{k}") for k in range(2)]
        hot_ready = sem("hot_ready")
        z_ready = sem("z_ready")
        dve_step = sem("dve_step")
        var_ready = sem("var_ready")
        pool_step = sem("pool_step")
        pool_passed, dve_passed = sem("pool_passed"), sem("dve_passed")
        rstd_ready = sem("rstd_ready")
        x_done = sem("x_done")
        block = ctx.enter_context(nc.Block())

        IDS = [("id_event", 0, 0, 64), ("id_fault", 0, 64, 64), ("id_syscall", 1, 0, P), ("id_opcode", 2, 0, P),
               ("id_transition", 3, 0, 64), ("id_result", 3, 64, 64)]

        @block.sync
        def _(sp):
            sp.dma_start(net.ident[:], t["ident"]).then_inc(loaded, 16)
            sp.dma_start(emb[:], t["tok_E"]).then_inc(loaded, 16)
            sp.dma_start(w[0:KW], t["tok_W"]).then_inc(loaded, 16)
            sp.dma_start(weff[KW:KW + 1], t["tok_b"]).then_inc(loaded, 16)
            sp.dma_start(vocab[:], t["vocab"]).then_inc(loaded, 16)
            for k, name in enumerate(("tok_gamma", "tok_beta", "pre_g", "pre_b")):
                sp.dma_start(affine[:, k, :], t[name].partition_broadcast(P)).then_inc(loaded, 16)

            def load_ids(p, k):
                for name, tile, first, rows in IDS:
                    src = t[name].rearrange("(q two) s -> q (two s)", two=2)[p].partition_broadcast(rows)
                    sp.dma_start(ids[k][first:first + rows, tile, :], src).then_inc(ids_loaded[k], 16)

            load_ids(0, 0)
            load_ids(1, 1) if PAIRS > 1 else None
            if PAIRS > 2:
                with sp.Fori(0, PAIRS // 2 - 1) as i:
                    for k in range(2):
                        sp.wait_ge(hot_ready, i * 2 + (k + 1))
                        load_ids(i * 2 + (k + 2), k)

        @block.gpsimd
        def _(pool):
            nc.gpsimd.memset(ones[:], 1.0).then_inc(set_up, 1)
            nc.gpsimd.memset(half[:], -0.5).then_inc(set_up, 1)
            pool.wait_ge(set_up, 2)

            def one_pair(p):
                for n in range(3):
                    st = Steps(pool, pool_step, p * 3 + n)
                    wait_all(pool, pool_passed, (var_ready, p * 3 + (n + 1)))
                    st.then(nc.gpsimd.tensor_scalar(rstd[:], total[:], 1.0 / D, EPS, ALU.mult, ALU.add))
                    nc.gpsimd.tensor_tensor(rstd[:], rstd[:], half[:], ALU.pow).then_inc(rstd_ready, 1)

            with pool.Fori(0, PAIRS) as p:
                one_pair(p)

        @block.vector
        def _(dve):
            dve.wait_ge(loaded, 16 * 9)
            st = Steps(dve, weff_ready, 0)
            st.then(nc.vector.scalar_tensor_tensor(absw[:], w[0:KW], -1.0, w[0:KW], ALU.mult, ALU.max))
            nc.vector.reduce_sum(wsum[:], absw[:].rearrange("p k d -> p (k d)"), axis=AX).then_inc(wsum_ready, 1)
            dve.wait_ge(scale_ready, 1)
            nw = 1.0 / (96 * D)
            st.then(nc.vector.tensor_scalar(thr[:, 0:1], sum_ps[:], nw, None, ALU.mult))
            st.then(nc.vector.tensor_scalar(thr[:, 1:2], thr[:, 0:1], 1e-8, 0.5, ALU.add, ALU.mult))
            st.then(nc.vector.tensor_scalar(thr[:, 2:3], thr[:, 1:2], -1.0, None, ALU.mult))
            st.then(nc.vector.tensor_scalar(pos[:], w[0:KW], thr[:, 1:2], thr[:, 0:1], ALU.is_gt, ALU.mult))
            st.then(nc.vector.tensor_scalar(neg[:], w[0:KW], thr[:, 2:3], thr[:, 0:1], ALU.is_lt, ALU.mult))
            st.then(nc.vector.tensor_tensor(pos[:], pos[:], neg[:], ALU.subtract))
            st.then(nc.vector.tensor_tensor(pos[:], pos[:], w[0:KW], ALU.subtract))
            st.then(nc.vector.tensor_tensor(weff[0:KW], w[0:KW], pos[:], ALU.add))
            dve.wait_ge(tables_ready, 1)
            st = Steps(dve, table_split, 0)
            st.then(nc.vector.tensor_copy(table[:, :, 0, :], tab_ps[:]))
            st.then(nc.vector.tensor_tensor(rest[:], tab_ps[:], table[:, :, 0, :], ALU.subtract))
            st.then(nc.vector.tensor_copy(table[:, :, 1, :], rest[:]))
            st.then(nc.vector.tensor_tensor(table[:, :, 2, :], rest[:], table[:, :, 1, :], ALU.subtract))

            def one_hot(p, k, turn):
                dve.wait_ge(ids_loaded[k], turn * (16 * len(IDS)) + 16 * len(IDS))
                if not (isinstance(p, int) and p < 2):
                    dve.wait_ge(z_ready, p - 1)
                for tile in range(NK):
                    last = nc.vector.tensor_scalar(hot[k][:, tile, :], ids[k][:, tile, :], vocab[:, tile:tile + 1],
                                                   None, ALU.is_equal)
                last.then_inc(hot_ready, 1)

            def normalise(p, k):
                xr = X[:, bass.ds(p * 2, 2)].rearrange("p b t d -> p (b t) d")
                hr = net.H[:, bass.ds(p * 2, 2)].rearrange("p b t d -> p (b t) d")
                st = Steps(dve, dve_step, p * STEPS, passed=dve_passed)
                dve.wait_ge(z_ready, p + 1)
                for n, (src, dst) in enumerate(((z[k][:], hr), (hr, xr), (xr, xr))):
                    centre_and_variance(nc, st, src, total[:], cen[:], sq[:], SHAPE).then_inc(var_ready, 1)
                    dve.wait_ge(rstd_ready, p * 3 + (n + 1))
                    st.then(nc.vector.tensor_tensor(dst, cen[:], rstd[:].unsqueeze(2).to_broadcast(SHAPE), ALU.mult))
                    if n != 1:
                        g, b = affine[:, n, :], affine[:, n + 1, :]
                        st.then(nc.vector.tensor_tensor(dst, dst, g.unsqueeze(1).to_broadcast(SHAPE), ALU.mult))
                        st.then(nc.vector.tensor_tensor(dst, dst, b.unsqueeze(1).to_broadcast(SHAPE), ALU.add))
                    
                assert st.n == STEPS

            STEPS = 3 * 4 + 4
            one_hot(0, 0, 0)
            if PAIRS > 1:
                one_hot(1, 1, 0)
            normalise(0, 0)
            if PAIRS > 2:
                with dve.Fori(0, PAIRS // 2 - 1) as i:
                    one_hot(i * 2 + 2, 0, i + 1)
                    normalise(i * 2 + 1, 1)
                    one_hot(i * 2 + 3, 1, i + 1)
                    normalise(i * 2 + 2, 0)
            if PAIRS > 1:
                normalise(PAIRS - 1, 1)

        @block.tensor
        def _(pe):
            pe.wait_ge(set_up, 2)
            pe.wait_ge(wsum_ready, 1)
            nc.tensor.matmul(sum_ps[:], ones[:], wsum[:], start=True, stop=True).then_inc(scale_ready, 1)
            pe.wait_ge(weff_ready, 9)
            for tile in range(NK):
                last = nc.tensor.matmul(tab_ps[:, tile, :], emb[:, tile, :], weff[:, tile, :], start=True, stop=True)
            last.then_inc(tables_ready, 1)
            pe.wait_ge(table_split, 4)

            def project(p, k):
                pe.wait_ge(hot_ready, p + 1)
                if not (isinstance(p, int) and p < 2):
                    pe.wait_ge(rstd_ready, p * 3 - 5)
                for m in range(NT):
                    for tile in range(NK):
                        for part in range(3):
                            last = nc.tensor.matmul(z[k][:, m, :], hot[k][:, tile, m * P:(m + 1) * P],
                                                    table[:, tile, part, :], start=(tile == 0 and part == 0),
                                                    stop=(tile == NK - 1 and part == 2))
                last.then_inc(z_ready, 1)

            project(0, 0)
            if PAIRS > 1:
                project(1, 1)
            if PAIRS > 2:
                with pe.Fori(0, PAIRS // 2 - 1) as i:
                    for k in range(2):
                        project(i * 2 + (k + 2), k)


AT = {'gated': 4, 'rms': 1, 'copy_x': 4, 'silu': 7, 'high': 9, 'middle': 10, 'spe': 9, 'spl': 12, 'skip': 1, 'resid': 5, 'squares': 0, 'norm': 2, 'rest': 9, 'low': 10, 'lost': 10, 'transp': 1, 'u0': 2, 'u1': 3, 'g0': 3, 'g1': 5, 'ssm': 5, 'dt': 7, 'out': 2, 'sizes': 14, 'exact': 15, 'dtu': 15, 'b_lead': 2, 'ahead': 5}


def mamba_stage(net, X, layer):
    nc, t, B, S, D, T = net.nc, net.t, net.B, net.S, net.D, net.T
    NC, NS = t["m_A_log"].shape[2:4]
    R = t["m_dtproj_w"].shape[1]
    BC = 2 * NS
    DT0 = 3 * BC
    L = layer
    with ExitStack() as ctx:
        def sb(name, shape, dt=F32):
            return ctx.enter_context(nc.sbuf_tensor(f"m{L}_{name}", shape, dt))

        def sem(name):
            return net.semaphore(ctx, f"m{L}_{name}")

        def bank(name):
            return ctx.enter_context(nc.psum_tensor(f"m{L}_{name}", [P, S], F32))

        w_in = sb("w_in", [P, 2 * NC * P])
        w_conv = sb("w_conv", [P, 2, NC * P])
        w_norm = sb("w_norm", [P, 1])
        w_u = sb("w_u", [P, 2, NC * P])
        w_g = sb("w_g", [D, NC * P])
        conv_b = sb("conv_b", [P, NC])
        w_x = sb("w_x", [P, NC, DT0 + R])
        w_dt = sb("w_dt", [P, NC * P])
        dt_b = sb("dt_b", [P, NC])
        decay = sb("decay", [P, NC, NS])
        skip = sb("skip", [P, NC])
        w_out = sb("w_out", [P, NC, D])
        pick = sb("pick", [DT0, BC, P], BF16)
        pick_row = sb("pick_row", [DT0, BC])
        half = sb("half", [P, T])
        sq = sb("sq", [P, T, D])
        ssq = sb("ssq", [P, T])
        rstd = sb("rstd", [P, T])
        xn = sb("xn", [P, T, 2, D])
        xT = sb("xT", [P, S + 3])
        u = [sb(f"u{k}", [P, NC, S]) for k in range(2)]
        gate = [sb(f"gate{k}", [P, NC, S]) for k in range(2)]
        dt = [sb(f"dt{k}", [P, NC, S]) for k in range(2)]
        dtu = [sb(f"dtu{k}", [P, NC, S]) for k in range(2)]
        parts = [sb(f"parts{k}", [DT0, S], BF16) for k in range(2)]
        dt_low = sb("dt_low", [P, S])
        rest = sb("rest", [DT0, S])
        mid = sb("mid", [DT0, S], BF16)
        pos = sb("pos", [P, NC, S])
        ex = sb("ex", [P, NC, S])
        one_ex = sb("one_ex", [P, NC, S])
        log = sb("log", [P, NC, S])
        lost = sb("lost", [P, NC, S])
        Bs = [sb(f"Bs{k}", [P, S]) for k in range(DEEP)]
        dA = [sb(f"dA{k}", [P, NC, S]) for k in range(2)]
        dBu = [sb(f"dBu{k}", [P, NC, S]) for k in range(DEEP)]
        hs = [sb(f"hs{k}", [P, NC, S]) for k in range(2)]
        hC = [sb(f"hC{k}", [P, NC, S]) for k in range(2)]
        yv = sb("yv", [P, NC, S])
        yg = sb("yg", [P, NC, S])
        W0, W1, W2 = bank("W0"), bank("W1"), bank("W2")
        Bb = bank("Bb")
        Cb = [bank(f"Cb{k}") for k in range(2)]
        Y = [bank(f"Y{c}") for c in range(NC)]

        loaded, pads, w_step, weights_ready = sem("loaded"), sem("pads"), sem("w_step"), sem("weights_ready")
        decay_ready = sem("decay_ready")
        sq_ready, ssq_ready, var_eps, rstd_ready = sem("sq_ready"), sem("ssq_ready"), sem("var_eps"), sem("rstd_ready")
        xn_ready, xT_ps_ready, xT_ready = sem("xn_ready"), sem("xT_ps_ready"), sem("xT_ready")
        proj_ready, silu_done, ssm_ready = sem("proj_ready"), sem("silu_done"), sem("ssm_ready")
        hi_ready, rest_ready, mid_ready = sem("hi_ready"), sem("rest_ready"), sem("mid_ready")
        mid_tmp, lo_ready = sem("mid_tmp"), sem("lo_ready")
        dt_ps_ready, dt_ps_read = sem("dt_ps_ready"), sem("dt_ps_read")
        abs_ready, ex_ready, one_ex_ready = sem("abs_ready"), sem("ex_ready"), sem("one_ex_ready")
        log_ready, lost_ready = sem("log_ready"), sem("lost_ready")
        dt_sum, dt_ready, dtu_ready = sem("dt_sum"), sem("dt_ready"), sem("dtu_ready")
        bb_ready, bb_copied, dbu_ready, da_ready = sem("bb_ready"), sem("bb_copied"), sem("dbu_ready"), sem("da_ready")
        cb_ready, scan_done, hc_ready, summed = sem("cb_ready"), sem("scan_done"), sem("hc_ready"), sem("summed")
        y_read, yg_ready, out_ready, x_done = sem("y_read"), sem("yg_ready"), sem("out_ready"), sem("x_done")
        pool_passed = sem("pool_passed")
        block = ctx.enter_context(nc.Block())

        def rows(eng, first, body):
            first()
            body(0, 0, False, True)
            if B > 2:
                with eng.Fori(0, B // 2 - 1) as i:
                    for k in range(2):
                        body(i * 2 + (k + 1), 1 - k, True, True)
            body(B - 1, 1, True, False)

        LOADS = 12
        B_LEAD = AT["b_lead"]
        AHEAD = AT["ahead"]

        @block.sync
        def _(sp):
            sp.dma_start(w_in[:], t["m_in_w"][L]).then_inc(loaded, 16)
            for pair in range(2):
                for copy in range(2):
                    sp.dma_start(w_conv[copy * D:(copy + 1) * D, pair, :],
                                 t["m_conv_w"][L, 3 - 2 * pair - copy].partition_broadcast(D)).then_inc(loaded, 16)
            sp.dma_start(w_norm[:], t["m_norm_w"][L]).then_inc(loaded, 16)
            sp.dma_start(conv_b[:], t["m_conv_b"][L]).then_inc(loaded, 16)
            sp.dma_start(w_x[:], t["m_xproj_w"][L]).then_inc(loaded, 16)
            sp.dma_start(w_dt[DT0:DT0 + R, :], t["m_dtproj_w"][L]).then_inc(loaded, 16)
            sp.dma_start(dt_b[:], t["m_dtproj_b"][L]).then_inc(loaded, 16)
            sp.dma_start(skip[:], t["m_D"][L]).then_inc(loaded, 16)
            sp.dma_start(w_out[:], t["m_out_w"][L]).then_inc(loaded, 16)
            sp.dma_start(decay[:], t["m_A_log"][L]).then_inc(decay_ready, 16)

        @block.gpsimd
        def _(pool):
            nc.gpsimd.memset(half[:], -0.5).then_inc(pads, 1)
            nc.gpsimd.memset(xT[:], 0.0).then_inc(pads, 1)
            pool.wait_ge(pads, 2)
            pool.sem_inc(dbu_ready, DEEP)

            def inverse_rms(r):
                wait_all(pool, pool_passed, (ssq_ready, r + 1))
                nc.gpsimd.tensor_scalar(rstd[:], ssq[:], 1.0 / D, EPS, ALU.mult, ALU.add).then_inc(var_eps, 1)
                pool.wait_ge(var_eps, r + 1)
                nc.gpsimd.tensor_tensor(rstd[:], rstd[:], half[:], ALU.pow).then_inc(rstd_ready, 1)

            def step_sizes(r):
                pool.wait_ge(log_ready, r + 1)
                nc.gpsimd.tensor_tensor(pos[:], pos[:], log[:], ALU.add).then_inc(dt_sum, 1)

            def step_sizes_exact(r, k):
                pool.wait_ge(dt_sum, r + 1)
                pool.wait_ge(lost_ready, r + 1)
                if not (isinstance(r, int) and r == 0):
                    pool.wait_ge(da_ready, r * NS - NS)
                nc.gpsimd.tensor_tensor(dt[k][:], pos[:], lost[:], ALU.subtract).then_inc(dt_ready, 1)

            def weighted_u(r, k):
                pool.wait_ge(dt_ready, r + 1)
                pool.wait_ge(silu_done, r * 4 + 4)
                nc.gpsimd.tensor_tensor(dtu[k][:], dt[k][:], u[k][:], ALU.mult).then_inc(dtu_ready, 1)
                pool.wait_ge(dtu_ready, r + 1)

            def state_input(r, k, n):
                q = r * NS + n
                pool.wait_ge(bb_copied, q + 2)
                pool.wait_ge(scan_done, q + 1)
                nc.gpsimd.tensor_tensor(dBu[n % DEEP][:], dtu[k][:], Bs[n % DEEP][:].unsqueeze(1).to_broadcast([P, NC, S]),
                                        ALU.mult).then_inc(dbu_ready, 1)

            def gated(r, k):
                pool.wait_ge(y_read, r + 1)
                pool.wait_ge(out_ready, r)
                nc.gpsimd.tensor_tensor(yg[:], yv[:], gate[k][:], ALU.mult).then_inc(yg_ready, 1)

            def first():
                inverse_rms(0)
                step_sizes(0)
                step_sizes_exact(0, 0)
                weighted_u(0, 0)

            def body(r, k, back, more):
                for n in range(NS):
                    state_input(r, k, n)
                    if back and n == AT["gated"]:
                        gated(r - 1, 1 - k)
                    if more and n == AT["rms"]:
                        inverse_rms(r + 1)
                    if more and n == AT["sizes"]:
                        step_sizes(r + 1)
                    if more and n == AT["exact"]:
                        step_sizes_exact(r + 1, 1 - k)
                    if more and n == AT["dtu"]:
                        weighted_u(r + 1, 1 - k)
                if not more:
                    gated(r, k)

            rows(pool, first, body)

        @block.scalar
        def _(act):
            act.wait_ge(decay_ready, 16)
            nc.scalar.activation(decay[:], decay[:], ACT.Exp).then_inc(decay_ready, 1)
            act.wait_ge(decay_ready, 17)
            nc.scalar.mul(decay[:], decay[:], -1.0).then_inc(decay_ready, 1)
            act.wait_ge(decay_ready, 18)
            act.wait_ge(loaded, 16 * LOADS)
            act.wait_ge(pads, 2)
            act.sem_inc(bb_copied, 1)

            def copy_xT(r):
                act.wait_ge(xT_ps_ready, r + 1)
                act.wait_ge(proj_ready, r * 4)
                nc.scalar.copy(xT[0:D, 2:S + 2], W0[0:D, :])
                nc.scalar.copy(xT[D:2 * D, 3:S + 3], W0[D:2 * D, :]).then_inc(xT_ready, 1)

            def activate(r, k):
                for j in range(2 * NC):
                    W = (W1, W2, W0, W1)[j]
                    dst = (u if j < NC else gate)[k][:, j % NC, :]
                    act.wait_ge(proj_ready, r * 4 + (j + 1))
                    if not (isinstance(r, int) and r == 0) and j == 0:
                        act.wait_ge(yg_ready, r - 1)
                    bias = conv_b[:, j:j + 1] if j < NC else 0.0
                    nc.scalar.activation(dst, W[:], ACT.Silu, bias=bias).then_inc(silu_done, 1)

            def high_part(r, k):
                act.wait_ge(ssm_ready, r + 1)
                act.wait_ge(dt_ps_ready, r * 2)
                if not (isinstance(r, int) and r == 0):
                    act.wait_ge(cb_ready, r * NS - NS)
                nc.scalar.copy(dt_low[DT0:DT0 + R, :], W2[DT0:DT0 + R, :])
                nc.scalar.copy(parts[k][:], W2[0:DT0, :]).then_inc(hi_ready, 1)

            def middle_part(r, k):
                m, lo = slice(BC, 2 * BC), slice(2 * BC, 3 * BC)
                act.wait_ge(rest_ready, r + 1)
                nc.scalar.copy(parts[k][m, :], rest[m, :]).then_inc(mid_ready, 1)
                act.wait_ge(lo_ready, r)
                nc.scalar.copy(mid[lo, :], rest[lo, :]).then_inc(mid_tmp, 1)

            def softplus_exp(r):
                act.wait_ge(dt_ready, r)
                act.wait_ge(lost_ready, r)
                for c in range(NC):
                    W = (W0, W1)[c]
                    act.wait_ge(dt_ps_ready, r * 2 + (c + 1))
                    nc.scalar.activation(ex[:, c, :], W[:], ACT.Abs, bias=dt_b[:, c:c + 1]).then_inc(abs_ready, 1)
                    nc.scalar.activation(pos[:, c, :], W[:], ACT.Relu, bias=dt_b[:, c:c + 1]).then_inc(dt_ps_read, 1)
                act.wait_ge(abs_ready, r * 2 + 2)
                nc.scalar.activation(ex[:], ex[:], ACT.Exp, scale=-1.0).then_inc(ex_ready, 1)

            def softplus_log(r):
                act.wait_ge(ex_ready, r + 1)
                nc.scalar.add(one_ex[:], ex[:], 1.0).then_inc(one_ex_ready, 1)
                act.wait_ge(one_ex_ready, r + 1)
                nc.scalar.activation(log[:], one_ex[:], ACT.Ln).then_inc(log_ready, 1)

            def copy_b(r, n):
                q = r * NS + n
                act.wait_ge(bb_ready, q + 1)
                act.wait_ge(dbu_ready, q + 1)
                nc.scalar.copy(Bs[n % DEEP][:], Bb[:]).then_inc(bb_copied, 1)

            def decays(r, k, n):
                q = r * NS + n
                if n == 0:
                    act.wait_ge(dt_ready, r + 1)
                act.wait_ge(scan_done, q + (DEEP - 1))
                for c in range(NC):
                    last = nc.scalar.activation(dA[n % 2][:, c, :], dt[k][:, c, :], ACT.Exp, scale=decay[:, c, n:n + 1])
                last.then_inc(da_ready, 1)

            def first():
                copy_xT(0)
                activate(0, 0)
                high_part(0, 0)
                middle_part(0, 0)
                softplus_exp(0)
                softplus_log(0)
                for n in range(B_LEAD):
                    copy_b(0, n)

            def body(r, k, back, more):
                for n in range(NS):
                    if n + B_LEAD < NS:
                        copy_b(r, n + B_LEAD)
                    elif more:
                        copy_b(r + 1, n + B_LEAD - NS)
                    decays(r, k, n)
                    if more and n == AT["copy_x"]:
                        copy_xT(r + 1)
                    if more and n == AT["silu"]:
                        activate(r + 1, 1 - k)
                    if more and n == AT["high"]:
                        high_part(r + 1, 1 - k)
                    if more and n == AT["middle"]:
                        middle_part(r + 1, 1 - k)
                    if more and n == AT["spe"]:
                        softplus_exp(r + 1)
                    if more and n == AT["spl"]:
                        softplus_log(r + 1)

            rows(act, first, body)

        @block.vector
        def _(dve):
            dve.wait_ge(loaded, 16 * LOADS)
            st = Steps(dve, w_step, 0)
            st.then(nc.vector.tensor_tensor(pick_row[:], net.ident[0:DT0, 0:BC], net.ident[0:DT0, BC:2 * BC], ALU.add))
            st.then(nc.vector.tensor_tensor(pick_row[:], pick_row[:], net.ident[0:DT0, 2 * BC:3 * BC], ALU.add))
            st.then(nc.vector.tensor_copy(pick[:], pick_row[:].unsqueeze(2).to_broadcast([DT0, BC, P])))
            st.then(nc.vector.tensor_scalar(w_in[:], w_in[:], w_norm[:, 0:1], None, ALU.mult))
            st.then(nc.vector.tensor_tensor(w_u[:], w_conv[:], w_in[:, 0:NC * P].unsqueeze(1).to_broadcast([P, 2, NC * P]),
                                            ALU.mult))
            nc.vector.tensor_copy(w_g[:], w_in[0:D, NC * P:2 * NC * P]).then_inc(weights_ready, 1)
            dve.sem_inc(scan_done, DEEP)
            dve.sem_inc(hc_ready, CREDIT)

            def row(r):
                return X[:, bass.ds(r, 1)].rearrange("p a t d -> p (a t) d")

            def squares(r):
                nc.vector.tensor_tensor(sq[:], row(r), row(r), ALU.mult).then_inc(sq_ready, 1)
                dve.wait_ge(sq_ready, r + 1)
                nc.vector.reduce_sum(ssq[:], sq[:], axis=AX).then_inc(ssq_ready, 1)

            def normalise(r):
                dve.wait_ge(rstd_ready, r + 1)
                dve.wait_ge(xT_ps_ready, r)
                shape = [P, T, 2, D]
                nc.vector.tensor_tensor(xn[:], row(r).unsqueeze(2).to_broadcast(shape),
                                        rstd[:].unsqueeze(2).unsqueeze(3).to_broadcast(shape),
                                        ALU.mult).then_inc(xn_ready, 1)

            def remainder(r, k):
                dve.wait_ge(hi_ready, r + 1)
                dve.wait_ge(mid_ready, r)
                dve.wait_ge(lo_ready, r)
                nc.vector.tensor_tensor(rest[:], W2[0:DT0, :], parts[k][:], ALU.subtract).then_inc(rest_ready, 1)

            def low_part(r, k):
                lo = slice(2 * BC, 3 * BC)
                dve.wait_ge(mid_tmp, r + 1)
                nc.vector.tensor_tensor(parts[k][lo, :], rest[lo, :], mid[lo, :], ALU.subtract).then_inc(lo_ready, 1)

            def rounding_loss(r):
                dve.wait_ge(one_ex_ready, r + 1)
                dve.wait_ge(dt_ready, r)
                nc.vector.scalar_tensor_tensor(lost[:], one_ex[:], -1.0, ex[:], ALU.add, ALU.subtract).then_inc(lost_ready, 1)

            def scan(r, n):
                q = r * NS + n
                dve.wait_ge(da_ready, q + 1)
                dve.wait_ge(dbu_ready, q + (DEEP + 1))
                dve.wait_ge(hc_ready, q + 1)
                for c in range(NC):
                    last = nc.vector.tensor_tensor_scan(hs[n % 2][:, c, :], dA[n % 2][:, c, :], dBu[n % DEEP][:, c, :], 0.0,
                                                        ALU.mult, ALU.add)
                last.then_inc(scan_done, 1)

            def times_c(r, n):
                q = r * NS + n
                dve.wait_ge(scan_done, q + (DEEP + 1))
                dve.wait_ge(cb_ready, q + 1)
                dve.wait_ge(summed, q + 1)
                nc.vector.tensor_tensor(hC[n % 2][:], hs[n % 2][:], Cb[n % 2][:].unsqueeze(1).to_broadcast([P, NC, S]),
                                        ALU.mult).then_inc(hc_ready, 1)

            def skip_path(r, k):
                dve.wait_ge(summed, r * NS + (CREDIT + NS))
                dve.wait_ge(yg_ready, r)
                for c in range(NC):
                    last = nc.vector.scalar_tensor_tensor(yv[:, c, :], u[k][:, c, :], skip[:, c:c + 1], Y[c][:],
                                                          ALU.mult, ALU.add)
                last.then_inc(y_read, 1)

            def residual(r):
                dve.wait_ge(out_ready, r + 1)
                nc.vector.tensor_tensor(row(r), row(r), W2[:, 0:T * D].rearrange("p (t d) -> p t d", d=D),
                                        ALU.add).then_inc(x_done, 1)

            def first():
                squares(0)
                normalise(0)
                remainder(0, 0)
                low_part(0, 0)
                rounding_loss(0)

            def body(r, k, back, more):
                for n in range(NS):
                    scan(r, n)
                    if n:
                        times_c(r, n - 1)
                    if back and n == 0:
                        times_c(r - 1, NS - 1)
                    if back and n == AT["skip"]:
                        skip_path(r - 1, 1 - k)
                    if back and n == AT["resid"]:
                        residual(r - 1)
                    if more and n == AT["squares"]:
                        squares(r + 1)
                    if more and n == AT["norm"]:
                        normalise(r + 1)
                    if more and n == AT["rest"]:
                        remainder(r + 1, 1 - k)
                    if more and n == AT["low"]:
                        low_part(r + 1, 1 - k)
                    if more and n == AT["lost"]:
                        rounding_loss(r + 1)
                if not more:
                    times_c(r, NS - 1)
                    skip_path(r, k)
                    residual(r)

            rows(dve, first, body)

        @block.tensor
        def _(pe):
            pe.wait_ge(weights_ready, 1)
            pe.wait_ge(loaded, 16 * LOADS)
            pe.sem_inc(summed, CREDIT)

            def transpose(r):
                pe.wait_ge(xn_ready, r + 1)
                pe.wait_ge(dt_ps_read, r * NC)
                for m in range(T):
                    last = nc.tensor.transpose(W0[:, m * P:(m + 1) * P], xn[:, m].rearrange("p a d -> p (a d)"), net.ident[:])
                last.then_inc(xT_ps_ready, 1)

            def project_u(r, c):
                pe.wait_ge(xT_ready, r + 1)
                if c == 1 and not (isinstance(r, int) and r == 0):
                    pe.wait_ge(x_done, r - 1)
                W = (W1, W2)[c]
                for pair in range(2):
                    last = nc.tensor.matmul(W[:], w_u[:, pair, c * P:(c + 1) * P], xT[:, 2 - 2 * pair:2 - 2 * pair + S],
                                            start=(pair == 0), stop=(pair == 1))
                last.then_inc(proj_ready, 1)

            def project_gate(r, c):
                if c == 1:
                    pe.wait_ge(silu_done, r * 4 + 1)
                W = (W0, W1)[c]
                nc.tensor.matmul(W[:], w_g[:, c * P:(c + 1) * P], xT[0:D, 2:2 + S], start=True, stop=True).then_inc(proj_ready, 1)

            def project_ssm(r, k):
                pe.wait_ge(silu_done, r * 4 + 2)
                for c in range(NC):
                    last = nc.tensor.matmul(W2[0:DT0 + R, :], w_x[:, c, :], u[k][:, c, :], start=(c == 0), stop=(c == NC - 1))
                last.then_inc(ssm_ready, 1)

            def project_dt(r):
                pe.wait_ge(hi_ready, r + 1)
                pe.wait_ge(silu_done, r * 4 + 4)
                for c in range(NC):
                    nc.tensor.matmul((W0, W1)[c][:], w_dt[DT0:DT0 + R, c * P:(c + 1) * P], dt_low[DT0:DT0 + R, :],
                                     start=True, stop=True).then_inc(dt_ps_ready, 1)

            def b_row(r, k, n):
                q = r * NS + n
                if n == 0:
                    pe.wait_ge(mid_ready, r + 1)
                    pe.wait_ge(lo_ready, r + 1)
                pe.wait_ge(bb_copied, q + 1)
                nc.tensor.matmul(Bb[:], pick[:, n, :], parts[k][:], start=True, stop=True).then_inc(bb_ready, 1)

            def c_row(r, k, n):
                q = r * NS + n
                if n == 0:
                    pe.wait_ge(mid_ready, r + 1)
                    pe.wait_ge(lo_ready, r + 1)
                pe.wait_ge(hc_ready, q + 1)
                nc.tensor.matmul(Cb[n % 2][:], pick[:, NS + n, :], parts[k][:], start=True, stop=True).then_inc(cb_ready, 1)

            def sum_state(r, n):
                q = r * NS + n
                pe.wait_ge(hc_ready, q + (CREDIT + 1))
                if n == 0:
                    pe.wait_ge(y_read, r)
                for c in range(NC):
                    last = nc.tensor.matmul(Y[c][:], net.ident[:], hC[n % 2][:, c, :], start=(n == 0), stop=(n == NS - 1))
                last.then_inc(summed, 1)

            def output(r, more):
                pe.wait_ge(yg_ready, r + 1)
                if more:
                    pe.wait_ge(rest_ready, r + 2)
                else:
                    pe.wait_ge(x_done, r)
                for m in range(T):
                    for c in range(NC):
                        last = nc.tensor.matmul(W2[:, m * D:(m + 1) * D], yg[:, c, m * P:(m + 1) * P], w_out[:, c, :],
                                                start=(c == 0), stop=(c == NC - 1))
                last.then_inc(out_ready, 1)


            def first():
                transpose(0)
                project_u(0, 0)
                project_u(0, 1)
                project_gate(0, 0)
                project_gate(0, 1)
                project_ssm(0, 0)
                project_dt(0)
                c_row(0, 0, 0)
                for n in range(AHEAD):
                    b_row(0, 0, n)

            def body(r, k, back, more):
                for n in range(NS):
                    if n + AHEAD < NS:
                        b_row(r, k, n + AHEAD)
                    elif more:
                        b_row(r + 1, 1 - k, n + AHEAD - NS)
                    if n + 1 < NS:
                        c_row(r, k, n + 1)
                    elif more:
                        c_row(r + 1, 1 - k, 0)
                    if more and n == AT["transp"]:
                        transpose(r + 1)
                    if more and n == AT["u0"]:
                        project_u(r + 1, 0)
                    if more and n == AT["u1"]:
                        project_u(r + 1, 1)
                    if more and n == AT["g0"]:
                        project_gate(r + 1, 0)
                    if more and n == AT["g1"]:
                        project_gate(r + 1, 1)
                    if more and n == AT["ssm"]:
                        project_ssm(r + 1, 1 - k)
                    if more and n == AT["dt"]:
                        project_dt(r + 1)
                    sum_state(r, n)
                    if back and n == AT["out"]:
                        output(r - 1, True)
                if not more:
                    output(r, False)

            rows(pe, first, body)


def mamba_end_stage(net, X):
    nc, t, B, S, D, T = net.nc, net.t, net.B, net.S, net.D, net.T
    G = 4 if B % 4 == 0 else 2
    SHAPE = [P, G * T, D]
    with ExitStack() as ctx:
        def sb(name, shape, dt=F32):
            return ctx.enter_context(nc.sbuf_tensor(f"e_{name}", shape, dt))

        affine = sb("affine", [P, 3, D])
        half = sb("half", [P, G * T])
        total = sb("total", [P, G * T])
        rstd = sb("rstd", [P, G * T])
        sq = sb("sq", SHAPE)
        v = sb("v", SHAPE)
        cen = sb("cen", SHAPE)
        loaded = net.semaphore(ctx, "e_loaded")
        set_up = net.semaphore(ctx, "e_set_up")
        dve_step = net.semaphore(ctx, "e_dve_step")
        var_ready = net.semaphore(ctx, "e_var_ready")
        pool_step = net.semaphore(ctx, "e_pool_step")
        pool_passed = net.semaphore(ctx, "e_pool_passed")
        rstd_ready = net.semaphore(ctx, "e_rstd_ready")
        block = ctx.enter_context(nc.Block())

        @block.sync
        def _(sp):
            for k, name in enumerate(("normf_w", "post_g", "post_b")):
                sp.dma_start(affine[:, k, :], t[name].partition_broadcast(P)).then_inc(loaded, 16)

        @block.gpsimd
        def _(pool):
            nc.gpsimd.memset(half[:], -0.5).then_inc(set_up, 1)
            pool.wait_ge(set_up, 1)
            with pool.Fori(0, 2 * (B // G)) as i:
                wait_all(pool, pool_passed, (var_ready, i + 1))
                st = Steps(pool, pool_step, i)
                st.then(nc.gpsimd.tensor_scalar(rstd[:], total[:], 1.0 / D, EPS, ALU.mult, ALU.add))
                nc.gpsimd.tensor_tensor(rstd[:], rstd[:], half[:], ALU.pow).then_inc(rstd_ready, 1)

        @block.vector
        def _(dve):
            dve.wait_ge(loaded, 48)
            STEPS = 9

            def vec(k):
                return affine[:, k, :].unsqueeze(1).to_broadcast(SHAPE)

            with dve.Fori(0, B // G) as i:
                x = X[:, bass.ds(i * G, G)].rearrange("p b t d -> p (b t) d")
                h = net.H[:, bass.ds(i * G, G)].rearrange("p b t d -> p (b t) d")
                r = rstd[:].unsqueeze(2).to_broadcast(SHAPE)
                st = Steps(dve, dve_step, i * STEPS)
                st.then(nc.vector.tensor_tensor(sq[:], x, x, ALU.mult))
                nc.vector.reduce_sum(total[:], sq[:], axis=AX).then_inc(var_ready, 1)
                dve.wait_ge(rstd_ready, i * 2 + 1)
                st.then(nc.vector.tensor_tensor(v[:], x, r, ALU.mult))
                st.then(nc.vector.tensor_tensor(v[:], v[:], vec(0), ALU.mult))
                centre_and_variance(nc, st, v[:], total[:], cen[:], sq[:], SHAPE).then_inc(var_ready, 1)
                dve.wait_ge(rstd_ready, i * 2 + 2)
                st.then(nc.vector.tensor_tensor(v[:], cen[:], r, ALU.mult))
                st.then(nc.vector.tensor_tensor(v[:], v[:], vec(1), ALU.mult))
                st.then(nc.vector.tensor_tensor(v[:], v[:], vec(2), ALU.add))
                nc.vector.tensor_tensor(h, h, v[:], ALU.add)
                assert st.n == STEPS


AT_E = {'centre': 0, 'variance': 1, 'take': 3, 'xn': 3, 'turn_x': 5, 'turn_x2': 1, 'gates': 7, 'best': 8, 'second': 9,
        'softmax': 10, 'parts': 12, 'turn_weights': 13, 'turn_y': 2}
AT_A = {'yT': 1, 'xT': 5, 'xT2': 6, 'exp': 10, 'combT': 14}


def experts_stage(net, name, final_out):
    nc, t, B, S, D, T = net.nc, net.t, net.B, net.S, net.D, net.T
    E = t[f"{name}_gate"].shape[1]
    J = t[f"{name}_w1"].shape[1]
    PER = J // E
    LAG = 2
    RING = 4
    PARTS = 3 * E
    final = final_out is not None
    with ExitStack() as ctx:
        def sb(n, shape, dt=F32):
            return ctx.enter_context(nc.sbuf_tensor(f"{name}_{n}", shape, dt))

        def sem(n):
            return net.semaphore(ctx, f"{name}_{n}")

        def bank(n):
            return ctx.enter_context(nc.psum_tensor(f"{name}_{n}", [P, S], F32))

        w1 = [sb(f"w1s{k}", [2 * D, J, P], BF16) for k in range(3)]
        w1_whole = sb("w1_whole", [2 * D, J, P])
        b1 = sb("b1s", [P, J])
        w2 = sb("w2s", [P, J, D])
        b2 = sb("b2s", [PARTS, D])
        w_gate = [sb(f"w_gate{k}", [2 * D, E], BF16) for k in range(3)]
        w_gate_whole = sb("w_gate_whole", [2 * D, E])
        gate_b = sb("gate_b", [P, E])
        order = sb("order", [P, E])
        affine = sb("affine", [P, 2, D])
        pick_row = sb("pick_row", [PARTS, E])
        pick = sb("pick", [PARTS, E, P], BF16)
        ident16 = sb("ident16", [P, P], BF16)
        half = sb("half", [P, T])
        total, rstd = sb("total", [P, T]), sb("rstd", [P, T])
        cen, sq = sb("cen", [P, T, D]), sb("sq", [P, T, D])
        xn = [sb(f"xn{k}", [P, T, D]) for k in range(2)]
        x_rest = sb("x_rest", [P, T, D])
        x_parts = sb("x_parts", [P, 2, T, 2, D], BF16)
        xT = [sb(f"xT{k}", [2 * D, 2, S], BF16) for k in range(2)]
        g = sb("g", [P, T, E])
        best = sb("best", [P, 4, T])
        mark = [sb(f"mark{k}", [P, T, E]) for k in range(4)]
        prob = sb("prob", [P, 4, T])
        comb = sb("comb", [P, T, E])
        parts = sb("parts", [P, T, 3, E], BF16)
        combT16 = [sb(f"combT16_{k}", [PARTS, S], BF16) for k in range(2)]
        combT = [sb(f"combT{k}", [PARTS, S]) for k in range(2)]
        hid = [sb(f"hid{k}", [P, S]) for k in range(RING)]
        relu = [sb(f"relu{k}", [P, S]) for k in range(2)]
        yT = sb("yT", [D, S])
        joined = sb("joined", [P, T, D])
        total2, rstd2 = sb("total2", [P, T]), sb("rstd2", [P, T])
        cen2, sq2 = sb("cen2", [P, T, D]), sb("sq2", [P, T, D])
        result = [sb(f"result{k}", [P, T, D]) for k in range(2)]
        h_ps = [bank(f"h_ps{k}") for k in range(2)]
        c_ps = [bank(f"c_ps{k}") for k in range(2)]
        y_ps = [bank(f"y_ps{k}") for k in range(2)]
        front_ps, back_ps = bank("front_ps"), bank("back_ps")

        loaded, set_up, made = sem("loaded"), sem("set_up"), sem("made")
        front_step, back_step, pool_step = sem("front_step"), sem("back_step"), sem("pool_step")
        var_ready, rstd_ready, xn_ready = sem("var_ready"), sem("rstd_ready"), sem("xn_ready")
        xT_ps_ready, xT_ready, gates_ready = sem("xT_ps_ready"), sem("xT_ready"), sem("gates_ready")
        diff_ready, exp_ready, parts_ready = sem("diff_ready"), sem("exp_ready"), sem("parts_ready")
        combT_ps_ready, combT_ready = sem("combT_ps_ready"), sem("combT_ready")
        relu_ready = sem("relu_ready")
        h_ready, hid_ready = sem("h_ready"), sem("hid_ready")
        y_ready, yT_ready, back_ready, back_taken = sem("y_ready"), sem("yT_ready"), sem("back_ready"), sem("back_taken")
        var2_ready, row_done = sem("var2_ready"), sem("row_done")
        stored = [sem(f"stored{k}") for k in range(2)]
        pool_passed, pe_passed, dve_passed = sem("pool_passed"), sem("pe_passed"), sem("dve_passed")
        block = ctx.enter_context(nc.Block())
        LOADS = 7 + 2 * final
        full, small = [P, T, D], [P, T, E]
        POOL_STEPS = 1 + (1 + 1 + 3) * final
        MADE = 4 + 2 * 5
        FRONT_STEPS = 3 + 5 + 4 + 4 + 4 + 3 + 3 + 4
        BACK_STEPS = 4

        def row_of_H(r):
            return net.H[:, bass.ds(r, 1)].rearrange("p a t d -> p (a t) d")

        @block.sync
        def _(sp):
            sp.dma_start(w1_whole[:], t[f"{name}_w1"]).then_inc(loaded, 16)
            sp.dma_start(b1[:], t[f"{name}_b1"]).then_inc(loaded, 16)
            sp.dma_start(w2[:], t[f"{name}_w2"]).then_inc(loaded, 16)
            sp.dma_start(b2[:], t[f"{name}_b2"]).then_inc(loaded, 16)
            sp.dma_start(w_gate_whole[:], t[f"{name}_gate"]).then_inc(loaded, 16)
            sp.dma_start(gate_b[:], t[f"{name}_gate_b"].partition_broadcast(P)).then_inc(loaded, 16)
            sp.dma_start(order[:], t[f"{name}_order"]).then_inc(loaded, 16)
            if final:
                sp.dma_start(affine[:, 0, :], t["f1_gamma"].partition_broadcast(P)).then_inc(loaded, 16)
                sp.dma_start(affine[:, 1, :], t["f1_beta"].partition_broadcast(P)).then_inc(loaded, 16)
                out = final_out.rearrange("b (t p) d -> b p t d", p=P)
                with sp.Fori(0, B // 2) as i:
                    for k in range(2):
                        sp.wait_ge(row_done, i * 2 + (k + 1))
                        sp.dma_start(out[i * 2 + k], result[k][:]).then_inc(stored[k], 16)
                for k in range(2):
                    sp.wait_ge(stored[k], 16 * (B // 2))

        @block.gpsimd
        def _(pool):
            nc.gpsimd.memset(half[:], -0.5).then_inc(set_up, 1)
            pool.wait_ge(set_up, 1)
            pool.wait_ge(loaded, 16 * LOADS)
            if not final:
                with pool.Fori(0, B) as r:
                    wait_all(pool, pool_passed, (var_ready, r + 1))
                    st = Steps(pool, pool_step, r)
                    st.then(nc.gpsimd.tensor_scalar(rstd[:], total[:], 1.0 / D, EPS, ALU.mult, ALU.add))
                    nc.gpsimd.tensor_tensor(rstd[:], rstd[:], half[:], ALU.pow).then_inc(rstd_ready, 1)
                return

            def front(r, st):
                wait_all(pool, pool_passed, (var_ready, r + 1))
                st.then(nc.gpsimd.tensor_scalar(rstd[:], total[:], 1.0 / D, EPS, ALU.mult, ALU.add))
                nc.gpsimd.tensor_tensor(rstd[:], rstd[:], half[:], ALU.pow).then_inc(rstd_ready, 1)

            def back(r, k, first, st):
                wait_all(pool, pool_passed, (var2_ready, r + 1))
                st.then(nc.gpsimd.tensor_scalar(rstd2[:], total2[:], 1.0 / D, EPS, ALU.mult, ALU.add))
                st.then(nc.gpsimd.tensor_tensor(rstd2[:], rstd2[:], half[:], ALU.pow))
                if not first:
                    wait_all(pool, pool_passed, (stored[k], 16 * ((r - k) // 2) if isinstance(r, int) else turn[0] * 16))
                y = result[k]
                st.then(nc.gpsimd.tensor_tensor(y[:], cen2[:], rstd2[:].unsqueeze(2).to_broadcast(full), ALU.mult))
                st.then(nc.gpsimd.tensor_tensor(y[:], y[:], affine[:, 0, :].unsqueeze(1).to_broadcast(full), ALU.mult))
                st.then(nc.gpsimd.tensor_tensor(y[:], y[:], affine[:, 1, :].unsqueeze(1).to_broadcast(full), ALU.add))
                nc.gpsimd.tensor_tensor(y[:], y[:], row_of_H(r), ALU.add).then_inc(row_done, 1)

            turn = [0]
            front(0, Steps(pool, pool_step, 0, pool_passed))
            front(1, Steps(pool, pool_step, 1, pool_passed))
            for r in range(2):
                st = Steps(pool, pool_step, 2 + r * POOL_STEPS, pool_passed)
                front(r + 2, st)
                back(r, r, True, st)
            with pool.Fori(1, B // 2 - 1) as i:
                turn[0] = i
                for k in range(2):
                    st = Steps(pool, pool_step, (i * 2 + k) * POOL_STEPS + 2, pool_passed)
                    front(i * 2 + (k + 2), st)
                    back(i * 2 + k, k, False, st)
            st = Steps(pool, pool_step, (B - 2) * POOL_STEPS + 2, pool_passed)
            for k in range(2):
                back(B - 2 + k, k, False, st)

        @block.scalar
        def _(act):
            act.wait_ge(loaded, 16 * LOADS)

            def front(r, k, e):
                if e == AT_A["xT"]:
                    act.wait_ge(xT_ps_ready, r * 2 + 1)
                    nc.scalar.copy(xT[k][:, 0, :], front_ps[:]).then_inc(xT_ready, 1)
                if e == AT_A["xT2"]:
                    act.wait_ge(xT_ps_ready, r * 2 + 2)
                    nc.scalar.copy(xT[k][:, 1, :], front_ps[:]).then_inc(xT_ready, 1)
                if e == AT_A["exp"]:
                    act.wait_ge(diff_ready, r + 1)
                    nc.scalar.activation(prob[:, 0, :], prob[:, 0, :], ACT.Exp).then_inc(exp_ready, 1)
                if e == AT_A["combT"]:
                    act.wait_ge(combT_ps_ready, r + 1)
                    nc.scalar.copy(combT16[k][:], front_ps[0:PARTS, :]).then_inc(combT_ready, 1)
                    nc.scalar.copy(combT[k][:], front_ps[0:PARTS, :]).then_inc(combT_ready, 1)

            def back(r, k):
                act.wait_ge(y_ready, r + 1)
                nc.scalar.copy(yT[:], y_ps[k][0:D, :]).then_inc(yT_ready, 1)

            def one_row(r, k, number=None):
                for j in range(J):
                    act.wait_ge(h_ready, r * J + (j + 1))
                    act.wait_ge(hid_ready, r * J + (j + 1))
                    nc.scalar.activation(relu[j % 2][:], h_ps[j % 2][:], ACT.Relu, bias=b1[:, j:j + 1]).then_inc(relu_ready, 1)
                    if j == AT_A["yT"] and number != 0:
                        back(r - 1, 1 - k)
                    if number != B - 1:
                        front(r + 1, 1 - k, j)

            for j in range(J):
                front(0, 0, j)
            one_row(0, 0, 0)
            one_row(1, 1, 1)
            with act.Fori(1, B // 2 - 1) as i:
                for k in range(2):
                    one_row(i * 2 + k, k)
            one_row(B - 2, 0, B - 2)
            one_row(B - 1, 1, B - 1)
            back(B - 1, 1)

        @block.vector
        def _(dve):
            dve.wait_ge(loaded, 16 * LOADS)
            st = Steps(dve, made, 0)
            st.then(nc.vector.tensor_tensor(pick_row[:], net.ident[0:PARTS, 0:E], net.ident[0:PARTS, E:2 * E], ALU.add))
            st.then(nc.vector.tensor_tensor(pick_row[:], pick_row[:], net.ident[0:PARTS, 2 * E:3 * E], ALU.add))
            st.then(nc.vector.tensor_copy(pick[:], pick_row[:].unsqueeze(2).to_broadcast([PARTS, E, P])))
            st.then(nc.vector.tensor_copy(ident16[:], net.ident[:]))
            for whole, part in ((w1_whole, w1), (w_gate_whole, w_gate)):
                st.then(nc.vector.tensor_copy(part[0][:], whole[:]))
                st.then(nc.vector.tensor_copy(part[2][:], whole[:]))
                st.then(nc.vector.tensor_tensor(whole[:], whole[:], part[0][:], ALU.subtract))
                st.then(nc.vector.tensor_copy(part[1][:], whole[:]))
                st.then(nc.vector.tensor_tensor(part[2][0:D], whole[0:D], part[1][0:D], ALU.subtract))
            assert st.n == MADE
            dve.sem_inc(hid_ready, LAG)

            def front(r, k, n, st):
                a, f, b, c = mark
                first, found, second, found2 = (best[:, m, :] for m in range(4))
                if n == AT_E["centre"]:
                    h = row_of_H(r)
                    st.then(nc.vector.reduce_sum(total[:], h, axis=AX))
                    st.then(nc.vector.scalar_tensor_tensor(cen[:], total[:].unsqueeze(2).to_broadcast(full), -1.0 / D, h,
                                                           ALU.mult, ALU.add))
                if n == AT_E["variance"]:
                    st.then(nc.vector.tensor_tensor(sq[:], cen[:], cen[:], ALU.mult))
                    nc.vector.reduce_sum(total[:], sq[:], axis=AX).then_inc(var_ready, 1)
                if n == AT_E["xn"]:
                    dve.wait_ge(rstd_ready, r + 1)
                    if final and not (isinstance(r, int) and r < 2):
                        dve.wait_ge(back_taken, r - 1)
                    st.then(nc.vector.tensor_tensor(xn[k][:], cen[:], rstd[:].unsqueeze(2).to_broadcast(full), ALU.mult))
                    st.then(nc.vector.tensor_copy(x_parts[:, 0, :, 0, :], xn[k][:]))
                    st.then(nc.vector.tensor_tensor(x_rest[:], xn[k][:], x_parts[:, 0, :, 0, :], ALU.subtract))
                if n == AT_E["xn"] + 1:
                    st.then(nc.vector.tensor_copy(x_parts[:, 0, :, 1, :], x_rest[:]))
                    dve.sem_inc(xn_ready, 1)
                    st.then(nc.vector.tensor_tensor(x_parts[:, 1, :, 1, :], x_rest[:], x_parts[:, 0, :, 1, :], ALU.subtract))
                    nc.vector.tensor_copy(x_parts[:, 1, :, 0, :], x_parts[:, 0, :, 0, :]).then_inc(xn_ready, 1)
                rank = order[:].unsqueeze(1).to_broadcast(small)
                if n == AT_E["best"]:
                    dve.wait_ge(gates_ready, r + 1)
                    st.then(nc.vector.tensor_tensor(g[:], front_ps[:, 0:T * E].rearrange("p (t e) -> p t e", t=T),
                                                    gate_b[:].unsqueeze(1).to_broadcast(small), ALU.add))
                    st.then(nc.vector.reduce_max(first, g[:], axis=AX))
                    st.then(nc.vector.tensor_tensor(a[:], g[:], first.unsqueeze(2).to_broadcast(small), ALU.is_equal))
                    st.then(nc.vector.tensor_tensor(a[:], a[:], rank, ALU.mult))
                if n == AT_E["best"] + 1:
                    st.then(nc.vector.reduce_max(found, a[:], axis=AX))
                    st.then(nc.vector.tensor_tensor(f[:], a[:], found.unsqueeze(2).to_broadcast(small), ALU.is_equal))
                    st.then(nc.vector.scalar_tensor_tensor(g[:], f[:], DROPPED, g[:], ALU.mult, ALU.add))
                    st.then(nc.vector.reduce_max(second, g[:], axis=AX))
                if n == AT_E["second"]:
                    nc.vector.tensor_tensor(prob[:, 0, :], second, first, ALU.subtract).then_inc(diff_ready, 1)
                    st.then(nc.vector.tensor_tensor(b[:], g[:], second.unsqueeze(2).to_broadcast(small), ALU.is_equal))
                    st.then(nc.vector.tensor_tensor(b[:], b[:], rank, ALU.mult))
                    st.then(nc.vector.reduce_max(found2, b[:], axis=AX))
                    st.then(nc.vector.tensor_tensor(c[:], b[:], found2.unsqueeze(2).to_broadcast(small), ALU.is_equal))
                if n == AT_E["softmax"]:
                    dve.wait_ge(exp_ready, r + 1)
                    st.then(nc.vector.tensor_scalar(prob[:, 1, :], prob[:, 0, :], 1.0, None, ALU.add))
                    st.then(nc.vector.reciprocal(prob[:, 2, :], prob[:, 1, :]))
                    st.then(nc.vector.tensor_tensor(prob[:, 3, :], prob[:, 0, :], prob[:, 2, :], ALU.mult))
                if n == AT_E["softmax"] + 1:
                    st.then(nc.vector.tensor_tensor(f[:], f[:], prob[:, 2, :].unsqueeze(2).to_broadcast(small), ALU.mult))
                    st.then(nc.vector.tensor_tensor(c[:], c[:], prob[:, 3, :].unsqueeze(2).to_broadcast(small), ALU.mult))
                    st.then(nc.vector.tensor_tensor(comb[:], f[:], c[:], ALU.add))
                if n == AT_E["parts"]:
                    st.then(nc.vector.tensor_copy(parts[:, :, 0, :], comb[:]))
                    st.then(nc.vector.tensor_tensor(comb[:], comb[:], parts[:, :, 0, :], ALU.subtract))
                    st.then(nc.vector.tensor_copy(parts[:, :, 1, :], comb[:]))
                    st.then(nc.vector.tensor_tensor(parts[:, :, 2, :], comb[:], parts[:, :, 1, :], ALU.subtract))
                    dve.sem_inc(parts_ready, 1)

            def back(r, k, n, st, first):
                if n == AT_E["take"]:
                    dve.wait_ge(back_ready, r + 1)
                    y = back_ps[:, 0:T * D].rearrange("p (t d) -> p t d", t=T)
                    if not final:
                        nc.vector.tensor_tensor(row_of_H(r), row_of_H(r), y, ALU.add).then_inc(back_taken, 1)
                    else:
                        nc.vector.tensor_tensor(joined[:], xn[k][:], y, ALU.add).then_inc(back_taken, 1)
                if final and n == AT_E["take"] + 1:
                    dve.wait_ge(back_taken, r + 1)
                    if not first:
                        dve.wait_ge(row_done, r)
                    st.then(nc.vector.reduce_sum(total2[:], joined[:], axis=AX))
                    st.then(nc.vector.scalar_tensor_tensor(cen2[:], total2[:].unsqueeze(2).to_broadcast(full), -1.0 / D, joined[:],
                                                           ALU.mult, ALU.add))
                if final and n == AT_E["take"] + 2:
                    st.then(nc.vector.tensor_tensor(sq2[:], cen2[:], cen2[:], ALU.mult))
                    st.then(nc.vector.reduce_sum(total2[:], sq2[:], axis=AX))
                    dve.sem_inc(var2_ready, 1)

            def one_row(r, k, number=None):
                ahead = Steps(dve, front_step, (r + 1) * FRONT_STEPS)
                done = Steps(dve, back_step, (r - 1) * BACK_STEPS)
                for j in range(J):
                    dve.wait_ge(relu_ready, r * J + (j + 1))
                    nc.vector.tensor_tensor(hid[j % RING][:], relu[j % 2][:], c_ps[(j // PER) % 2][:], ALU.mult).then_inc(hid_ready, 1)
                    if number != 0:
                        back(r - 1, 1 - k, j, done, number == 1)
                    if number != B - 1:
                        front(r + 1, 1 - k, j, ahead)

            st = Steps(dve, front_step, 0)
            for j in range(J):
                front(0, 0, j, st)
            assert st.n == FRONT_STEPS, st.n
            one_row(0, 0, 0)
            one_row(1, 1, 1)
            with dve.Fori(1, B // 2 - 1) as i:
                for k in range(2):
                    one_row(i * 2 + k, k)
            one_row(B - 2, 0, B - 2)
            one_row(B - 1, 1, B - 1)
            st = Steps(dve, back_step, (B - 1) * BACK_STEPS)
            for j in range(J):
                back(B - 1, 1, j, st, False)

        @block.tensor
        def _(pe):
            pe.wait_ge(loaded, 16 * LOADS)
            pe.wait_ge(made, MADE)

            def front(r, k, n):
                for p in range(2):
                    if n == AT_E["turn_x"] + p * AT_E["turn_x2"]:
                        if isinstance(r, int) and r == 0 and p == 0:
                            wait_all(pe, pe_passed, (xn_ready, 1))
                        elif p == 0:
                            wait_all(pe, pe_passed, (combT_ready, r * 2), (xn_ready, r * 2 + 1))
                        else:
                            wait_all(pe, pe_passed, (xT_ready, r * 2 + 1), (xn_ready, r * 2 + 2))
                        for m in range(T):
                            last = nc.tensor.matmul(front_ps[:, m * P:(m + 1) * P], x_parts[:, p, m].rearrange("p a d -> p (a d)"),
                                                    ident16[:], start=True, stop=True)
                        last.then_inc(xT_ps_ready, 1)
                if n == AT_E["gates"]:
                    pe.wait_ge(xT_ready, r * 2 + 2)
                    for m in range(T):
                        for p in range(3):
                            last = nc.tensor.matmul(front_ps[:, m * E:(m + 1) * E], xT[k][:, p // 2, m * P:(m + 1) * P], w_gate[p][:],
                                                    start=(p == 0), stop=(p == 2))
                    last.then_inc(gates_ready, 1)
                if n == AT_E["turn_weights"]:
                    wait_all(pe, pe_passed, (parts_ready, r + 1))
                    for m in range(T):
                        last = nc.tensor.matmul(front_ps[0:PARTS, m * P:(m + 1) * P], parts[:, m].rearrange("p a e -> p (a e)"),
                                                ident16[:], start=True, stop=True)
                    last.then_inc(combT_ps_ready, 1)

            def back(r, k, n, first):
                if n == AT_E["turn_y"]:
                    if first:
                        wait_all(pe, pe_passed, (yT_ready, r + 1))
                    else:
                        wait_all(pe, pe_passed, (back_taken, r), (yT_ready, r + 1))
                    for m in range(T):
                        last = nc.tensor.transpose(back_ps[:, m * D:(m + 1) * D], yT[:, m * P:(m + 1) * P], net.ident[0:D, 0:D])
                    last.then_inc(back_ready, 1)

            def down(r, k, j, first):
                y = y_ps[k][0:D, :]
                if j == 0:
                    if not first:
                        wait_all(pe, pe_passed, (yT_ready, r - 1))
                    nc.tensor.matmul(y, b2[:], combT[k][:], start=True, stop=False)
                last = nc.tensor.matmul(y, w2[:, j, :], hid[j % RING][:], start=False, stop=(j == J - 1))
                if j == J - 1:
                    last.then_inc(y_ready, 1)

            def one_row(r, k, number=None):
                pe.wait_ge(combT_ready, r * 2 + 2)
                for j in range(J):
                    pe.wait_ge(hid_ready, r * J + (j + 1))
                    if j % PER == 0:
                        nc.tensor.matmul(c_ps[(j // PER) % 2][:], pick[:, j // PER, :], combT16[k][:], start=True, stop=True)
                    for p in range(3):
                        last = nc.tensor.matmul(h_ps[j % 2][:], w1[p][:, j, :], xT[k][:, p // 2, :], start=(p == 0), stop=(p == 2))
                    last.then_inc(h_ready, 1)
                    if j >= LAG:
                        down(r, k, j - LAG, number in (0, 1))
                    elif number != 0:
                        down(r - 1, 1 - k, j - LAG + J, False)
                    if number != 0:
                        back(r - 1, 1 - k, j, number == 1)
                    if number != B - 1:
                        front(r + 1, 1 - k, j)

            for j in range(J):
                front(0, 0, j)
            one_row(0, 0, 0)
            one_row(1, 1, 1)
            with pe.Fori(1, B // 2 - 1) as i:
                for k in range(2):
                    one_row(i * 2 + k, k)
            one_row(B - 2, 0, B - 2)
            one_row(B - 1, 1, B - 1)
            for j in range(LAG):
                pe.wait_ge(hid_ready, B * J + (j + 1))
                down(B - 1, 1, j - LAG + J, False)
            for j in range(J):
                back(B - 1, 1, j, False)


def attention_stage(net):
    nc, t, B, S, D, T = net.nc, net.t, net.B, net.S, net.D, net.T
    SCALE = float(D) ** -0.5
    RING = 4
    with ExitStack() as ctx:
        def sb(n, shape, dt=F32):
            return ctx.enter_context(nc.sbuf_tensor(f"a_{n}", shape, dt))

        def sem(n):
            return net.semaphore(ctx, f"a_{n}")

        def bank(n):
            return ctx.enter_context(nc.psum_tensor(f"a_{n}", [P, S], F32))

        wq = sb("wq", [D + 1, D])
        wk = sb("wk", [D + 1, D])
        wv = sb("wv", [D, D + 1])
        wo = sb("wo", [D, D])
        wvo = sb("wvo", [D + 1, D + 2])
        bo = sb("bo", [P, D])
        half = sb("half", [P, T])
        total, rstd = sb("total", [P, T]), sb("rstd", [P, T])
        cen, sq, xn = sb("cen", [P, T, D]), sb("sq", [P, T, D]), sb("xn", [P, T, D])
        xT = sb("xT", [D + 1, S])
        qT = [sb(f"qT{k}", [D, S]) for k in range(2)]
        kT = [sb(f"kT{k}", [D, S]) for k in range(2)]
        v = [sb(f"v{k}", [P, T, D + 1]) for k in range(2)]
        mask = [sb(f"mask{k}", [P, T, 2]) for k in range(2)]
        mx, bias = sb("mx", [P, T]), sb("bias", [P, T])
        p = [sb(f"p{k}", [P, S]) for k in range(RING)]
        pT = [sb(f"pT{k}", [P, T, P]) for k in range(2)]
        factor = sb("factor", [P, T])
        o = sb("o", [P, T, D])
        s_ps = [bank(f"s_ps{k}") for k in range(2)]
        pT_ps = [bank(f"pT_ps{k}") for k in range(2)]
        o_ps = [bank(f"o_ps{k}") for k in range(2)]
        xk_ps, qv_ps = bank("xk_ps"), bank("qv_ps")

        loaded, set_up, wvo_ps_ready, wvo_ready = sem("loaded"), sem("set_up"), sem("wvo_ps_ready"), sem("wvo_ready")
        ln_step, pool_step, end_step = sem("ln_step"), sem("pool_step"), sem("end_step")
        var_ready, rstd_ready, xn_ready = sem("var_ready"), sem("rstd_ready"), sem("xn_ready")
        xT_ps_ready, xT_ready = sem("xT_ps_ready"), sem("xT_ready")
        q_ps_ready, q_ready, k_ps_ready, k_ready = sem("q_ps_ready"), sem("q_ready"), sem("k_ps_ready"), sem("k_ready")
        v_ps_ready, v_ready, mask_ready = sem("v_ps_ready"), sem("v_ready"), sem("mask_ready")
        s_ready, mx_ready, bias_ready, p_ready = sem("s_ready"), sem("mx_ready"), sem("bias_ready"), sem("p_ready")
        pT_ps_ready, pT_ready, o_ready, o_taken = sem("pT_ps_ready"), sem("pT_ready"), sem("o_ready"), sem("o_taken")
        pool_passed, pe_passed = sem("pool_passed"), sem("pe_passed")
        block = ctx.enter_context(nc.Block())
        LOADS = 6
        SET_UP = 4
        LN_STEPS = 3
        END_STEPS = 5
        full = [P, T, D]

        def row_of_H(r):
            return net.H[:, bass.ds(r, 1)].rearrange("p a t d -> p (a t) d")

        def v_of(ps):
            return ps[:, 0:T * (D + 2)].rearrange("p (t d) -> p t d", t=T)

        @block.sync
        def _(sp):
            sp.dma_start(wq[:], t["a_wq"]).then_inc(loaded, 16)
            sp.dma_start(wk[:], t["a_wk"]).then_inc(loaded, 16)
            sp.dma_start(wv[:], t["a_wv"]).then_inc(loaded, 16)
            sp.dma_start(wo[:], t["a_wo"]).then_inc(loaded, 16)
            sp.dma_start(bo[:], t["a_bo"].partition_broadcast(P)).then_inc(loaded, 16)
            sp.dma_start(wvo[:, D:D + 2], t["a_first"]).then_inc(loaded, 16)

        @block.gpsimd
        def _(pool):
            nc.gpsimd.memset(half[:], -0.5).then_inc(set_up, 1)
            nc.gpsimd.memset(xT[:], 1.0).then_inc(set_up, 1)
            for k in range(2):
                nc.gpsimd.memset(v[k][:], 1.0).then_inc(set_up, 1)
            pool.wait_ge(set_up, SET_UP)
            with pool.Fori(0, B) as r:
                wait_all(pool, pool_passed, (var_ready, r + 1))
                st = Steps(pool, pool_step, r)
                st.then(nc.gpsimd.tensor_scalar(rstd[:], total[:], 1.0 / D, EPS, ALU.mult, ALU.add))
                nc.gpsimd.tensor_tensor(rstd[:], rstd[:], half[:], ALU.pow).then_inc(rstd_ready, 1)

        @block.scalar
        def _(act):
            act.wait_ge(set_up, SET_UP)
            act.wait_ge(loaded, 16 * LOADS)
            act.wait_ge(wvo_ps_ready, 1)
            nc.scalar.copy(wvo[:, 0:D], qv_ps[0:D + 1, 0:D]).then_inc(wvo_ready, 1)

            def front(r, k, m):
                if m == 1:
                    act.wait_ge(xT_ps_ready, r + 1)
                    nc.scalar.copy(xT[0:D, :], xk_ps[0:D, :]).then_inc(xT_ready, 1)
                if m == 2:
                    act.wait_ge(q_ps_ready, r + 1)
                    nc.scalar.copy(qT[k][:], qv_ps[0:D, :]).then_inc(q_ready, 1)
                if m == 3:
                    act.wait_ge(k_ps_ready, r + 1)
                    nc.scalar.copy(kT[k][:], xk_ps[0:D, :]).then_inc(k_ready, 1)
                    act.wait_ge(v_ps_ready, r + 1)
                    nc.scalar.copy(v[k][:, :, 0:D], v_of(qv_ps)[:, :, 0:D]).then_inc(v_ready, 1)

            def turned(r, m):
                act.wait_ge(pT_ps_ready, r * T + (m + 1))
                nc.scalar.copy(pT[m % 2][:], pT_ps[m % 2][:].rearrange("p (t q) -> p t q", t=T)).then_inc(pT_ready, 1)

            def one_row(r, k, number=None):
                for m in range(T):
                    if m >= 2:
                        turned(r, m - 2)
                    elif number != 0:
                        turned(r - 1, m - 2 + T)
                    act.wait_ge(bias_ready, r * T + (m + 1))
                    nc.scalar.activation(p[m][:], s_ps[m % 2][:], ACT.Exp, bias=bias[:, m:m + 1], scale=SCALE).then_inc(p_ready, 1)
                    if number != B - 1:
                        front(r + 1, 1 - k, m)

            for m in range(T):
                front(0, 0, m)
            one_row(0, 0, 0)
            one_row(1, 1, 1)
            with act.Fori(1, B // 2 - 1) as i:
                for k in range(2):
                    one_row(i * 2 + k, k)
            one_row(B - 2, 0, B - 2)
            one_row(B - 1, 1, B - 1)
            for m in (T - 2, T - 1):
                turned(B - 1, m)

        @block.vector
        def _(dve):
            dve.wait_ge(loaded, 16 * LOADS)
            dve.wait_ge(set_up, SET_UP)

            def centre(r):
                st = Steps(dve, ln_step, r * LN_STEPS)
                h = row_of_H(r)
                st.then(nc.vector.reduce_sum(total[:], h, axis=AX))
                st.then(nc.vector.scalar_tensor_tensor(cen[:], total[:].unsqueeze(2).to_broadcast(full), -1.0 / D, h, ALU.mult, ALU.add))

            def variance(r):
                st = Steps(dve, ln_step, r * LN_STEPS + (LN_STEPS - 1))
                st.then(nc.vector.tensor_tensor(sq[:], cen[:], cen[:], ALU.mult))
                nc.vector.reduce_sum(total[:], sq[:], axis=AX).then_inc(var_ready, 1)

            def normalise(r):
                dve.wait_ge(rstd_ready, r + 1)
                if not (isinstance(r, int) and r == 0):
                    dve.wait_ge(xT_ps_ready, r)
                nc.vector.tensor_tensor(xn[:], cen[:], rstd[:].unsqueeze(2).to_broadcast(full), ALU.mult).then_inc(xn_ready, 1)

            def finish(r, k):
                st = Steps(dve, end_step, r * END_STEPS)
                ops = v_of(o_ps[k])
                dve.wait_ge(o_ready, r + 1)
                st.then(nc.vector.reciprocal(factor[:], ops[:, :, D]))
                st.then(nc.vector.tensor_tensor(factor[:], factor[:], mask[k][:, :, 0], ALU.mult))
                st.then(nc.vector.tensor_tensor(factor[:], factor[:], mask[k][:, :, 1], ALU.mult))
                nc.vector.tensor_tensor(o[:], ops[:, :, 0:D], factor[:].unsqueeze(2).to_broadcast(full), ALU.mult).then_inc(o_taken, 1)
                st.then(nc.vector.tensor_tensor(row_of_H(r), row_of_H(r), bo[:].unsqueeze(1).to_broadcast(full), ALU.add))
                dve.wait_ge(o_taken, r + 1)
                st.then(nc.vector.tensor_tensor(row_of_H(r), row_of_H(r), o[:], ALU.add))

            def one_row(r, k, number=None):
                for m in range(T):
                    dve.wait_ge(s_ready, r * T + (m + 1))
                    nc.vector.reduce_max(mx[:, m:m + 1], s_ps[m % 2][:], axis=AX).then_inc(mx_ready, 1)
                    dve.wait_ge(mx_ready, r * T + (m + 1))
                    nc.vector.tensor_scalar(bias[:, m:m + 1], mx[:, m:m + 1], -SCALE, None, ALU.mult).then_inc(bias_ready, 1)
                    if m == 0:
                        dve.wait_ge(v_ready, r + 1)
                        nc.vector.tensor_scalar(mask[k][:], v_of(qv_ps)[:, :, D:D + 2], 0.0, None, ALU.not_equal).then_inc(mask_ready, 1)
                        if number != B - 1:
                            normalise(r + 1)
                    more = number not in (B - 2, B - 1)
                    if m == 1 and more:
                        centre(r + 2)
                    if m == 2 and more:
                        variance(r + 2)
                    if m == 3 and number != 0:
                        dve.wait_ge(mask_ready, r)
                        finish(r - 1, 1 - k)

            centre(0)
            variance(0)
            normalise(0)
            dve.wait_ge(xn_ready, 1)
            centre(1)
            variance(1)
            one_row(0, 0, 0)
            one_row(1, 1, 1)
            with dve.Fori(1, B // 2 - 1) as i:
                for k in range(2):
                    one_row(i * 2 + k, k)
            one_row(B - 2, 0, B - 2)
            one_row(B - 1, 1, B - 1)
            dve.wait_ge(mask_ready, B)
            finish(B - 1, 1)

        @block.tensor
        def _(pe):
            pe.wait_ge(loaded, 16 * LOADS)
            pe.wait_ge(set_up, SET_UP)
            nc.tensor.matmul(qv_ps[0:D + 1, 0:D], wv[:], wo[:], start=True, stop=True).then_inc(wvo_ps_ready, 1)
            pe.wait_ge(wvo_ready, 1)
            pe.sem_inc(p_ready, CREDIT)

            def front(r, k, m):
                first = isinstance(r, int) and r == 0
                if m == 1:
                    wait_all(pe, pe_passed, (xn_ready, r + 1))
                    for c in range(T):
                        last = nc.tensor.transpose(xk_ps[0:D, c * P:(c + 1) * P], xn[:, c, :], net.ident[:])
                    last.then_inc(xT_ps_ready, 1)
                if m == 2:
                    if first:
                        wait_all(pe, pe_passed, (xT_ready, r + 1))
                    else:
                        wait_all(pe, pe_passed, (xT_ready, r + 1), (mask_ready, r))
                    nc.tensor.matmul(qv_ps[0:D, :], wq[:], xT[:], start=True, stop=True).then_inc(q_ps_ready, 1)
                    nc.tensor.matmul(xk_ps[0:D, :], wk[:], xT[:], start=True, stop=True).then_inc(k_ps_ready, 1)
                if m == 3:
                    wait_all(pe, pe_passed, (q_ready, r + 1))
                    for c in range(T):
                        last = nc.tensor.matmul(v_of(qv_ps)[:, c, :], xT[:, c * P:(c + 1) * P], wvo[:], start=True, stop=True)
                    last.then_inc(v_ps_ready, 1)

            def turn(m):
                for c in range(T):
                    last = nc.tensor.transpose(pT_ps[m % 2][:, c * P:(c + 1) * P], p[m][:, c * P:(c + 1) * P], net.ident[:])
                last.then_inc(pT_ps_ready, 1)

            def values(r, k, m, first):
                wait_all(pe, pe_passed, (pT_ready, r * T + (m + 1)))
                if m == 0:
                    if first:
                        wait_all(pe, pe_passed, (v_ready, r + 1))
                    else:
                        wait_all(pe, pe_passed, (v_ready, r + 1), (o_taken, r - 1))
                for c in range(T):
                    last = nc.tensor.matmul(v_of(o_ps[k])[:, m, 0:D + 1], pT[m % 2][:, c, :], v[k][:, c, :],
                                            start=(c == 0), stop=(c == T - 1))
                if m == T - 1:
                    last.then_inc(o_ready, 1)

            def one_row(r, k, number=None):
                wait_all(pe, pe_passed, (q_ready, r + 1), (k_ready, r + 1))
                for m in range(T):
                    wait_all(pe, pe_passed, (p_ready, r * T + (m + 1)))
                    nc.tensor.matmul(s_ps[m % 2][:], qT[k][:, m * P:(m + 1) * P], kT[k][:], start=True, stop=True).then_inc(s_ready, 1)
                    if m >= 2 or number != 0:
                        turn((m - 2) % T)
                    if m >= 3:
                        values(r, k, m - 3, number in (0, 1))
                    elif number != 0:
                        values(r - 1, 1 - k, m - 3 + T, False)
                    if number != B - 1:
                        front(r + 1, 1 - k, m)

            for m in range(T):
                front(0, 0, m)
            one_row(0, 0, 0)
            one_row(1, 1, 1)
            with pe.Fori(1, B // 2 - 1) as i:
                for k in range(2):
                    one_row(i * 2 + k, k)
            one_row(B - 2, 0, B - 2)
            one_row(B - 1, 1, B - 1)
            for m in range(3):
                if m < 2:
                    pe.wait_ge(p_ready, B * T + (m + 1))
                    turn(m - 2 + T)
                values(B - 1, 1, m - 3 + T, False)


def tower(nc, t, out, stages=5):
    B, S, D = out.shape
    with ExitStack() as ctx:
        net = Net(nc, ctx, t, B, S, D)
        with nc.sbuf_tensor("X", [P, B, S // P, D], F32) as X:
            token_stage(net, X)
            net.clear_semaphores()
            if stages > 1:
                for layer in range(2):
                    mamba_stage(net, X, layer)
                    net.clear_semaphores()
            if stages > 1:
                mamba_end_stage(net, X)
                net.clear_semaphores()
        if stages > 2:
            experts_stage(net, "f0", None)
            net.clear_semaphores()
        if stages > 3:
            attention_stage(net)
            net.clear_semaphores()
        if stages > 4:
            experts_stage(net, "f1", out)
            net.clear_semaphores()
        else:
            with nc.semaphore("dbg") as dbg, nc.Block() as block:
                @block.sync
                def _(sp):
                    sp.dma_start(out.rearrange("b (t p) d -> p b t d", p=P), net.H[:]).then_inc(dbg, 16)
                    sp.wait_ge(dbg, 16)


def lay_out(i):
    import numpy as np

    def c(*a, axis=0):
        return np.concatenate([np.asarray(x) for x in a], axis)

    a = {k: np.asarray(v) for k, v in i.items()}
    t = {"ident": np.eye(P, dtype=np.float32)}
    for name, k in (("id_event", "x"), ("id_fault", "itok_BS_0_255"), ("id_syscall", "itok_BS_0_511"),
                    ("id_opcode", "itok_BS_0_127"), ("id_transition", "itok_BS_0_63"), ("id_result", "itok_BS_0_3")):
        t[name] = a[k]
    W = a["L0_tok_W"]
    D = W.shape[0]
    tables = [("et", 0, 0, 0), ("fc", 0, 16, 64), ("sc", 1, 0, 0), ("of", 2, 0, 0), ("tt", 3, 0, 0), ("rc", 3, 16, 64)]
    E = np.zeros((33, 4, P), np.float32)
    Wt = np.zeros((32, 4, D), np.float32)
    ids = np.full((P, 4), -1, np.float32)
    for n, (name, tile, row, col) in enumerate(tables):
        e = a[f"L0_tok_E_{name}"]
        E[row:row + 16, tile, col:col + len(e)] = e.T
        Wt[row:row + 16, tile] = W[:, 16 * n:16 * n + 16].T
        ids[col:col + len(e), tile] = np.arange(len(e))
    E[32, 0, 0:64] = 1
    b = np.zeros((1, 4, D), np.float32)
    b[0, 0] = a["L0_tok_b"]
    t |= {"tok_E": E, "tok_W": Wt, "tok_b": b, "vocab": ids, "tok_gamma": a["L0_tok_gamma"], "tok_beta": a["L0_tok_beta"],
          "pre_g": a["L0_attn_pre_g"], "pre_b": a["L0_attn_pre_b"], "normf_w": a["L0_attn_normf_w"],
          "post_g": a["L0_attn_post_g"], "post_b": a["L0_attn_post_b"]}
    inw = a["L0_attn_inproj_w"].transpose(0, 2, 1)
    NL, _, E2 = inw.shape
    NC = E2 // 2 // P

    def channels(x):
        return np.ascontiguousarray(x.reshape(NL, NC, P, *x.shape[2:]).swapaxes(1, 2))

    xp = a["L0_attn_xproj_w"]
    R, NS = a["L0_attn_dtproj_w"].shape[2], a["L0_attn_A_log"].shape[2]
    bc = xp[:, R:]
    rows = c(bc, bc, bc, xp[:, :R], axis=1).transpose(0, 2, 1)
    t |= {"m_in_w": c(inw, inw, axis=1), "m_norm_w": c(a["L0_attn_norm_w"], a["L0_attn_norm_w"], axis=1)[:, :, None],
          "m_conv_w": a["L0_attn_conv_w"][:, :, 0, :].transpose(0, 2, 1), "m_conv_b": channels(a["L0_attn_conv_b"]),
          "m_xproj_w": channels(rows), "m_dtproj_w": a["L0_attn_dtproj_w"].transpose(0, 2, 1),
          "m_dtproj_b": channels(a["L0_attn_dtproj_b"]), "m_A_log": channels(a["L0_attn_A_log"]),
          "m_D": channels(a["L0_attn_D_param"]), "m_out_w": channels(a["L0_attn_outproj_w"].transpose(0, 2, 1))}

    def experts(name, w1, b1, w2, b2, gate, gate_b):
        E, H, D = w1.shape
        J = E * H // P
        t[f"{name}_w1"] = np.tile(w1.reshape(J * P, D).T, (2, 1)).reshape(2 * D, J, P)
        t[f"{name}_b1"] = b1.reshape(J, P).T
        t[f"{name}_w2"] = w2.reshape(J, P, D).transpose(1, 0, 2)
        t[f"{name}_b2"] = np.tile(b2, (3, 1))
        t[f"{name}_gate"] = np.tile(gate, (2, 1))
        t[f"{name}_gate_b"] = gate_b
        t[f"{name}_order"] = np.tile(np.arange(E, 0, -1, dtype=np.float32), (P, 1))

    experts("f0", a["L0_ffn_W1"], a["L0_ffn_b1"], a["L0_ffn_W2"].transpose(0, 2, 1), a["L0_ffn_b2"],
            a["L0_ffn_Wg"].T, a["L0_ffn_bg"])
    experts("f1", a["L1_ffn_w1"].transpose(0, 2, 1), a["L1_ffn_b1"], a["L1_ffn_w2"], a["L1_ffn_b2"],
            a["L1_ffn_gate_w"], a["L1_ffn_gate_b"])
    t |= {"f1_gamma": a["L1_ffn_gamma"], "f1_beta": a["L1_ffn_beta"]}
    wq, wk, bq, bk = a["L1_attn_Wq"], a["L1_attn_Wk"], a["L1_attn_bq"], a["L1_attn_bk"]
    t |= {"a_wq": c(wq.T, bq[None]), "a_wk": c(wk.T, bk[None]), "a_wv": c(a["L1_attn_Wv"], a["L1_attn_bv"][:, None], axis=1),
          "a_wo": a["L1_attn_Wo"].T, "a_bo": a["L1_attn_bo"],
          "a_first": c(c(wq[0:1].T, bq[None, 0:1]), c(wk[0:1].T, bk[None, 0:1]), axis=1)}
    return {k: np.ascontiguousarray(v) for k, v in t.items()}


def kernel(**inputs):
    import numpy as _np
    import concourse.bacc as _bacc
    from concourse.bass_utils import run_bass_kernel_spmd as _run

    nc = _bacc.Bacc("TRN2", target_bir_lowering=False, num_devices=1)
    arrays = lay_out(inputs)
    t = {k: nc.dram_tensor(f"in_{k}", v.shape, mybir.dt.from_np(v.dtype), kind="ExternalInput").ap() for k, v in arrays.items()}
    B, S = inputs["x"].shape
    D = inputs["L0_tok_W"].shape[0]
    out = nc.dram_tensor("out", (B, S, D), F32, kind="ExternalOutput").ap()
    tower(nc, t, out)
    return _run(nc, [{f"in_{k}": v for k, v in arrays.items()}], core_ids=[0]).results[0]["out"]
```

```python
from contextlib import ExitStack

import concourse.bass as bass
from concourse import mybir

ALU = mybir.AluOpType
ACT = mybir.ActivationFunctionType
F32 = mybir.dt.float32
BF16 = mybir.dt.bfloat16
I32 = mybir.dt.int32
AX = mybir.AxisListType.X

P = 128
CREDIT = 2
DEEP = 4
EPS = 1e-5
DROPPED = -1e30


def wait_all(eng, passed, *waits):
    for sem, value in waits:
        eng.wait_ge(sem, value)
    eng.sem_inc(passed, 1)


class Steps:

    def __init__(self, eng, sem, base, passed=None):
        self.eng, self.sem, self.base, self.n, self.passed = eng, sem, base, 0, passed

    def then(self, ins):
        ins.then_inc(self.sem, 1)
        self.n += 1
        if self.passed is not None:
            wait_all(self.eng, self.passed, (self.sem, self.base + self.n))
        else:
            self.eng.wait_ge(self.sem, self.base + self.n)


def spread(ap, shape):
    return ap.to_broadcast(shape)


class Net:

    def __init__(self, nc, ctx, t, B, S, D):
        self.nc, self.t, self.B, self.S, self.D = nc, t, B, S, D
        self.T = S // P
        self.H = ctx.enter_context(nc.sbuf_tensor("H", [P, B, self.T, D], F32))
        self.ident = ctx.enter_context(nc.sbuf_tensor("ident", [P, P], F32))
        self.used = []

    def semaphore(self, ctx, name):
        sem = ctx.enter_context(self.nc.semaphore(name))
        self.used.append(sem)
        return sem

    def clear_semaphores(self):
        numbers = [s.num for s in self.used]
        self.used = []
        with self.nc.Block() as block:
            @block.gpsimd
            def _(pool):
                pool.sem_clear(range(min(numbers), max(numbers) + 1))


def centre_and_variance(nc, st, x, total, centred, square, shape):
    D = shape[-1]
    st.then(nc.vector.reduce_sum(total, x, axis=AX))
    st.then(nc.vector.scalar_tensor_tensor(centred, total.unsqueeze(2).to_broadcast(shape), -1.0 / D, x,
                                           ALU.mult, ALU.add))
    st.then(nc.vector.tensor_tensor(square, centred, centred, ALU.mult))
    return nc.vector.reduce_sum(total, square, axis=AX)


def token_stage(net, X):
    nc, t, B, S, D, T = net.nc, net.t, net.B, net.S, net.D, net.T
    PAIRS = B // 2
    N = 2 * S
    NT = 2 * T
    NK = 4
    KW = t["tok_W"].shape[0]
    SHAPE = [P, NT, D]
    LN_STEPS = 3
    with ExitStack() as ctx:
        def sb(name, shape, dt=F32):
            return ctx.enter_context(nc.sbuf_tensor(name, shape, dt))

        def sem(name):
            return net.semaphore(ctx, name)

        emb = sb("t_emb", [KW + 1, NK, P])
        w = sb("w", [KW + 1, NK, D])
        absw = sb("absw", [KW, NK, D])
        wsum = sb("wsum", [KW, 1])
        ones = sb("ones", [KW, KW])
        thr = sb("thr", [KW, 3])
        pos = sb("pos", [KW, NK, D])
        neg = sb("neg", [KW, NK, D])
        weff = sb("weff", [KW + 1, NK, D])
        table = sb("table", [P, NK, 3, D], BF16)
        rest = sb("rest", [P, NK, D])
        vocab = sb("vocab", [P, NK])
        affine = sb("affine", [P, 4, D])
        half = sb("half", [P, NT])
        ids = [sb(f"ids{k}", [P, NK, N], I32) for k in range(2)]
        hot = [sb(f"hot{k}", [P, NK, N], BF16) for k in range(2)]
        total = sb("total", [P, NT])
        rstd = sb("rstd", [P, NT])
        cen = sb("cen", SHAPE)
        sq = sb("sq", SHAPE)
        z = [ctx.enter_context(nc.psum_tensor(f"z{k}", SHAPE, F32)) for k in range(2)]
        tab_ps = ctx.enter_context(nc.psum_tensor("tab_ps", [P, NK, D], F32))
        sum_ps = ctx.enter_context(nc.psum_tensor("sum_ps", [KW, 1], F32))

        loaded = sem("loaded")
        set_up = sem("set_up")
        wsum_ready = sem("wsum_ready")
        scale_ready = sem("scale_ready")
        weff_ready = sem("weff_ready")
        tables_ready = sem("tables_ready")
        table_split = sem("table_split")
        ids_loaded = [sem(f"ids_loaded{k}") for k in range(2)]
        hot_ready = sem("hot_ready")
        z_ready = sem("z_ready")
        dve_step = sem("dve_step")
        var_ready = sem("var_ready")
        pool_step = sem("pool_step")
        pool_passed, dve_passed = sem("pool_passed"), sem("dve_passed")
        rstd_ready = sem("rstd_ready")
        x_scaled, x_done = sem("x_scaled"), sem("x_done")
        block = ctx.enter_context(nc.Block())

        IDS = [("id_event", 0, 0, 64), ("id_fault", 0, 64, 64), ("id_syscall", 1, 0, P), ("id_opcode", 2, 0, P),
               ("id_transition", 3, 0, 64), ("id_result", 3, 64, 64)]

        @block.sync
        def _(sp):
            sp.dma_start(net.ident[:], t["ident"]).then_inc(loaded, 16)
            sp.dma_start(emb[:], t["tok_E"]).then_inc(loaded, 16)
            sp.dma_start(w[0:KW], t["tok_W"]).then_inc(loaded, 16)
            sp.dma_start(weff[KW:KW + 1], t["tok_b"]).then_inc(loaded, 16)
            sp.dma_start(vocab[:], t["vocab"]).then_inc(loaded, 16)
            for k, name in enumerate(("tok_gamma", "tok_beta", "pre_g", "pre_b")):
                sp.dma_start(affine[:, k, :], t[name].partition_broadcast(P)).then_inc(loaded, 16)

            def load_ids(p, k):
                for name, tile, first, rows in IDS:
                    src = t[name].rearrange("(q two) s -> q (two s)", two=2)[p].partition_broadcast(rows)
                    sp.dma_start(ids[k][first:first + rows, tile, :], src).then_inc(ids_loaded[k], 16)

            load_ids(0, 0)
            load_ids(1, 1) if PAIRS > 1 else None
            if PAIRS > 2:
                with sp.Fori(0, PAIRS // 2 - 1) as i:
                    for k in range(2):
                        sp.wait_ge(hot_ready, i * 2 + (k + 1))
                        load_ids(i * 2 + (k + 2), k)

        @block.gpsimd
        def _(pool):
            nc.gpsimd.memset(ones[:], 1.0).then_inc(set_up, 1)
            nc.gpsimd.memset(half[:], -0.5).then_inc(set_up, 1)
            pool.wait_ge(set_up, 2)
            pool.wait_ge(loaded, 16 * 9)

            def one_pair(p):
                for n in range(3):
                    st = Steps(pool, pool_step, p * 3 + n)
                    wait_all(pool, pool_passed, (var_ready, p * 3 + (n + 1)))
                    st.then(nc.gpsimd.tensor_scalar(rstd[:], total[:], 1.0 / D, EPS, ALU.mult, ALU.add))
                    nc.gpsimd.tensor_tensor(rstd[:], rstd[:], half[:], ALU.pow).then_inc(rstd_ready, 1)
                wait_all(pool, pool_passed, (x_scaled, p + 1))
                x = X[:, bass.ds(p * 2, 2)].rearrange("p b t d -> p (b t) d")
                nc.gpsimd.tensor_tensor(x, x, affine[:, 2, :].unsqueeze(1).to_broadcast(SHAPE), ALU.mult).then_inc(x_done, 1)
                wait_all(pool, pool_passed, (x_done, p * 2 + 1))
                nc.gpsimd.tensor_tensor(x, x, affine[:, 3, :].unsqueeze(1).to_broadcast(SHAPE), ALU.add).then_inc(x_done, 1)

            with pool.Fori(0, PAIRS) as p:
                one_pair(p)

        @block.vector
        def _(dve):
            dve.wait_ge(loaded, 16 * 9)
            st = Steps(dve, weff_ready, 0)
            st.then(nc.vector.scalar_tensor_tensor(absw[:], w[0:KW], -1.0, w[0:KW], ALU.mult, ALU.max))
            nc.vector.reduce_sum(wsum[:], absw[:].rearrange("p k d -> p (k d)"), axis=AX).then_inc(wsum_ready, 1)
            dve.wait_ge(scale_ready, 1)
            nw = 1.0 / (96 * D)
            st.then(nc.vector.tensor_scalar(thr[:, 0:1], sum_ps[:], nw, None, ALU.mult))
            st.then(nc.vector.tensor_scalar(thr[:, 1:2], thr[:, 0:1], 1e-8, 0.5, ALU.add, ALU.mult))
            st.then(nc.vector.tensor_scalar(thr[:, 2:3], thr[:, 1:2], -1.0, None, ALU.mult))
            st.then(nc.vector.tensor_scalar(pos[:], w[0:KW], thr[:, 1:2], thr[:, 0:1], ALU.is_gt, ALU.mult))
            st.then(nc.vector.tensor_scalar(neg[:], w[0:KW], thr[:, 2:3], thr[:, 0:1], ALU.is_lt, ALU.mult))
            st.then(nc.vector.tensor_tensor(pos[:], pos[:], neg[:], ALU.subtract))
            st.then(nc.vector.tensor_tensor(pos[:], pos[:], w[0:KW], ALU.subtract))
            st.then(nc.vector.tensor_tensor(weff[0:KW], w[0:KW], pos[:], ALU.add))
            dve.wait_ge(tables_ready, 1)
            st = Steps(dve, table_split, 0)
            st.then(nc.vector.tensor_copy(table[:, :, 0, :], tab_ps[:]))
            st.then(nc.vector.tensor_tensor(rest[:], tab_ps[:], table[:, :, 0, :], ALU.subtract))
            st.then(nc.vector.tensor_copy(table[:, :, 1, :], rest[:]))
            st.then(nc.vector.tensor_tensor(table[:, :, 2, :], rest[:], table[:, :, 1, :], ALU.subtract))

            def one_hot(p, k, turn, tiles=range(NK)):
                dve.wait_ge(ids_loaded[k], turn * (16 * len(IDS)) + 16 * len(IDS))
                if not (isinstance(p, int) and p < 2):
                    dve.wait_ge(z_ready, p - 1)
                for tile in tiles:
                    last = nc.vector.tensor_scalar(hot[k][:, tile, :], ids[k][:, tile, :], vocab[:, tile:tile + 1],
                                                   None, ALU.is_equal)
                if tiles[-1] == NK - 1:
                    last.then_inc(hot_ready, 1)

            def normalise(p, k, following=None):
                xr = X[:, bass.ds(p * 2, 2)].rearrange("p b t d -> p (b t) d")
                hr = net.H[:, bass.ds(p * 2, 2)].rearrange("p b t d -> p (b t) d")
                st = Steps(dve, dve_step, p * STEPS, passed=dve_passed)
                dve.wait_ge(z_ready, p + 1)
                for n, (src, dst) in enumerate(((z[k][:], hr), (hr, xr), (xr, xr))):
                    centre_and_variance(nc, st, src, total[:], cen[:], sq[:], SHAPE).then_inc(var_ready, 1)
                    if following is not None and n < 2:
                        one_hot(*following, range(n * NK // 2, (n + 1) * NK // 2))
                    dve.wait_ge(rstd_ready, p * 3 + (n + 1))
                    st.then(nc.vector.tensor_tensor(dst, cen[:], rstd[:].unsqueeze(2).to_broadcast(SHAPE), ALU.mult))
                    if n == 2:
                        dve.sem_inc(x_scaled, 1)
                    if n == 0:
                        g, b = affine[:, n, :], affine[:, n + 1, :]
                        st.then(nc.vector.tensor_tensor(dst, dst, g.unsqueeze(1).to_broadcast(SHAPE), ALU.mult))
                        st.then(nc.vector.tensor_tensor(dst, dst, b.unsqueeze(1).to_broadcast(SHAPE), ALU.add))
                assert st.n == STEPS

            STEPS = 3 * 4 + 2
            one_hot(0, 0, 0)
            if PAIRS > 1:
                one_hot(1, 1, 0)
            normalise(0, 0)
            if PAIRS > 2:
                with dve.Fori(0, PAIRS // 2 - 1) as i:
                    normalise(i * 2 + 1, 1, (i * 2 + 2, 0, i + 1))
                    normalise(i * 2 + 2, 0, (i * 2 + 3, 1, i + 1))
            if PAIRS > 1:
                normalise(PAIRS - 1, 1)

        @block.tensor
        def _(pe):
            pe.wait_ge(set_up, 2)
            pe.wait_ge(wsum_ready, 1)
            nc.tensor.matmul(sum_ps[:], ones[:], wsum[:], start=True, stop=True).then_inc(scale_ready, 1)
            pe.wait_ge(weff_ready, 9)
            for tile in range(NK):
                last = nc.tensor.matmul(tab_ps[:, tile, :], emb[:, tile, :], weff[:, tile, :], start=True, stop=True)
            last.then_inc(tables_ready, 1)
            pe.wait_ge(table_split, 4)

            def project(p, k):
                pe.wait_ge(hot_ready, p + 1)
                if not (isinstance(p, int) and p < 2):
                    pe.wait_ge(rstd_ready, p * 3 - 5)
                for m in range(NT):
                    for tile in range(NK):
                        for part in range(3):
                            last = nc.tensor.matmul(z[k][:, m, :], hot[k][:, tile, m * P:(m + 1) * P],
                                                    table[:, tile, part, :], start=(tile == 0 and part == 0),
                                                    stop=(tile == NK - 1 and part == 2))
                last.then_inc(z_ready, 1)

            project(0, 0)
            if PAIRS > 1:
                project(1, 1)
            if PAIRS > 2:
                with pe.Fori(0, PAIRS // 2 - 1) as i:
                    for k in range(2):
                        project(i * 2 + (k + 2), k)


MAMBA_STATE = {
    "gate_output": 4, "inverse_rms": 2, "step_sizes": 15, "weighted_u": 15,
    "copy_xT": 4, "activate": 7, "high_part": 8, "middle_part": 9, "softplus_exp": 9, "softplus_log": 12,
    "skip_path": 1, "residual": 6, "squares": 0, "normalise": 1, "remainder": 7, "low_part": 9,
    "rounding_loss": 11, "exact_log": 12,
    "transpose": 1, "project_u0": 3, "project_u1": 5, "project_gate0": 5, "project_gate1": 5,
    "project_ssm": 6, "project_dt": 7, "output": 2,
}


def mamba_stage(net, X, layer):
    nc, t, B, S, D, T = net.nc, net.t, net.B, net.S, net.D, net.T
    NC, NS = t["m_A_log"].shape[2:4]
    R = t["m_dtproj_w"].shape[1]
    BC = 2 * NS
    DT0 = 3 * BC
    L = layer
    with ExitStack() as ctx:
        def sb(name, shape, dt=F32):
            return ctx.enter_context(nc.sbuf_tensor(f"m{L}_{name}", shape, dt))

        def sem(name):
            return net.semaphore(ctx, f"m{L}_{name}")

        def bank(name):
            return ctx.enter_context(nc.psum_tensor(f"m{L}_{name}", [P, S], F32))

        w_in = sb("w_in", [P, 2 * NC * P])
        w_conv = sb("w_conv", [P, 2, NC * P])
        w_norm = sb("w_norm", [P, 1])
        w_u = sb("w_u", [P, 2, NC * P])
        w_g = sb("w_g", [D, NC * P])
        conv_b = sb("conv_b", [P, NC])
        w_x = sb("w_x", [P, NC, DT0 + R])
        w_dt = sb("w_dt", [P, NC * P])
        dt_b = sb("dt_b", [P, NC])
        decay = sb("decay", [P, NC, NS])
        skip = sb("skip", [P, NC])
        w_out = sb("w_out", [P, NC, D])
        pick = sb("pick", [DT0, BC, P], BF16)
        pick_row = sb("pick_row", [DT0, BC])
        half = sb("half", [P, T])
        sq = sb("sq", [P, T, D])
        ssq = sb("ssq", [P, T])
        rstd = sb("rstd", [P, T])
        xn = sb("xn", [P, T, 2, D])
        xT = sb("xT", [P, S + 3])
        u = [sb(f"u{k}", [P, NC, S]) for k in range(2)]
        gate = [sb(f"gate{k}", [P, NC, S]) for k in range(2)]
        dt = [sb(f"dt{k}", [P, NC, S]) for k in range(2)]
        dtu = [sb(f"dtu{k}", [P, NC, S]) for k in range(2)]
        parts = [sb(f"parts{k}", [DT0, S], BF16) for k in range(2)]
        dt_low = sb("dt_low", [P, S])
        rest = sb("rest", [DT0, S])
        mid = sb("mid", [DT0, S], BF16)
        pos = sb("pos", [P, NC, S])
        ex = sb("ex", [P, NC, S])
        one_ex = sb("one_ex", [P, NC, S])
        log = sb("log", [P, NC, S])
        lost = sb("lost", [P, NC, S])
        Bs = [sb(f"Bs{k}", [P, S]) for k in range(DEEP)]
        dA = [sb(f"dA{k}", [P, NC, S]) for k in range(2)]
        dBu = [sb(f"dBu{k}", [P, NC, S]) for k in range(DEEP)]
        hs = [sb(f"hs{k}", [P, NC, S]) for k in range(2)]
        hC = [sb(f"hC{k}", [P, NC, S]) for k in range(2)]
        yv = sb("yv", [P, NC, S])
        yg = sb("yg", [P, NC, S])
        W0, W1, W2 = bank("W0"), bank("W1"), bank("W2")
        Bb = bank("Bb")
        Cb = [bank(f"Cb{k}") for k in range(2)]
        Y = [bank(f"Y{c}") for c in range(NC)]

        loaded, pads, w_step, weights_ready = sem("loaded"), sem("pads"), sem("w_step"), sem("weights_ready")
        decay_ready = sem("decay_ready")
        sq_ready, ssq_ready, var_eps, rstd_ready = sem("sq_ready"), sem("ssq_ready"), sem("var_eps"), sem("rstd_ready")
        xn_ready, xT_ps_ready, xT_ready = sem("xn_ready"), sem("xT_ps_ready"), sem("xT_ready")
        proj_ready, silu_done, ssm_ready = sem("proj_ready"), sem("silu_done"), sem("ssm_ready")
        hi_ready, rest_ready, mid_ready = sem("hi_ready"), sem("rest_ready"), sem("mid_ready")
        mid_tmp, lo_ready = sem("mid_tmp"), sem("lo_ready")
        dt_ps_ready, dt_ps_read = sem("dt_ps_ready"), sem("dt_ps_read")
        abs_ready, ex_ready, one_ex_ready = sem("abs_ready"), sem("ex_ready"), sem("one_ex_ready")
        log_ready, lost_ready = sem("log_ready"), sem("lost_ready")
        exact_log_ready, dt_ready, dtu_ready = sem("exact_log_ready"), sem("dt_ready"), sem("dtu_ready")
        bb_ready, bb_copied, dbu_ready, da_ready = sem("bb_ready"), sem("bb_copied"), sem("dbu_ready"), sem("da_ready")
        cb_ready, scan_done, hc_ready, summed = sem("cb_ready"), sem("scan_done"), sem("hc_ready"), sem("summed")
        y_read, yg_ready, out_ready, x_done = sem("y_read"), sem("yg_ready"), sem("out_ready"), sem("x_done")
        pool_passed = sem("pool_passed")
        block = ctx.enter_context(nc.Block())

        def rows(eng, first, body):
            first()
            body(0, 0, False, True)
            if B > 2:
                with eng.Fori(0, B // 2 - 1) as i:
                    for k in range(2):
                        body(i * 2 + (k + 1), 1 - k, True, True)
            body(B - 1, 1, True, False)

        LOADS = 12
        B_LEAD = 2
        AHEAD = 5

        @block.sync
        def _(sp):
            sp.dma_start(w_in[:], t["m_in_w"][L]).then_inc(loaded, 16)
            for pair in range(2):
                for copy in range(2):
                    sp.dma_start(w_conv[copy * D:(copy + 1) * D, pair, :],
                                 t["m_conv_w"][L, 3 - 2 * pair - copy].partition_broadcast(D)).then_inc(loaded, 16)
            sp.dma_start(w_norm[:], t["m_norm_w"][L]).then_inc(loaded, 16)
            sp.dma_start(conv_b[:], t["m_conv_b"][L]).then_inc(loaded, 16)
            sp.dma_start(w_x[:], t["m_xproj_w"][L]).then_inc(loaded, 16)
            sp.dma_start(w_dt[DT0:DT0 + R, :], t["m_dtproj_w"][L]).then_inc(loaded, 16)
            sp.dma_start(dt_b[:], t["m_dtproj_b"][L]).then_inc(loaded, 16)
            sp.dma_start(skip[:], t["m_D"][L]).then_inc(loaded, 16)
            sp.dma_start(w_out[:], t["m_out_w"][L]).then_inc(loaded, 16)
            sp.dma_start(decay[:], t["m_A_log"][L]).then_inc(decay_ready, 16)

        @block.gpsimd
        def _(pool):
            nc.gpsimd.memset(half[:], -0.5).then_inc(pads, 1)
            nc.gpsimd.memset(xT[:], 0.0).then_inc(pads, 1)
            pool.wait_ge(pads, 2)
            pool.sem_inc(dbu_ready, DEEP)

            def inverse_rms(r):
                wait_all(pool, pool_passed, (ssq_ready, r + 1))
                nc.gpsimd.tensor_scalar(rstd[:], ssq[:], 1.0 / D, EPS, ALU.mult, ALU.add).then_inc(var_eps, 1)
                pool.wait_ge(var_eps, r + 1)
                nc.gpsimd.tensor_tensor(rstd[:], rstd[:], half[:], ALU.pow).then_inc(rstd_ready, 1)

            def step_sizes(r, k):
                pool.wait_ge(exact_log_ready, r + 1)
                if not (isinstance(r, int) and r == 0):
                    pool.wait_ge(da_ready, r * NS - NS)
                nc.gpsimd.tensor_tensor(dt[k][:], pos[:], log[:], ALU.add).then_inc(dt_ready, 1)

            def weighted_u(r, k):
                pool.wait_ge(dt_ready, r + 1)
                pool.wait_ge(silu_done, r * 4 + 4)
                nc.gpsimd.tensor_tensor(dtu[k][:], dt[k][:], u[k][:], ALU.mult).then_inc(dtu_ready, 1)
                pool.wait_ge(dtu_ready, r + 1)

            def state_input(r, k, n):
                q = r * NS + n
                pool.wait_ge(bb_copied, q + 2)
                pool.wait_ge(scan_done, q + 1)
                nc.gpsimd.tensor_tensor(dBu[n % DEEP][:], dtu[k][:], Bs[n % DEEP][:].unsqueeze(1).to_broadcast([P, NC, S]),
                                        ALU.mult).then_inc(dbu_ready, 1)

            def gated(r, k):
                pool.wait_ge(y_read, r + 1)
                pool.wait_ge(out_ready, r)
                nc.gpsimd.tensor_tensor(yg[:], yv[:], gate[k][:], ALU.mult).then_inc(yg_ready, 1)

            def first():
                inverse_rms(0)
                step_sizes(0, 0)
                weighted_u(0, 0)

            def body(r, k, back, more):
                for n in range(NS):
                    state_input(r, k, n)
                    if back and n == MAMBA_STATE["gate_output"]:
                        gated(r - 1, 1 - k)
                    if more and n == MAMBA_STATE["inverse_rms"]:
                        inverse_rms(r + 1)
                    if more and n == MAMBA_STATE["step_sizes"]:
                        step_sizes(r + 1, 1 - k)
                    if more and n == MAMBA_STATE["weighted_u"]:
                        weighted_u(r + 1, 1 - k)
                if not more:
                    gated(r, k)

            rows(pool, first, body)

        @block.scalar
        def _(act):
            act.wait_ge(decay_ready, 16)
            nc.scalar.activation(decay[:], decay[:], ACT.Exp).then_inc(decay_ready, 1)
            act.wait_ge(decay_ready, 17)
            nc.scalar.mul(decay[:], decay[:], -1.0).then_inc(decay_ready, 1)
            act.wait_ge(decay_ready, 18)
            act.wait_ge(loaded, 16 * LOADS)
            act.wait_ge(pads, 2)
            act.sem_inc(bb_copied, 1)

            def copy_xT(r):
                act.wait_ge(xT_ps_ready, r + 1)
                act.wait_ge(proj_ready, r * 4)
                nc.scalar.copy(xT[0:D, 2:S + 2], W0[0:D, :])
                nc.scalar.copy(xT[D:2 * D, 3:S + 3], W0[D:2 * D, :]).then_inc(xT_ready, 1)

            def activate(r, k):
                for j in range(2 * NC):
                    W = (W1, W2, W0, W1)[j]
                    dst = (u if j < NC else gate)[k][:, j % NC, :]
                    act.wait_ge(proj_ready, r * 4 + (j + 1))
                    if not (isinstance(r, int) and r == 0) and j == 0:
                        act.wait_ge(yg_ready, r - 1)
                    bias = conv_b[:, j:j + 1] if j < NC else 0.0
                    nc.scalar.activation(dst, W[:], ACT.Silu, bias=bias).then_inc(silu_done, 1)

            def high_part(r, k):
                act.wait_ge(ssm_ready, r + 1)
                act.wait_ge(dt_ps_ready, r * 2)
                if not (isinstance(r, int) and r == 0):
                    act.wait_ge(cb_ready, r * NS - NS)
                nc.scalar.copy(dt_low[DT0:DT0 + R, :], W2[DT0:DT0 + R, :])
                nc.scalar.copy(parts[k][:], W2[0:DT0, :]).then_inc(hi_ready, 1)

            def middle_part(r, k):
                m, lo = slice(BC, 2 * BC), slice(2 * BC, 3 * BC)
                act.wait_ge(rest_ready, r + 1)
                nc.scalar.copy(parts[k][m, :], rest[m, :]).then_inc(mid_ready, 1)
                act.wait_ge(lo_ready, r)
                nc.scalar.copy(mid[lo, :], rest[lo, :]).then_inc(mid_tmp, 1)

            def softplus_exp(r):
                act.wait_ge(dt_ready, r)
                act.wait_ge(lost_ready, r)
                for c in range(NC):
                    W = (W0, W1)[c]
                    act.wait_ge(dt_ps_ready, r * 2 + (c + 1))
                    nc.scalar.activation(ex[:, c, :], W[:], ACT.Abs, bias=dt_b[:, c:c + 1]).then_inc(abs_ready, 1)
                    nc.scalar.activation(pos[:, c, :], W[:], ACT.Relu, bias=dt_b[:, c:c + 1]).then_inc(dt_ps_read, 1)
                act.wait_ge(abs_ready, r * 2 + 2)
                nc.scalar.activation(ex[:], ex[:], ACT.Exp, scale=-1.0).then_inc(ex_ready, 1)

            def softplus_log(r):
                act.wait_ge(ex_ready, r + 1)
                nc.scalar.add(one_ex[:], ex[:], 1.0).then_inc(one_ex_ready, 1)
                act.wait_ge(one_ex_ready, r + 1)
                nc.scalar.activation(log[:], one_ex[:], ACT.Ln).then_inc(log_ready, 1)

            def copy_b(r, n):
                q = r * NS + n
                act.wait_ge(bb_ready, q + 1)
                act.wait_ge(dbu_ready, q + 1)
                nc.scalar.copy(Bs[n % DEEP][:], Bb[:]).then_inc(bb_copied, 1)

            def decays(r, k, n):
                q = r * NS + n
                if n == 0:
                    act.wait_ge(dt_ready, r + 1)
                act.wait_ge(scan_done, q + (DEEP - 1))
                for c in range(NC):
                    last = nc.scalar.activation(dA[n % 2][:, c, :], dt[k][:, c, :], ACT.Exp, scale=decay[:, c, n:n + 1])
                last.then_inc(da_ready, 1)

            def first():
                copy_xT(0)
                activate(0, 0)
                high_part(0, 0)
                middle_part(0, 0)
                softplus_exp(0)
                softplus_log(0)
                for n in range(B_LEAD):
                    copy_b(0, n)

            def body(r, k, back, more):
                for n in range(NS):
                    if n + B_LEAD < NS:
                        copy_b(r, n + B_LEAD)
                    elif more:
                        copy_b(r + 1, n + B_LEAD - NS)
                    decays(r, k, n)
                    if more and n == MAMBA_STATE["copy_xT"]:
                        copy_xT(r + 1)
                    if more and n == MAMBA_STATE["activate"]:
                        activate(r + 1, 1 - k)
                    if more and n == MAMBA_STATE["high_part"]:
                        high_part(r + 1, 1 - k)
                    if more and n == MAMBA_STATE["middle_part"]:
                        middle_part(r + 1, 1 - k)
                    if more and n == MAMBA_STATE["softplus_exp"]:
                        softplus_exp(r + 1)
                    if more and n == MAMBA_STATE["softplus_log"]:
                        softplus_log(r + 1)

            rows(act, first, body)

        @block.vector
        def _(dve):
            dve.wait_ge(loaded, 16 * LOADS)
            st = Steps(dve, w_step, 0)
            st.then(nc.vector.tensor_tensor(pick_row[:], net.ident[0:DT0, 0:BC], net.ident[0:DT0, BC:2 * BC], ALU.add))
            st.then(nc.vector.tensor_tensor(pick_row[:], pick_row[:], net.ident[0:DT0, 2 * BC:3 * BC], ALU.add))
            st.then(nc.vector.tensor_copy(pick[:], pick_row[:].unsqueeze(2).to_broadcast([DT0, BC, P])))
            st.then(nc.vector.tensor_scalar(w_in[:], w_in[:], w_norm[:, 0:1], None, ALU.mult))
            st.then(nc.vector.tensor_tensor(w_u[:], w_conv[:], w_in[:, 0:NC * P].unsqueeze(1).to_broadcast([P, 2, NC * P]),
                                            ALU.mult))
            nc.vector.tensor_copy(w_g[:], w_in[0:D, NC * P:2 * NC * P]).then_inc(weights_ready, 1)
            dve.sem_inc(scan_done, DEEP)
            dve.sem_inc(hc_ready, CREDIT)

            def row(r):
                return X[:, bass.ds(r, 1)].rearrange("p a t d -> p (a t) d")

            def squares(r):
                nc.vector.tensor_tensor(sq[:], row(r), row(r), ALU.mult).then_inc(sq_ready, 1)
                dve.wait_ge(sq_ready, r + 1)
                nc.vector.reduce_sum(ssq[:], sq[:], axis=AX).then_inc(ssq_ready, 1)

            def normalise(r):
                dve.wait_ge(rstd_ready, r + 1)
                dve.wait_ge(xT_ps_ready, r)
                shape = [P, T, 2, D]
                nc.vector.tensor_tensor(xn[:], row(r).unsqueeze(2).to_broadcast(shape),
                                        rstd[:].unsqueeze(2).unsqueeze(3).to_broadcast(shape),
                                        ALU.mult).then_inc(xn_ready, 1)

            def remainder(r, k):
                dve.wait_ge(hi_ready, r + 1)
                dve.wait_ge(mid_ready, r)
                dve.wait_ge(lo_ready, r)
                nc.vector.tensor_tensor(rest[:], W2[0:DT0, :], parts[k][:], ALU.subtract).then_inc(rest_ready, 1)

            def low_part(r, k):
                lo = slice(2 * BC, 3 * BC)
                dve.wait_ge(mid_tmp, r + 1)
                nc.vector.tensor_tensor(parts[k][lo, :], rest[lo, :], mid[lo, :], ALU.subtract).then_inc(lo_ready, 1)

            def rounding_loss(r):
                dve.wait_ge(one_ex_ready, r + 1)
                dve.wait_ge(dt_ready, r)
                nc.vector.scalar_tensor_tensor(lost[:], one_ex[:], -1.0, ex[:], ALU.add, ALU.subtract).then_inc(lost_ready, 1)

            def exact_log(r):
                dve.wait_ge(log_ready, r + 1)
                dve.wait_ge(lost_ready, r + 1)
                nc.vector.tensor_tensor(log[:], log[:], lost[:], ALU.subtract).then_inc(exact_log_ready, 1)

            def scan(r, n):
                q = r * NS + n
                dve.wait_ge(da_ready, q + 1)
                dve.wait_ge(dbu_ready, q + (DEEP + 1))
                dve.wait_ge(hc_ready, q + 1)
                for c in range(NC):
                    last = nc.vector.tensor_tensor_scan(hs[n % 2][:, c, :], dA[n % 2][:, c, :], dBu[n % DEEP][:, c, :], 0.0,
                                                        ALU.mult, ALU.add)
                last.then_inc(scan_done, 1)

            def times_c(r, n):
                q = r * NS + n
                dve.wait_ge(scan_done, q + (DEEP + 1))
                dve.wait_ge(cb_ready, q + 1)
                dve.wait_ge(summed, q + 1)
                nc.vector.tensor_tensor(hC[n % 2][:], hs[n % 2][:], Cb[n % 2][:].unsqueeze(1).to_broadcast([P, NC, S]),
                                        ALU.mult).then_inc(hc_ready, 1)

            def skip_path(r, k):
                dve.wait_ge(summed, r * NS + (CREDIT + NS))
                dve.wait_ge(yg_ready, r)
                for c in range(NC):
                    last = nc.vector.scalar_tensor_tensor(yv[:, c, :], u[k][:, c, :], skip[:, c:c + 1], Y[c][:],
                                                          ALU.mult, ALU.add)
                last.then_inc(y_read, 1)

            def residual(r):
                dve.wait_ge(out_ready, r + 1)
                nc.vector.tensor_tensor(row(r), row(r), W2[:, 0:T * D].rearrange("p (t d) -> p t d", d=D),
                                        ALU.add).then_inc(x_done, 1)

            def first():
                squares(0)
                normalise(0)
                remainder(0, 0)
                low_part(0, 0)
                rounding_loss(0)
                exact_log(0)

            def body(r, k, back, more):
                for n in range(NS):
                    scan(r, n)
                    if n:
                        times_c(r, n - 1)
                    if back and n == 0:
                        times_c(r - 1, NS - 1)
                    if back and n == MAMBA_STATE["skip_path"]:
                        skip_path(r - 1, 1 - k)
                    if back and n == MAMBA_STATE["residual"]:
                        residual(r - 1)
                    if more and n == MAMBA_STATE["squares"]:
                        squares(r + 1)
                    if more and n == MAMBA_STATE["normalise"]:
                        normalise(r + 1)
                    if more and n == MAMBA_STATE["remainder"]:
                        remainder(r + 1, 1 - k)
                    if more and n == MAMBA_STATE["low_part"]:
                        low_part(r + 1, 1 - k)
                    if more and n == MAMBA_STATE["rounding_loss"]:
                        rounding_loss(r + 1)
                    if more and n == MAMBA_STATE["exact_log"]:
                        exact_log(r + 1)
                if not more:
                    times_c(r, NS - 1)
                    skip_path(r, k)
                    residual(r)

            rows(dve, first, body)

        @block.tensor
        def _(pe):
            pe.wait_ge(weights_ready, 1)
            pe.wait_ge(loaded, 16 * LOADS)
            pe.sem_inc(summed, CREDIT)

            def transpose(r):
                pe.wait_ge(xn_ready, r + 1)
                pe.wait_ge(dt_ps_read, r * NC)
                for m in range(T):
                    last = nc.tensor.transpose(W0[:, m * P:(m + 1) * P], xn[:, m].rearrange("p a d -> p (a d)"), net.ident[:])
                last.then_inc(xT_ps_ready, 1)

            def project_u(r, c):
                pe.wait_ge(xT_ready, r + 1)
                if c == 1 and not (isinstance(r, int) and r == 0):
                    pe.wait_ge(x_done, r - 1)
                W = (W1, W2)[c]
                for pair in range(2):
                    last = nc.tensor.matmul(W[:], w_u[:, pair, c * P:(c + 1) * P], xT[:, 2 - 2 * pair:2 - 2 * pair + S],
                                            start=(pair == 0), stop=(pair == 1))
                last.then_inc(proj_ready, 1)

            def project_gate(r, c):
                if c == 1:
                    pe.wait_ge(silu_done, r * 4 + 1)
                W = (W0, W1)[c]
                nc.tensor.matmul(W[:], w_g[:, c * P:(c + 1) * P], xT[0:D, 2:2 + S], start=True, stop=True).then_inc(proj_ready, 1)

            def project_ssm(r, k):
                pe.wait_ge(silu_done, r * 4 + 2)
                for c in range(NC):
                    last = nc.tensor.matmul(W2[0:DT0 + R, :], w_x[:, c, :], u[k][:, c, :], start=(c == 0), stop=(c == NC - 1))
                last.then_inc(ssm_ready, 1)

            def project_dt(r):
                pe.wait_ge(hi_ready, r + 1)
                pe.wait_ge(silu_done, r * 4 + 4)
                for c in range(NC):
                    nc.tensor.matmul((W0, W1)[c][:], w_dt[DT0:DT0 + R, c * P:(c + 1) * P], dt_low[DT0:DT0 + R, :],
                                     start=True, stop=True).then_inc(dt_ps_ready, 1)

            def b_row(r, k, n):
                q = r * NS + n
                if n == 0:
                    pe.wait_ge(mid_ready, r + 1)
                    pe.wait_ge(lo_ready, r + 1)
                pe.wait_ge(bb_copied, q + 1)
                nc.tensor.matmul(Bb[:], pick[:, n, :], parts[k][:], start=True, stop=True).then_inc(bb_ready, 1)

            def c_row(r, k, n):
                q = r * NS + n
                if n == 0:
                    pe.wait_ge(mid_ready, r + 1)
                    pe.wait_ge(lo_ready, r + 1)
                pe.wait_ge(hc_ready, q + 1)
                nc.tensor.matmul(Cb[n % 2][:], pick[:, NS + n, :], parts[k][:], start=True, stop=True).then_inc(cb_ready, 1)

            def sum_state(r, n):
                q = r * NS + n
                pe.wait_ge(hc_ready, q + (CREDIT + 1))
                if n == 0:
                    pe.wait_ge(y_read, r)
                for c in range(NC):
                    last = nc.tensor.matmul(Y[c][:], net.ident[:], hC[n % 2][:, c, :], start=(n == 0), stop=(n == NS - 1))
                last.then_inc(summed, 1)

            def output(r, more):
                pe.wait_ge(yg_ready, r + 1)
                if more:
                    pe.wait_ge(rest_ready, r + 2)
                else:
                    pe.wait_ge(x_done, r)
                for m in range(T):
                    for c in range(NC):
                        last = nc.tensor.matmul(W2[:, m * D:(m + 1) * D], yg[:, c, m * P:(m + 1) * P], w_out[:, c, :],
                                                start=(c == 0), stop=(c == NC - 1))
                last.then_inc(out_ready, 1)


            def first():
                transpose(0)
                project_u(0, 0)
                project_u(0, 1)
                project_gate(0, 0)
                project_gate(0, 1)
                project_ssm(0, 0)
                project_dt(0)
                c_row(0, 0, 0)
                for n in range(AHEAD):
                    b_row(0, 0, n)

            def body(r, k, back, more):
                for n in range(NS):
                    if n + AHEAD < NS:
                        b_row(r, k, n + AHEAD)
                    elif more:
                        b_row(r + 1, 1 - k, n + AHEAD - NS)
                    if n + 1 < NS:
                        c_row(r, k, n + 1)
                    elif more:
                        c_row(r + 1, 1 - k, 0)
                    if more and n == MAMBA_STATE["transpose"]:
                        transpose(r + 1)
                    if more and n == MAMBA_STATE["project_u0"]:
                        project_u(r + 1, 0)
                    if more and n == MAMBA_STATE["project_u1"]:
                        project_u(r + 1, 1)
                    if more and n == MAMBA_STATE["project_gate0"]:
                        project_gate(r + 1, 0)
                    if more and n == MAMBA_STATE["project_gate1"]:
                        project_gate(r + 1, 1)
                    if more and n == MAMBA_STATE["project_ssm"]:
                        project_ssm(r + 1, 1 - k)
                    if more and n == MAMBA_STATE["project_dt"]:
                        project_dt(r + 1)
                    sum_state(r, n)
                    if back and n == MAMBA_STATE["output"]:
                        output(r - 1, True)
                if not more:
                    output(r, False)

            rows(pe, first, body)


def mamba_end_stage(net, X):
    nc, t, B, S, D, T = net.nc, net.t, net.B, net.S, net.D, net.T
    G = 4 if B % 4 == 0 else 2
    GROUPS = B // G
    SHAPE = [P, G * T, D]
    with ExitStack() as ctx:
        def sb(name, shape, dt=F32):
            return ctx.enter_context(nc.sbuf_tensor(f"e_{name}", shape, dt))

        def sem(name):
            return net.semaphore(ctx, f"e_{name}")

        affine = sb("affine", [P, 3, D])
        half = sb("half", [P, G * T])
        total_x, rstd_x = sb("total_x", [P, G * T]), sb("rstd_x", [P, G * T])
        total, rstd = sb("total", [P, G * T]), sb("rstd", [P, G * T])
        sq_x, sq = sb("sq_x", SHAPE), sb("sq", SHAPE)
        v, cen, w = sb("v", SHAPE), sb("cen", SHAPE), sb("w", SHAPE)
        loaded, set_up, dve_step, pool_step = sem("loaded"), sem("set_up"), sem("dve_step"), sem("pool_step")
        sq_x_ready, ssq_ready, rstd_x_ready = sem("sq_x_ready"), sem("ssq_ready"), sem("rstd_x_ready")
        cen_ready, sq_ready, var_ready, rstd_ready = sem("cen_ready"), sem("sq_ready"), sem("var_ready"), sem("rstd_ready")
        w_ready, added, pool_passed = sem("w_ready"), sem("added"), sem("pool_passed")
        block = ctx.enter_context(nc.Block())

        def rows(tensor, i):
            return tensor[:, bass.ds(i * G, G)].rearrange("p b t d -> p (b t) d")

        def vec(k):
            return affine[:, k, :].unsqueeze(1).to_broadcast(SHAPE)

        @block.sync
        def _(sp):
            for k, name in enumerate(("normf_w", "post_g", "post_b")):
                sp.dma_start(affine[:, k, :], t[name].partition_broadcast(P)).then_inc(loaded, 16)

        @block.gpsimd
        def _(pool):
            nc.gpsimd.memset(half[:], -0.5).then_inc(set_up, 1)
            pool.wait_ge(set_up, 1)
            pool.wait_ge(loaded, 48)

            def inverse_root(st, src, dst, ready):
                st.then(nc.gpsimd.tensor_scalar(dst[:], src[:], 1.0 / D, EPS, ALU.mult, ALU.add))
                nc.gpsimd.tensor_tensor(dst[:], dst[:], half[:], ALU.pow).then_inc(ready, 1)

            def one_group(i, more):
                st = Steps(pool, pool_step, i * POOL_STEPS + 1, pool_passed)
                if more:
                    wait_all(pool, pool_passed, (ssq_ready, i + 2))
                    inverse_root(st, total_x, rstd_x, rstd_x_ready)
                wait_all(pool, pool_passed, (var_ready, i + 1))
                inverse_root(st, total, rstd, rstd_ready)
                wait_all(pool, pool_passed, (w_ready, i + 1))
                st.then(nc.gpsimd.tensor_tensor(w[:], w[:], vec(1), ALU.mult))
                st.then(nc.gpsimd.tensor_tensor(w[:], w[:], vec(2), ALU.add))
                nc.gpsimd.tensor_tensor(rows(net.H, i), rows(net.H, i), w[:], ALU.add).then_inc(added, 1)

            POOL_STEPS = 4
            pool.wait_ge(ssq_ready, 1)
            inverse_root(Steps(pool, pool_step, 0), total_x, rstd_x, rstd_x_ready)
            with pool.Fori(0, GROUPS - 1) as i:
                one_group(i, True)
            one_group(GROUPS - 1, False)

        @block.scalar
        def _(act):
            def square_x(i):
                nc.scalar.activation(sq_x[:], rows(X, i), ACT.Square).then_inc(sq_x_ready, 1)

            def square(i):
                act.wait_ge(cen_ready, i + 1)
                nc.scalar.activation(sq[:], cen[:], ACT.Square).then_inc(sq_ready, 1)

            square_x(0)
            with act.Fori(0, GROUPS - 1) as i:
                act.wait_ge(ssq_ready, i + 1)
                square_x(i + 1)
                square(i)
            square(GROUPS - 1)

        @block.vector
        def _(dve):
            dve.wait_ge(loaded, 48)

            def sum_squares_x(i):
                dve.wait_ge(sq_x_ready, i + 1)
                nc.vector.reduce_sum(total_x[:], sq_x[:], axis=AX).then_inc(ssq_ready, 1)

            def one_group(i, more):
                st = Steps(dve, dve_step, i * DVE_STEPS)
                dve.wait_ge(rstd_x_ready, i + 1)
                st.then(nc.vector.tensor_tensor(v[:], rows(X, i), rstd_x[:].unsqueeze(2).to_broadcast(SHAPE), ALU.mult))
                st.then(nc.vector.tensor_tensor(v[:], v[:], vec(0), ALU.mult))
                st.then(nc.vector.reduce_sum(total[:], v[:], axis=AX))
                nc.vector.scalar_tensor_tensor(cen[:], total[:].unsqueeze(2).to_broadcast(SHAPE), -1.0 / D, v[:],
                                               ALU.mult, ALU.add).then_inc(cen_ready, 1)
                if more:
                    sum_squares_x(i + 1)
                dve.wait_ge(cen_ready, i + 1)
                dve.wait_ge(sq_ready, i + 1)
                nc.vector.reduce_sum(total[:], sq[:], axis=AX).then_inc(var_ready, 1)
                dve.wait_ge(rstd_ready, i + 1)
                if not (isinstance(i, int) and i == 0):
                    dve.wait_ge(added, i)
                st.then(nc.vector.tensor_tensor(w[:], cen[:], rstd[:].unsqueeze(2).to_broadcast(SHAPE), ALU.mult))
                dve.sem_inc(w_ready, 1)

            DVE_STEPS = 4
            sum_squares_x(0)
            one_group(0, True)
            with dve.Fori(1, GROUPS - 1) as i:
                one_group(i, True)
            one_group(GROUPS - 1, False)


EXPERT_TILE = {
    "centre": 0, "variance": 1, "take": 3, "xn": 3, "turn_x": 5, "gates": 7, "best": 8,
    "second": 9, "softmax": 10, "parts": 12, "turn_weights": 13, "turn_y": 2,
}
EXPERT_TILE_SCALAR = {
    "yT": 1, "xT": 5, "xT2": 6, "exp": 10, "combT": 14,
}


def experts_stage(net, name, final_out):
    nc, t, B, S, D, T = net.nc, net.t, net.B, net.S, net.D, net.T
    E = t[f"{name}_gate"].shape[1]
    J = t[f"{name}_w1"].shape[1]
    PER = J // E
    LAG = 2
    RING = 4
    PARTS = 3 * E
    final = final_out is not None
    with ExitStack() as ctx:
        def sb(n, shape, dt=F32):
            return ctx.enter_context(nc.sbuf_tensor(f"{name}_{n}", shape, dt))

        def sem(n):
            return net.semaphore(ctx, f"{name}_{n}")

        def bank(n):
            return ctx.enter_context(nc.psum_tensor(f"{name}_{n}", [P, S], F32))

        w1 = [sb(f"w1s{k}", [2 * D, J, P], BF16) for k in range(3)]
        w1_whole = sb("w1_whole", [2 * D, J, P])
        b1 = sb("b1s", [P, J])
        w2 = sb("w2s", [P, J, D])
        b2 = sb("b2s", [PARTS, D])
        w_gate = [sb(f"w_gate{k}", [2 * D, E], BF16) for k in range(3)]
        w_gate_whole = sb("w_gate_whole", [2 * D, E])
        gate_b = sb("gate_b", [P, E])
        order = sb("order", [P, E])
        affine = sb("affine", [P, 2, D])
        pick_row = sb("pick_row", [PARTS, E])
        pick = sb("pick", [PARTS, E, P], BF16)
        ident16 = sb("ident16", [P, P], BF16)
        half = sb("half", [P, T])
        total, rstd = sb("total", [P, T]), sb("rstd", [P, T])
        cen, sq = sb("cen", [P, T, D]), sb("sq", [P, T, D])
        xn = [sb(f"xn{k}", [P, T, D]) for k in range(2)]
        x_rest = sb("x_rest", [P, T, D])
        x_parts = sb("x_parts", [P, 2, T, 2, D], BF16)
        xT = [sb(f"xT{k}", [2 * D, 2, S], BF16) for k in range(2)]
        g = sb("g", [P, T, E])
        best = sb("best", [P, 4, T])
        mark = [sb(f"mark{k}", [P, T, E]) for k in range(4)]
        prob = sb("prob", [P, 4, T])
        comb = sb("comb", [P, T, E])
        parts = sb("parts", [P, T, 3, E], BF16)
        combT16 = [sb(f"combT16_{k}", [PARTS, S], BF16) for k in range(2)]
        combT = [sb(f"combT{k}", [PARTS, S]) for k in range(2)]
        hid = [sb(f"hid{k}", [P, S]) for k in range(RING)]
        relu = [sb(f"relu{k}", [P, S]) for k in range(2)]
        yT = sb("yT", [D, S])
        joined = sb("joined", [P, T, D])
        total2, rstd2 = sb("total2", [P, T]), sb("rstd2", [P, T])
        cen2, sq2 = sb("cen2", [P, T, D]), sb("sq2", [P, T, D])
        result = [sb(f"result{k}", [P, T, D]) for k in range(2)]
        h_ps = [bank(f"h_ps{k}") for k in range(2)]
        c_ps = [bank(f"c_ps{k}") for k in range(2)]
        y_ps = [bank(f"y_ps{k}") for k in range(2)]
        front_ps, back_ps = bank("front_ps"), bank("back_ps")

        loaded, set_up, made = sem("loaded"), sem("set_up"), sem("made")
        front_step, back_step, pool_step = sem("front_step"), sem("back_step"), sem("pool_step")
        var_ready, rstd_ready, xn_ready = sem("var_ready"), sem("rstd_ready"), sem("xn_ready")
        xT_ps_ready, xT_ready, gates_ready = sem("xT_ps_ready"), sem("xT_ready"), sem("gates_ready")
        diff_ready, exp_ready, parts_ready = sem("diff_ready"), sem("exp_ready"), sem("parts_ready")
        combT_ps_ready, combT_ready = sem("combT_ps_ready"), sem("combT_ready")
        relu_ready = sem("relu_ready")
        h_ready, hid_ready = sem("h_ready"), sem("hid_ready")
        y_ready, yT_ready, back_ready, back_taken = sem("y_ready"), sem("yT_ready"), sem("back_ready"), sem("back_taken")
        var2_ready, row_done = sem("var2_ready"), sem("row_done")
        stored = [sem(f"stored{k}") for k in range(2)]
        pool_passed, pe_passed, dve_passed = sem("pool_passed"), sem("pe_passed"), sem("dve_passed")
        block = ctx.enter_context(nc.Block())
        LOADS = 7 + 2 * final
        full, small = [P, T, D], [P, T, E]
        POOL_STEPS = 1 + (1 + 1 + 3) * final
        MADE = 4 + 2 * 5
        FRONT_STEPS = 3 + 5 + 4 + 4 + 4 + 3 + 3 + 4
        BACK_STEPS = 4

        def row_of_H(r):
            return net.H[:, bass.ds(r, 1)].rearrange("p a t d -> p (a t) d")

        @block.sync
        def _(sp):
            sp.dma_start(w1_whole[:], t[f"{name}_w1"]).then_inc(loaded, 16)
            sp.dma_start(b1[:], t[f"{name}_b1"]).then_inc(loaded, 16)
            sp.dma_start(w2[:], t[f"{name}_w2"]).then_inc(loaded, 16)
            sp.dma_start(b2[:], t[f"{name}_b2"]).then_inc(loaded, 16)
            sp.dma_start(w_gate_whole[:], t[f"{name}_gate"]).then_inc(loaded, 16)
            sp.dma_start(gate_b[:], t[f"{name}_gate_b"].partition_broadcast(P)).then_inc(loaded, 16)
            sp.dma_start(order[:], t[f"{name}_order"]).then_inc(loaded, 16)
            if final:
                sp.dma_start(affine[:, 0, :], t["f1_gamma"].partition_broadcast(P)).then_inc(loaded, 16)
                sp.dma_start(affine[:, 1, :], t["f1_beta"].partition_broadcast(P)).then_inc(loaded, 16)
                out = final_out.rearrange("b (t p) d -> b p t d", p=P)
                with sp.Fori(0, B // 2) as i:
                    for k in range(2):
                        sp.wait_ge(row_done, i * 2 + (k + 1))
                        sp.dma_start(out[i * 2 + k], result[k][:]).then_inc(stored[k], 16)
                for k in range(2):
                    sp.wait_ge(stored[k], 16 * (B // 2))

        @block.gpsimd
        def _(pool):
            nc.gpsimd.memset(half[:], -0.5).then_inc(set_up, 1)
            pool.wait_ge(set_up, 1)
            pool.wait_ge(loaded, 16 * LOADS)
            if not final:
                with pool.Fori(0, B) as r:
                    wait_all(pool, pool_passed, (var_ready, r + 1))
                    st = Steps(pool, pool_step, r)
                    st.then(nc.gpsimd.tensor_scalar(rstd[:], total[:], 1.0 / D, EPS, ALU.mult, ALU.add))
                    nc.gpsimd.tensor_tensor(rstd[:], rstd[:], half[:], ALU.pow).then_inc(rstd_ready, 1)
                return

            def front(r, st):
                wait_all(pool, pool_passed, (var_ready, r + 1))
                st.then(nc.gpsimd.tensor_scalar(rstd[:], total[:], 1.0 / D, EPS, ALU.mult, ALU.add))
                nc.gpsimd.tensor_tensor(rstd[:], rstd[:], half[:], ALU.pow).then_inc(rstd_ready, 1)

            def back(r, k, turn, st):
                wait_all(pool, pool_passed, (var2_ready, r + 1))
                st.then(nc.gpsimd.tensor_scalar(rstd2[:], total2[:], 1.0 / D, EPS, ALU.mult, ALU.add))
                st.then(nc.gpsimd.tensor_tensor(rstd2[:], rstd2[:], half[:], ALU.pow))
                if not (isinstance(turn, int) and turn == 0):
                    wait_all(pool, pool_passed, (stored[k], turn * 16))
                y = result[k]
                st.then(nc.gpsimd.tensor_tensor(y[:], cen2[:], rstd2[:].unsqueeze(2).to_broadcast(full), ALU.mult))
                st.then(nc.gpsimd.tensor_tensor(y[:], y[:], affine[:, 0, :].unsqueeze(1).to_broadcast(full), ALU.mult))
                st.then(nc.gpsimd.tensor_tensor(y[:], y[:], affine[:, 1, :].unsqueeze(1).to_broadcast(full), ALU.add))
                nc.gpsimd.tensor_tensor(y[:], y[:], row_of_H(r), ALU.add).then_inc(row_done, 1)

            front(0, Steps(pool, pool_step, 0, pool_passed))
            front(1, Steps(pool, pool_step, 1, pool_passed))
            for r in range(2):
                st = Steps(pool, pool_step, 2 + r * POOL_STEPS, pool_passed)
                front(r + 2, st)
                back(r, r, 0, st)
            with pool.Fori(1, B // 2 - 1) as i:
                for k in range(2):
                    st = Steps(pool, pool_step, (i * 2 + k) * POOL_STEPS + 2, pool_passed)
                    front(i * 2 + (k + 2), st)
                    back(i * 2 + k, k, i, st)
            st = Steps(pool, pool_step, (B - 2) * POOL_STEPS + 2, pool_passed)
            for k in range(2):
                back(B - 2 + k, k, B // 2 - 1, st)

        @block.scalar
        def _(act):
            act.wait_ge(loaded, 16 * LOADS)

            def front(r, k, e):
                if e == EXPERT_TILE_SCALAR["xT"]:
                    act.wait_ge(xT_ps_ready, r * 2 + 1)
                    nc.scalar.copy(xT[k][:, 0, :], front_ps[:]).then_inc(xT_ready, 1)
                if e == EXPERT_TILE_SCALAR["xT2"]:
                    act.wait_ge(xT_ps_ready, r * 2 + 2)
                    nc.scalar.copy(xT[k][:, 1, :], front_ps[:]).then_inc(xT_ready, 1)
                if e == EXPERT_TILE_SCALAR["exp"]:
                    act.wait_ge(diff_ready, r + 1)
                    nc.scalar.activation(prob[:, 0, :], prob[:, 0, :], ACT.Exp).then_inc(exp_ready, 1)
                if e == EXPERT_TILE_SCALAR["combT"]:
                    act.wait_ge(combT_ps_ready, r + 1)
                    nc.scalar.copy(combT16[k][:], front_ps[0:PARTS, :]).then_inc(combT_ready, 1)
                    nc.scalar.copy(combT[k][:], front_ps[0:PARTS, :]).then_inc(combT_ready, 1)

            def back(r, k):
                act.wait_ge(y_ready, r + 1)
                nc.scalar.copy(yT[:], y_ps[k][0:D, :]).then_inc(yT_ready, 1)

            def one_row(r, k, number=None):
                for j in range(J):
                    act.wait_ge(h_ready, r * J + (j + 1))
                    act.wait_ge(hid_ready, r * J + (j + 1))
                    nc.scalar.activation(relu[j % 2][:], h_ps[j % 2][:], ACT.Relu, bias=b1[:, j:j + 1]).then_inc(relu_ready, 1)
                    if j == EXPERT_TILE_SCALAR["yT"] and number != 0:
                        back(r - 1, 1 - k)
                    if number != B - 1:
                        front(r + 1, 1 - k, j)

            for j in range(J):
                front(0, 0, j)
            one_row(0, 0, 0)
            one_row(1, 1, 1)
            with act.Fori(1, B // 2 - 1) as i:
                for k in range(2):
                    one_row(i * 2 + k, k)
            one_row(B - 2, 0, B - 2)
            one_row(B - 1, 1, B - 1)
            back(B - 1, 1)

        @block.vector
        def _(dve):
            dve.wait_ge(loaded, 16 * LOADS)
            st = Steps(dve, made, 0)
            st.then(nc.vector.tensor_tensor(pick_row[:], net.ident[0:PARTS, 0:E], net.ident[0:PARTS, E:2 * E], ALU.add))
            st.then(nc.vector.tensor_tensor(pick_row[:], pick_row[:], net.ident[0:PARTS, 2 * E:3 * E], ALU.add))
            st.then(nc.vector.tensor_copy(pick[:], pick_row[:].unsqueeze(2).to_broadcast([PARTS, E, P])))
            st.then(nc.vector.tensor_copy(ident16[:], net.ident[:]))
            for whole, part in ((w1_whole, w1), (w_gate_whole, w_gate)):
                st.then(nc.vector.tensor_copy(part[0][:], whole[:]))
                st.then(nc.vector.tensor_copy(part[2][:], whole[:]))
                st.then(nc.vector.tensor_tensor(whole[:], whole[:], part[0][:], ALU.subtract))
                st.then(nc.vector.tensor_copy(part[1][:], whole[:]))
                st.then(nc.vector.tensor_tensor(part[2][0:D], whole[0:D], part[1][0:D], ALU.subtract))
            assert st.n == MADE
            dve.sem_inc(hid_ready, LAG)

            def front(r, k, n, st):
                a, f, b, c = mark
                first, found, second, found2 = (best[:, m, :] for m in range(4))
                if n == EXPERT_TILE["centre"]:
                    h = row_of_H(r)
                    st.then(nc.vector.reduce_sum(total[:], h, axis=AX))
                    st.then(nc.vector.scalar_tensor_tensor(cen[:], total[:].unsqueeze(2).to_broadcast(full), -1.0 / D, h,
                                                           ALU.mult, ALU.add))
                if n == EXPERT_TILE["variance"]:
                    st.then(nc.vector.tensor_tensor(sq[:], cen[:], cen[:], ALU.mult))
                    nc.vector.reduce_sum(total[:], sq[:], axis=AX).then_inc(var_ready, 1)
                if n == EXPERT_TILE["xn"]:
                    dve.wait_ge(rstd_ready, r + 1)
                    if final and not (isinstance(r, int) and r < 2):
                        dve.wait_ge(back_taken, r - 1)
                    st.then(nc.vector.tensor_tensor(xn[k][:], cen[:], rstd[:].unsqueeze(2).to_broadcast(full), ALU.mult))
                    st.then(nc.vector.tensor_copy(x_parts[:, 0, :, 0, :], xn[k][:]))
                    st.then(nc.vector.tensor_tensor(x_rest[:], xn[k][:], x_parts[:, 0, :, 0, :], ALU.subtract))
                if n == EXPERT_TILE["xn"] + 1:
                    st.then(nc.vector.tensor_copy(x_parts[:, 0, :, 1, :], x_rest[:]))
                    dve.sem_inc(xn_ready, 1)
                    st.then(nc.vector.tensor_tensor(x_parts[:, 1, :, 1, :], x_rest[:], x_parts[:, 0, :, 1, :], ALU.subtract))
                    nc.vector.tensor_copy(x_parts[:, 1, :, 0, :], x_parts[:, 0, :, 0, :]).then_inc(xn_ready, 1)
                rank = order[:].unsqueeze(1).to_broadcast(small)
                if n == EXPERT_TILE["best"]:
                    dve.wait_ge(gates_ready, r + 1)
                    st.then(nc.vector.tensor_tensor(g[:], front_ps[:, 0:T * E].rearrange("p (t e) -> p t e", t=T),
                                                    gate_b[:].unsqueeze(1).to_broadcast(small), ALU.add))
                    st.then(nc.vector.reduce_max(first, g[:], axis=AX))
                    st.then(nc.vector.tensor_tensor(a[:], g[:], first.unsqueeze(2).to_broadcast(small), ALU.is_equal))
                    st.then(nc.vector.tensor_tensor(a[:], a[:], rank, ALU.mult))
                if n == EXPERT_TILE["best"] + 1:
                    st.then(nc.vector.reduce_max(found, a[:], axis=AX))
                    st.then(nc.vector.tensor_tensor(f[:], a[:], found.unsqueeze(2).to_broadcast(small), ALU.is_equal))
                    st.then(nc.vector.scalar_tensor_tensor(g[:], f[:], DROPPED, g[:], ALU.mult, ALU.add))
                    st.then(nc.vector.reduce_max(second, g[:], axis=AX))
                if n == EXPERT_TILE["second"]:
                    nc.vector.tensor_tensor(prob[:, 0, :], second, first, ALU.subtract).then_inc(diff_ready, 1)
                    st.then(nc.vector.tensor_tensor(b[:], g[:], second.unsqueeze(2).to_broadcast(small), ALU.is_equal))
                    st.then(nc.vector.tensor_tensor(b[:], b[:], rank, ALU.mult))
                    st.then(nc.vector.reduce_max(found2, b[:], axis=AX))
                    st.then(nc.vector.tensor_tensor(c[:], b[:], found2.unsqueeze(2).to_broadcast(small), ALU.is_equal))
                if n == EXPERT_TILE["softmax"]:
                    dve.wait_ge(exp_ready, r + 1)
                    st.then(nc.vector.tensor_scalar(prob[:, 1, :], prob[:, 0, :], 1.0, None, ALU.add))
                    st.then(nc.vector.reciprocal(prob[:, 2, :], prob[:, 1, :]))
                    st.then(nc.vector.tensor_tensor(prob[:, 3, :], prob[:, 0, :], prob[:, 2, :], ALU.mult))
                if n == EXPERT_TILE["softmax"] + 1:
                    st.then(nc.vector.tensor_tensor(f[:], f[:], prob[:, 2, :].unsqueeze(2).to_broadcast(small), ALU.mult))
                    st.then(nc.vector.tensor_tensor(c[:], c[:], prob[:, 3, :].unsqueeze(2).to_broadcast(small), ALU.mult))
                    st.then(nc.vector.tensor_tensor(comb[:], f[:], c[:], ALU.add))
                if n == EXPERT_TILE["parts"]:
                    st.then(nc.vector.tensor_copy(parts[:, :, 0, :], comb[:]))
                    st.then(nc.vector.tensor_tensor(comb[:], comb[:], parts[:, :, 0, :], ALU.subtract))
                    st.then(nc.vector.tensor_copy(parts[:, :, 1, :], comb[:]))
                    st.then(nc.vector.tensor_tensor(parts[:, :, 2, :], comb[:], parts[:, :, 1, :], ALU.subtract))
                    dve.sem_inc(parts_ready, 1)

            def back(r, k, n, st, first):
                if n == EXPERT_TILE["take"]:
                    dve.wait_ge(back_ready, r + 1)
                    y = back_ps[:, 0:T * D].rearrange("p (t d) -> p t d", t=T)
                    if not final:
                        nc.vector.tensor_tensor(row_of_H(r), row_of_H(r), y, ALU.add).then_inc(back_taken, 1)
                    else:
                        nc.vector.tensor_tensor(joined[:], xn[k][:], y, ALU.add).then_inc(back_taken, 1)
                if final and n == EXPERT_TILE["take"] + 1:
                    dve.wait_ge(back_taken, r + 1)
                    if not first:
                        dve.wait_ge(row_done, r)
                    st.then(nc.vector.reduce_sum(total2[:], joined[:], axis=AX))
                    st.then(nc.vector.scalar_tensor_tensor(cen2[:], total2[:].unsqueeze(2).to_broadcast(full), -1.0 / D, joined[:],
                                                           ALU.mult, ALU.add))
                if final and n == EXPERT_TILE["take"] + 2:
                    st.then(nc.vector.tensor_tensor(sq2[:], cen2[:], cen2[:], ALU.mult))
                    st.then(nc.vector.reduce_sum(total2[:], sq2[:], axis=AX))
                    dve.sem_inc(var2_ready, 1)

            def one_row(r, k, number=None):
                ahead = Steps(dve, front_step, (r + 1) * FRONT_STEPS)
                done = Steps(dve, back_step, (r - 1) * BACK_STEPS)
                for j in range(J):
                    dve.wait_ge(relu_ready, r * J + (j + 1))
                    nc.vector.tensor_tensor(hid[j % RING][:], relu[j % 2][:], c_ps[(j // PER) % 2][:], ALU.mult).then_inc(hid_ready, 1)
                    if number != 0:
                        back(r - 1, 1 - k, j, done, number == 1)
                    if number != B - 1:
                        front(r + 1, 1 - k, j, ahead)

            st = Steps(dve, front_step, 0)
            for j in range(J):
                front(0, 0, j, st)
            assert st.n == FRONT_STEPS, st.n
            one_row(0, 0, 0)
            one_row(1, 1, 1)
            with dve.Fori(1, B // 2 - 1) as i:
                for k in range(2):
                    one_row(i * 2 + k, k)
            one_row(B - 2, 0, B - 2)
            one_row(B - 1, 1, B - 1)
            st = Steps(dve, back_step, (B - 1) * BACK_STEPS)
            for j in range(J):
                back(B - 1, 1, j, st, False)

        @block.tensor
        def _(pe):
            pe.wait_ge(loaded, 16 * LOADS)
            pe.wait_ge(made, MADE)

            def front(r, k, n):
                for p in range(2):
                    if n == EXPERT_TILE["turn_x"] + p:
                        if isinstance(r, int) and r == 0 and p == 0:
                            wait_all(pe, pe_passed, (xn_ready, 1))
                        elif p == 0:
                            wait_all(pe, pe_passed, (combT_ready, r * 2), (xn_ready, r * 2 + 1))
                        else:
                            wait_all(pe, pe_passed, (xT_ready, r * 2 + 1), (xn_ready, r * 2 + 2))
                        for m in range(T):
                            last = nc.tensor.matmul(front_ps[:, m * P:(m + 1) * P], x_parts[:, p, m].rearrange("p a d -> p (a d)"),
                                                    ident16[:], start=True, stop=True)
                        last.then_inc(xT_ps_ready, 1)
                if n == EXPERT_TILE["gates"]:
                    pe.wait_ge(xT_ready, r * 2 + 2)
                    for m in range(T):
                        for p in range(3):
                            last = nc.tensor.matmul(front_ps[:, m * E:(m + 1) * E], xT[k][:, p // 2, m * P:(m + 1) * P], w_gate[p][:],
                                                    start=(p == 0), stop=(p == 2))
                    last.then_inc(gates_ready, 1)
                if n == EXPERT_TILE["turn_weights"]:
                    wait_all(pe, pe_passed, (parts_ready, r + 1))
                    for m in range(T):
                        last = nc.tensor.matmul(front_ps[0:PARTS, m * P:(m + 1) * P], parts[:, m].rearrange("p a e -> p (a e)"),
                                                ident16[:], start=True, stop=True)
                    last.then_inc(combT_ps_ready, 1)

            def back(r, k, n, first):
                if n == EXPERT_TILE["turn_y"]:
                    if first:
                        wait_all(pe, pe_passed, (yT_ready, r + 1))
                    else:
                        wait_all(pe, pe_passed, (back_taken, r), (yT_ready, r + 1))
                    for m in range(T):
                        last = nc.tensor.transpose(back_ps[:, m * D:(m + 1) * D], yT[:, m * P:(m + 1) * P], net.ident[0:D, 0:D])
                    last.then_inc(back_ready, 1)

            def down(r, k, j, first):
                y = y_ps[k][0:D, :]
                if j == 0:
                    if not first:
                        wait_all(pe, pe_passed, (yT_ready, r - 1))
                    nc.tensor.matmul(y, b2[:], combT[k][:], start=True, stop=False)
                last = nc.tensor.matmul(y, w2[:, j, :], hid[j % RING][:], start=False, stop=(j == J - 1))
                if j == J - 1:
                    last.then_inc(y_ready, 1)

            def one_row(r, k, number=None):
                pe.wait_ge(combT_ready, r * 2 + 2)
                for j in range(J):
                    pe.wait_ge(hid_ready, r * J + (j + 1))
                    if j % PER == 0:
                        nc.tensor.matmul(c_ps[(j // PER) % 2][:], pick[:, j // PER, :], combT16[k][:], start=True, stop=True)
                    for p in range(3):
                        last = nc.tensor.matmul(h_ps[j % 2][:], w1[p][:, j, :], xT[k][:, p // 2, :], start=(p == 0), stop=(p == 2))
                    last.then_inc(h_ready, 1)
                    if j >= LAG:
                        down(r, k, j - LAG, number in (0, 1))
                    elif number != 0:
                        down(r - 1, 1 - k, j - LAG + J, False)
                    if number != 0:
                        back(r - 1, 1 - k, j, number == 1)
                    if number != B - 1:
                        front(r + 1, 1 - k, j)

            for j in range(J):
                front(0, 0, j)
            one_row(0, 0, 0)
            one_row(1, 1, 1)
            with pe.Fori(1, B // 2 - 1) as i:
                for k in range(2):
                    one_row(i * 2 + k, k)
            one_row(B - 2, 0, B - 2)
            one_row(B - 1, 1, B - 1)
            for j in range(LAG):
                pe.wait_ge(hid_ready, B * J + (j + 1))
                down(B - 1, 1, j - LAG + J, False)
            for j in range(J):
                back(B - 1, 1, j, False)


def attention_stage(net):
    nc, t, B, S, D, T = net.nc, net.t, net.B, net.S, net.D, net.T
    SCALE = float(D) ** -0.5
    RING = 4
    with ExitStack() as ctx:
        def sb(n, shape, dt=F32):
            return ctx.enter_context(nc.sbuf_tensor(f"a_{n}", shape, dt))

        def sem(n):
            return net.semaphore(ctx, f"a_{n}")

        def bank(n):
            return ctx.enter_context(nc.psum_tensor(f"a_{n}", [P, S], F32))

        wq = sb("wq", [D + 1, D])
        wk = sb("wk", [D + 1, D])
        wv = sb("wv", [D, D + 1])
        wo = sb("wo", [D, D])
        wvo = sb("wvo", [D + 1, D + 2])
        bo = sb("bo", [P, D])
        half = sb("half", [P, T])
        total, rstd = sb("total", [P, T]), sb("rstd", [P, T])
        cen, sq, xn = sb("cen", [P, T, D]), sb("sq", [P, T, D]), sb("xn", [P, T, D])
        xT = sb("xT", [D + 1, S])
        qT = [sb(f"qT{k}", [D, S]) for k in range(2)]
        kT = [sb(f"kT{k}", [D, S]) for k in range(2)]
        v = [sb(f"v{k}", [P, T, D + 1]) for k in range(2)]
        mask = [sb(f"mask{k}", [P, T, 2]) for k in range(2)]
        mx, bias = sb("mx", [P, T]), sb("bias", [P, T])
        p = [sb(f"p{k}", [P, S]) for k in range(RING)]
        pT = [sb(f"pT{k}", [P, T, P]) for k in range(2)]
        factor = sb("factor", [P, T])
        o = sb("o", [P, T, D])
        s_ps = [bank(f"s_ps{k}") for k in range(2)]
        pT_ps = [bank(f"pT_ps{k}") for k in range(2)]
        o_ps = [bank(f"o_ps{k}") for k in range(2)]
        xk_ps, qv_ps = bank("xk_ps"), bank("qv_ps")

        loaded, set_up, wvo_ps_ready, wvo_ready = sem("loaded"), sem("set_up"), sem("wvo_ps_ready"), sem("wvo_ready")
        ln_step, pool_step, end_step = sem("ln_step"), sem("pool_step"), sem("end_step")
        var_ready, rstd_ready, xn_ready = sem("var_ready"), sem("rstd_ready"), sem("xn_ready")
        xT_ps_ready, xT_ready = sem("xT_ps_ready"), sem("xT_ready")
        q_ps_ready, q_ready, k_ps_ready, k_ready = sem("q_ps_ready"), sem("q_ready"), sem("k_ps_ready"), sem("k_ready")
        v_ps_ready, v_ready, mask_ready = sem("v_ps_ready"), sem("v_ready"), sem("mask_ready")
        s_ready, mx_ready, bias_ready, p_ready = sem("s_ready"), sem("mx_ready"), sem("bias_ready"), sem("p_ready")
        pT_ps_ready, pT_ready, o_ready, o_taken = sem("pT_ps_ready"), sem("pT_ready"), sem("o_ready"), sem("o_taken")
        pool_passed, pe_passed = sem("pool_passed"), sem("pe_passed")
        block = ctx.enter_context(nc.Block())
        LOADS = 6
        SET_UP = 4
        LN_STEPS = 3
        END_STEPS = 5
        full = [P, T, D]

        def row_of_H(r):
            return net.H[:, bass.ds(r, 1)].rearrange("p a t d -> p (a t) d")

        def v_of(ps):
            return ps[:, 0:T * (D + 2)].rearrange("p (t d) -> p t d", t=T)

        @block.sync
        def _(sp):
            sp.dma_start(wq[:], t["a_wq"]).then_inc(loaded, 16)
            sp.dma_start(wk[:], t["a_wk"]).then_inc(loaded, 16)
            sp.dma_start(wv[:], t["a_wv"]).then_inc(loaded, 16)
            sp.dma_start(wo[:], t["a_wo"]).then_inc(loaded, 16)
            sp.dma_start(bo[:], t["a_bo"].partition_broadcast(P)).then_inc(loaded, 16)
            sp.dma_start(wvo[:, D:D + 2], t["a_first"]).then_inc(loaded, 16)

        @block.gpsimd
        def _(pool):
            nc.gpsimd.memset(half[:], -0.5).then_inc(set_up, 1)
            nc.gpsimd.memset(xT[:], 1.0).then_inc(set_up, 1)
            for k in range(2):
                nc.gpsimd.memset(v[k][:], 1.0).then_inc(set_up, 1)
            pool.wait_ge(set_up, SET_UP)
            with pool.Fori(0, B) as r:
                wait_all(pool, pool_passed, (var_ready, r + 1))
                st = Steps(pool, pool_step, r)
                st.then(nc.gpsimd.tensor_scalar(rstd[:], total[:], 1.0 / D, EPS, ALU.mult, ALU.add))
                nc.gpsimd.tensor_tensor(rstd[:], rstd[:], half[:], ALU.pow).then_inc(rstd_ready, 1)

        @block.scalar
        def _(act):
            act.wait_ge(set_up, SET_UP)
            act.wait_ge(loaded, 16 * LOADS)
            act.wait_ge(wvo_ps_ready, 1)
            nc.scalar.copy(wvo[:, 0:D], qv_ps[0:D + 1, 0:D]).then_inc(wvo_ready, 1)

            def front(r, k, m):
                if m == 1:
                    act.wait_ge(xT_ps_ready, r + 1)
                    nc.scalar.copy(xT[0:D, :], xk_ps[0:D, :]).then_inc(xT_ready, 1)
                if m == 2:
                    act.wait_ge(q_ps_ready, r + 1)
                    nc.scalar.copy(qT[k][:], qv_ps[0:D, :]).then_inc(q_ready, 1)
                if m == 3:
                    act.wait_ge(k_ps_ready, r + 1)
                    nc.scalar.copy(kT[k][:], xk_ps[0:D, :]).then_inc(k_ready, 1)
                    act.wait_ge(v_ps_ready, r + 1)
                    nc.scalar.copy(v[k][:, :, 0:D], v_of(qv_ps)[:, :, 0:D]).then_inc(v_ready, 1)

            def turned(r, m):
                act.wait_ge(pT_ps_ready, r * T + (m + 1))
                nc.scalar.copy(pT[m % 2][:], pT_ps[m % 2][:].rearrange("p (t q) -> p t q", t=T)).then_inc(pT_ready, 1)

            def one_row(r, k, number=None):
                for m in range(T):
                    if m >= 2:
                        turned(r, m - 2)
                    elif number != 0:
                        turned(r - 1, m - 2 + T)
                    act.wait_ge(bias_ready, r * T + (m + 1))
                    nc.scalar.activation(p[m][:], s_ps[m % 2][:], ACT.Exp, bias=bias[:, m:m + 1], scale=SCALE).then_inc(p_ready, 1)
                    if number != B - 1:
                        front(r + 1, 1 - k, m)

            for m in range(T):
                front(0, 0, m)
            one_row(0, 0, 0)
            one_row(1, 1, 1)
            with act.Fori(1, B // 2 - 1) as i:
                for k in range(2):
                    one_row(i * 2 + k, k)
            one_row(B - 2, 0, B - 2)
            one_row(B - 1, 1, B - 1)
            for m in (T - 2, T - 1):
                turned(B - 1, m)

        @block.vector
        def _(dve):
            dve.wait_ge(loaded, 16 * LOADS)
            dve.wait_ge(set_up, SET_UP)

            def centre(r):
                st = Steps(dve, ln_step, r * LN_STEPS)
                h = row_of_H(r)
                st.then(nc.vector.reduce_sum(total[:], h, axis=AX))
                st.then(nc.vector.scalar_tensor_tensor(cen[:], total[:].unsqueeze(2).to_broadcast(full), -1.0 / D, h, ALU.mult, ALU.add))

            def variance(r):
                st = Steps(dve, ln_step, r * LN_STEPS + (LN_STEPS - 1))
                st.then(nc.vector.tensor_tensor(sq[:], cen[:], cen[:], ALU.mult))
                nc.vector.reduce_sum(total[:], sq[:], axis=AX).then_inc(var_ready, 1)

            def normalise(r):
                dve.wait_ge(rstd_ready, r + 1)
                if not (isinstance(r, int) and r == 0):
                    dve.wait_ge(xT_ps_ready, r)
                nc.vector.tensor_tensor(xn[:], cen[:], rstd[:].unsqueeze(2).to_broadcast(full), ALU.mult).then_inc(xn_ready, 1)

            def finish(r, k):
                st = Steps(dve, end_step, r * END_STEPS)
                ops = v_of(o_ps[k])
                dve.wait_ge(o_ready, r + 1)
                st.then(nc.vector.reciprocal(factor[:], ops[:, :, D]))
                st.then(nc.vector.tensor_tensor(factor[:], factor[:], mask[k][:, :, 0], ALU.mult))
                st.then(nc.vector.tensor_tensor(factor[:], factor[:], mask[k][:, :, 1], ALU.mult))
                nc.vector.tensor_tensor(o[:], ops[:, :, 0:D], factor[:].unsqueeze(2).to_broadcast(full), ALU.mult).then_inc(o_taken, 1)
                st.then(nc.vector.tensor_tensor(row_of_H(r), row_of_H(r), bo[:].unsqueeze(1).to_broadcast(full), ALU.add))
                dve.wait_ge(o_taken, r + 1)
                st.then(nc.vector.tensor_tensor(row_of_H(r), row_of_H(r), o[:], ALU.add))

            def one_row(r, k, number=None):
                for m in range(T):
                    dve.wait_ge(s_ready, r * T + (m + 1))
                    nc.vector.reduce_max(mx[:, m:m + 1], s_ps[m % 2][:], axis=AX).then_inc(mx_ready, 1)
                    dve.wait_ge(mx_ready, r * T + (m + 1))
                    nc.vector.tensor_scalar(bias[:, m:m + 1], mx[:, m:m + 1], -SCALE, None, ALU.mult).then_inc(bias_ready, 1)
                    if m == 0:
                        dve.wait_ge(v_ready, r + 1)
                        nc.vector.tensor_scalar(mask[k][:], v_of(qv_ps)[:, :, D:D + 2], 0.0, None, ALU.not_equal).then_inc(mask_ready, 1)
                        if number != B - 1:
                            normalise(r + 1)
                    more = number not in (B - 2, B - 1)
                    if m == 1 and more:
                        centre(r + 2)
                    if m == 2 and more:
                        variance(r + 2)
                    if m == 3 and number != 0:
                        dve.wait_ge(mask_ready, r)
                        finish(r - 1, 1 - k)

            centre(0)
            variance(0)
            normalise(0)
            dve.wait_ge(xn_ready, 1)
            centre(1)
            variance(1)
            one_row(0, 0, 0)
            one_row(1, 1, 1)
            with dve.Fori(1, B // 2 - 1) as i:
                for k in range(2):
                    one_row(i * 2 + k, k)
            one_row(B - 2, 0, B - 2)
            one_row(B - 1, 1, B - 1)
            dve.wait_ge(mask_ready, B)
            finish(B - 1, 1)

        @block.tensor
        def _(pe):
            pe.wait_ge(loaded, 16 * LOADS)
            pe.wait_ge(set_up, SET_UP)
            nc.tensor.matmul(qv_ps[0:D + 1, 0:D], wv[:], wo[:], start=True, stop=True).then_inc(wvo_ps_ready, 1)
            pe.wait_ge(wvo_ready, 1)
            pe.sem_inc(p_ready, CREDIT)

            def front(r, k, m):
                first = isinstance(r, int) and r == 0
                if m == 1:
                    wait_all(pe, pe_passed, (xn_ready, r + 1))
                    for c in range(T):
                        last = nc.tensor.transpose(xk_ps[0:D, c * P:(c + 1) * P], xn[:, c, :], net.ident[:])
                    last.then_inc(xT_ps_ready, 1)
                if m == 2:
                    if first:
                        wait_all(pe, pe_passed, (xT_ready, r + 1))
                    else:
                        wait_all(pe, pe_passed, (xT_ready, r + 1), (mask_ready, r))
                    nc.tensor.matmul(qv_ps[0:D, :], wq[:], xT[:], start=True, stop=True).then_inc(q_ps_ready, 1)
                    nc.tensor.matmul(xk_ps[0:D, :], wk[:], xT[:], start=True, stop=True).then_inc(k_ps_ready, 1)
                if m == 3:
                    wait_all(pe, pe_passed, (q_ready, r + 1))
                    for c in range(T):
                        last = nc.tensor.matmul(v_of(qv_ps)[:, c, :], xT[:, c * P:(c + 1) * P], wvo[:], start=True, stop=True)
                    last.then_inc(v_ps_ready, 1)

            def turn(m):
                for c in range(T):
                    last = nc.tensor.transpose(pT_ps[m % 2][:, c * P:(c + 1) * P], p[m][:, c * P:(c + 1) * P], net.ident[:])
                last.then_inc(pT_ps_ready, 1)

            def values(r, k, m, first):
                wait_all(pe, pe_passed, (pT_ready, r * T + (m + 1)))
                if m == 0:
                    if first:
                        wait_all(pe, pe_passed, (v_ready, r + 1))
                    else:
                        wait_all(pe, pe_passed, (v_ready, r + 1), (o_taken, r - 1))
                for c in range(T):
                    last = nc.tensor.matmul(v_of(o_ps[k])[:, m, 0:D + 1], pT[m % 2][:, c, :], v[k][:, c, :],
                                            start=(c == 0), stop=(c == T - 1))
                if m == T - 1:
                    last.then_inc(o_ready, 1)

            def one_row(r, k, number=None):
                wait_all(pe, pe_passed, (q_ready, r + 1), (k_ready, r + 1))
                for m in range(T):
                    wait_all(pe, pe_passed, (p_ready, r * T + (m + 1)))
                    nc.tensor.matmul(s_ps[m % 2][:], qT[k][:, m * P:(m + 1) * P], kT[k][:], start=True, stop=True).then_inc(s_ready, 1)
                    if m >= 2 or number != 0:
                        turn((m - 2) % T)
                    if m >= 3:
                        values(r, k, m - 3, number in (0, 1))
                    elif number != 0:
                        values(r - 1, 1 - k, m - 3 + T, False)
                    if number != B - 1:
                        front(r + 1, 1 - k, m)

            for m in range(T):
                front(0, 0, m)
            one_row(0, 0, 0)
            one_row(1, 1, 1)
            with pe.Fori(1, B // 2 - 1) as i:
                for k in range(2):
                    one_row(i * 2 + k, k)
            one_row(B - 2, 0, B - 2)
            one_row(B - 1, 1, B - 1)
            for m in range(3):
                if m < 2:
                    pe.wait_ge(p_ready, B * T + (m + 1))
                    turn(m - 2 + T)
                values(B - 1, 1, m - 3 + T, False)


def tower(nc, t, out):
    B, S, D = out.shape
    with ExitStack() as ctx:
        net = Net(nc, ctx, t, B, S, D)
        with nc.sbuf_tensor("X", [P, B, S // P, D], F32) as X:
            token_stage(net, X)
            net.clear_semaphores()
            for layer in range(2):
                mamba_stage(net, X, layer)
                net.clear_semaphores()
            mamba_end_stage(net, X)
            net.clear_semaphores()
        experts_stage(net, "f0", None)
        net.clear_semaphores()
        attention_stage(net)
        net.clear_semaphores()
        experts_stage(net, "f1", out)
        net.clear_semaphores()


def lay_out(i):
    import numpy as np

    def c(*a, axis=0):
        return np.concatenate([np.asarray(x) for x in a], axis)

    a = {k: np.asarray(v) for k, v in i.items()}
    t = {"ident": np.eye(P, dtype=np.float32)}
    for name, k in (("id_event", "x"), ("id_fault", "itok_BS_0_255"), ("id_syscall", "itok_BS_0_511"),
                    ("id_opcode", "itok_BS_0_127"), ("id_transition", "itok_BS_0_63"), ("id_result", "itok_BS_0_3")):
        t[name] = a[k]
    W = a["L0_tok_W"]
    D = W.shape[0]
    tables = [("et", 0, 0, 0), ("fc", 0, 16, 64), ("sc", 1, 0, 0), ("of", 2, 0, 0), ("tt", 3, 0, 0), ("rc", 3, 16, 64)]
    E = np.zeros((33, 4, P), np.float32)
    Wt = np.zeros((32, 4, D), np.float32)
    ids = np.full((P, 4), -1, np.float32)
    for n, (name, tile, row, col) in enumerate(tables):
        e = a[f"L0_tok_E_{name}"]
        E[row:row + 16, tile, col:col + len(e)] = e.T
        Wt[row:row + 16, tile] = W[:, 16 * n:16 * n + 16].T
        ids[col:col + len(e), tile] = np.arange(len(e))
    E[32, 0, 0:64] = 1
    b = np.zeros((1, 4, D), np.float32)
    b[0, 0] = a["L0_tok_b"]
    t |= {"tok_E": E, "tok_W": Wt, "tok_b": b, "vocab": ids, "tok_gamma": a["L0_tok_gamma"], "tok_beta": a["L0_tok_beta"],
          "pre_g": a["L0_attn_pre_g"], "pre_b": a["L0_attn_pre_b"], "normf_w": a["L0_attn_normf_w"],
          "post_g": a["L0_attn_post_g"], "post_b": a["L0_attn_post_b"]}
    inw = a["L0_attn_inproj_w"].transpose(0, 2, 1)
    NL, _, E2 = inw.shape
    NC = E2 // 2 // P

    def channels(x):
        return np.ascontiguousarray(x.reshape(NL, NC, P, *x.shape[2:]).swapaxes(1, 2))

    xp = a["L0_attn_xproj_w"]
    R, NS = a["L0_attn_dtproj_w"].shape[2], a["L0_attn_A_log"].shape[2]
    bc = xp[:, R:]
    rows = c(bc, bc, bc, xp[:, :R], axis=1).transpose(0, 2, 1)
    t |= {"m_in_w": c(inw, inw, axis=1), "m_norm_w": c(a["L0_attn_norm_w"], a["L0_attn_norm_w"], axis=1)[:, :, None],
          "m_conv_w": a["L0_attn_conv_w"][:, :, 0, :].transpose(0, 2, 1), "m_conv_b": channels(a["L0_attn_conv_b"]),
          "m_xproj_w": channels(rows), "m_dtproj_w": a["L0_attn_dtproj_w"].transpose(0, 2, 1),
          "m_dtproj_b": channels(a["L0_attn_dtproj_b"]), "m_A_log": channels(a["L0_attn_A_log"]),
          "m_D": channels(a["L0_attn_D_param"]), "m_out_w": channels(a["L0_attn_outproj_w"].transpose(0, 2, 1))}

    def experts(name, w1, b1, w2, b2, gate, gate_b):
        E, H, D = w1.shape
        J = E * H // P
        t[f"{name}_w1"] = np.tile(w1.reshape(J * P, D).T, (2, 1)).reshape(2 * D, J, P)
        t[f"{name}_b1"] = b1.reshape(J, P).T
        t[f"{name}_w2"] = w2.reshape(J, P, D).transpose(1, 0, 2)
        t[f"{name}_b2"] = np.tile(b2, (3, 1))
        t[f"{name}_gate"] = np.tile(gate, (2, 1))
        t[f"{name}_gate_b"] = gate_b
        t[f"{name}_order"] = np.tile(np.arange(E, 0, -1, dtype=np.float32), (P, 1))

    experts("f0", a["L0_ffn_W1"], a["L0_ffn_b1"], a["L0_ffn_W2"].transpose(0, 2, 1), a["L0_ffn_b2"],
            a["L0_ffn_Wg"].T, a["L0_ffn_bg"])
    experts("f1", a["L1_ffn_w1"].transpose(0, 2, 1), a["L1_ffn_b1"], a["L1_ffn_w2"], a["L1_ffn_b2"],
            a["L1_ffn_gate_w"], a["L1_ffn_gate_b"])
    t |= {"f1_gamma": a["L1_ffn_gamma"], "f1_beta": a["L1_ffn_beta"]}
    wq, wk, bq, bk = a["L1_attn_Wq"], a["L1_attn_Wk"], a["L1_attn_bq"], a["L1_attn_bk"]
    t |= {"a_wq": c(wq.T, bq[None]), "a_wk": c(wk.T, bk[None]), "a_wv": c(a["L1_attn_Wv"], a["L1_attn_bv"][:, None], axis=1),
          "a_wo": a["L1_attn_Wo"].T, "a_bo": a["L1_attn_bo"],
          "a_first": c(c(wq[0:1].T, bq[None, 0:1]), c(wk[0:1].T, bk[None, 0:1]), axis=1)}
    return {k: np.ascontiguousarray(v) for k, v in t.items()}


def kernel(**inputs):
    import numpy as _np
    import concourse.bacc as _bacc
    from concourse.bass_utils import run_bass_kernel_spmd as _run

    nc = _bacc.Bacc("TRN2", target_bir_lowering=False, num_devices=1)
    arrays = lay_out(inputs)
    t = {k: nc.dram_tensor(f"in_{k}", v.shape, mybir.dt.from_np(v.dtype), kind="ExternalInput").ap() for k, v in arrays.items()}
    B, S = inputs["x"].shape
    D = inputs["L0_tok_W"].shape[0]
    out = nc.dram_tensor("out", (B, S, D), F32, kind="ExternalOutput").ap()
    tower(nc, t, out)
    return _run(nc, [{f"in_{k}": v for k, v in arrays.items()}], core_ids=[0]).results[0]["out"]
```
